# Optimizing a Trainium2 kernel written in Bass

```python
import numpy as np
import jax
import jax.numpy as jnp

def _softmax(x, axis=-1):
    return jax.nn.softmax(x, axis=axis)

def _gelu(x):
    return jax.nn.gelu(x, approximate=True)

def _silu(x):
    return jax.nn.silu(x)

def _sigmoid(x):
    return jax.nn.sigmoid(x)

def _layernorm(x, axis=-1, eps=1e-05):
    m = jnp.mean(x, axis=axis, keepdims=True)
    v = jnp.var(x, axis=axis, keepdims=True)
    return (x - m) / jnp.sqrt(v + eps)

def _scatter_add(tgt, idx, src, axis=0):
    return tgt.at[idx].add(src)

def _segment_sum(src, seg, n):
    return jax.ops.segment_sum(src, seg, n)
kernel_name = 'mk_gps_d1_gnn_r32_65b0d6'

def setup_inputs(seed: int=0):
    np.random.seed(seed)
    _w = jnp.asarray

    def _rec_inputs():
        import jax
        import jax.numpy as jnp
        _gk = jax.random.key(seed)
        x = -0.0002117 + 1 * jax.random.normal(jax.random.fold_in(_gk, 1), (3125, 256), jnp.float32)
        _s = jax.random.randint(jax.random.fold_in(_gk, 2), (25000,), 0, 3125, jnp.int32)
        _d = jax.random.randint(jax.random.fold_in(_gk, 3), (25000,), 0, 3125, jnp.int32)
        _loop = jnp.arange(3125, dtype=jnp.int32)
        src = jnp.concatenate([_s, _d, _loop])
        dst = jnp.concatenate([_d, _s, _loop])
        _o = jnp.argsort(dst, stable=True)
        src = src[_o]
        dst = dst[_o]
        edge_weight = jax.random.uniform(jax.random.fold_in(_gk, 12), (53125,), jnp.float32, 0.0, 1)
        return (x, src, dst, edge_weight)
    x, src, dst, edge_weight = _rec_inputs()

    def _L0_gnn_setup():
        import jax, jax.numpy as jnp
        import numpy as np
        N_NODES = 3125
        N_EDGES = 100000
        D_IN = 256
        D_OUT = 256
        key = jax.random.key(seed)
        k1, k2, k3, k4, k5 = jax.random.split(key, 5)
        X = jax.random.normal(k1, (N_NODES, D_IN), dtype=jnp.float32)
        edge_row = jax.random.randint(k2, (N_EDGES,), 0, N_NODES, dtype=jnp.int32)
        edge_col = jax.random.randint(k3, (N_EDGES,), 0, N_NODES, dtype=jnp.int32)
        edge_val = jax.random.uniform(k4, (N_EDGES,), dtype=jnp.float32)
        W = jax.random.normal(k5, (D_OUT, D_IN), dtype=jnp.float32) * (6.0 / (D_IN + D_OUT)) ** 0.5
        b = jnp.zeros((D_OUT,), dtype=jnp.float32)
        return {'X': X, 'edge_row': edge_row, 'edge_col': edge_col, 'edge_val': edge_val, 'W': W, 'b': b}
    _L0_gnn_all = _L0_gnn_setup()
    _L0_gnn_in = {k: v for k, v in _L0_gnn_all.items() if k in ('W', 'b')}
    del _L0_gnn_all

    def _L0_mix_setup():
        import jax, jax.numpy as jnp
        import numpy as np
        N, F, C, H = (32, 128, 256, 8)
        D = C // H
        EPS_ATTN = 1e-06
        EPS_LN = 1e-05

        def layer_norm(x, g, b):
            mu = jnp.mean(x, axis=-1, keepdims=True)
            var = jnp.var(x, axis=-1, keepdims=True)
            return (x - mu) * jax.lax.rsqrt(var + EPS_LN) * g + b
        key = jax.random.key(seed)
        ks = jax.random.split(key, 8)
        s = 1.0 / np.sqrt(C)
        return {'x': jax.random.normal(ks[0], (N, F, C), jnp.float32), 'Wqkv': jax.random.uniform(ks[1], (3 * C, C), jnp.float32, -s, s), 'ln1_g': jnp.ones((C,), jnp.float32), 'ln1_b': jnp.zeros((C,), jnp.float32), 'W1': jax.random.uniform(ks[2], (C, C), jnp.float32, -s, s), 'b1': jax.random.uniform(ks[3], (C,), jnp.float32, -s, s), 'W2': jax.random.uniform(ks[4], (C, C), jnp.float32, -s, s), 'b2': jax.random.uniform(ks[5], (C,), jnp.float32, -s, s), 'ln2_g': jnp.ones((C,), jnp.float32), 'ln2_b': jnp.zeros((C,), jnp.float32)}
    _L0_mix_all = _L0_mix_setup()
    _L0_mix_in = {k: v for k, v in _L0_mix_all.items() if k in ('Wqkv', 'ln1_g', 'ln1_b', 'W1', 'b1', 'W2', 'b2', 'ln2_g', 'ln2_b')}
    del _L0_mix_all

    def _L0_ffn_setup():
        import math
        import jax, jax.numpy as jnp
        import numpy as np
        CAPACITY_FACTOR = 1.25
        TOP_K = 2
        LN_EPS = 1e-05

        def _layer_norm(x, gamma, beta):
            mu = jnp.mean(x, axis=-1, keepdims=True)
            var = jnp.var(x, axis=-1, keepdims=True)
            return (x - mu) * jax.lax.rsqrt(var + LN_EPS) * gamma + beta
        key = jax.random.key(seed)
        ks = jax.random.split(key, 4)
        B, S, D, F, E = (8, 128, 256, 512, 8)
        x = jax.random.normal(ks[0], (B, S, D), dtype=jnp.float32)
        Wr = jax.random.normal(ks[1], (D, E), dtype=jnp.float32) / np.sqrt(D)
        br = jnp.zeros((E,), jnp.float32)
        W1 = jax.random.normal(ks[2], (E, D, F), dtype=jnp.float32) / np.sqrt(D)
        b1 = jnp.zeros((E, F), jnp.float32)
        W2 = jax.random.normal(ks[3], (E, F, D), dtype=jnp.float32) / np.sqrt(F)
        b2 = jnp.zeros((E, D), jnp.float32)
        gamma = jnp.ones((D,), jnp.float32)
        beta = jnp.zeros((D,), jnp.float32)
        return {'x': x, 'Wr': Wr, 'br': br, 'W1': W1, 'b1': b1, 'W2': W2, 'b2': b2, 'gamma': gamma, 'beta': beta}
    _L0_ffn_all = _L0_ffn_setup()
    _L0_ffn_in = {k: v for k, v in _L0_ffn_all.items() if k in ('Wr', 'br', 'W1', 'b1', 'W2', 'b2', 'gamma', 'beta')}
    del _L0_ffn_all
    return {'x': x, 'src': src, 'dst': dst, 'edge_weight': edge_weight, 'L0_gnn_W': _L0_gnn_in['W'], 'L0_gnn_b': _L0_gnn_in['b'], 'L0_mix_Wqkv': _L0_mix_in['Wqkv'], 'L0_mix_ln1_g': _L0_mix_in['ln1_g'], 'L0_mix_ln1_b': _L0_mix_in['ln1_b'], 'L0_mix_W1': _L0_mix_in['W1'], 'L0_mix_b1': _L0_mix_in['b1'], 'L0_mix_W2': _L0_mix_in['W2'], 'L0_mix_b2': _L0_mix_in['b2'], 'L0_mix_ln2_g': _L0_mix_in['ln2_g'], 'L0_mix_ln2_b': _L0_mix_in['ln2_b'], 'L0_ffn_Wr': _L0_ffn_in['Wr'], 'L0_ffn_br': _L0_ffn_in['br'], 'L0_ffn_W1': _L0_ffn_in['W1'], 'L0_ffn_b1': _L0_ffn_in['b1'], 'L0_ffn_W2': _L0_ffn_in['W2'], 'L0_ffn_b2': _L0_ffn_in['b2'], 'L0_ffn_gamma': _L0_ffn_in['gamma'], 'L0_ffn_beta': _L0_ffn_in['beta']}

def reference(x, src, dst, edge_weight, L0_gnn_W, L0_gnn_b, L0_mix_Wqkv, L0_mix_ln1_g, L0_mix_ln1_b, L0_mix_W1, L0_mix_b1, L0_mix_W2, L0_mix_b2, L0_mix_ln2_g, L0_mix_ln2_b, L0_ffn_Wr, L0_ffn_br, L0_ffn_W1, L0_ffn_b1, L0_ffn_W2, L0_ffn_b2, L0_ffn_gamma, L0_ffn_beta):
    import jax
    import jax.numpy as jnp

    def _L0_gnn_ref(X, edge_row, edge_col, edge_val, W, b):
        import jax, jax.numpy as jnp
        import numpy as np
        N_NODES = 3125
        N_EDGES = 100000
        D_IN = 256
        D_OUT = 256
        msgs = edge_val[:, None] * X[edge_col]
        h = jax.ops.segment_sum(msgs, edge_row, num_segments=N_NODES)
        return h @ W.T + b

    def _L0_mix_ref(x, Wqkv, ln1_g, ln1_b, W1, b1, W2, b2, ln2_g, ln2_b):
        import jax, jax.numpy as jnp
        import numpy as np
        N, F, C, H = (32, 128, 256, 8)
        D = C // H
        EPS_ATTN = 1e-06
        EPS_LN = 1e-05

        def layer_norm(x, g, b):
            mu = jnp.mean(x, axis=-1, keepdims=True)
            var = jnp.var(x, axis=-1, keepdims=True)
            return (x - mu) * jax.lax.rsqrt(var + EPS_LN) * g + b
        n, f, c = x.shape
        qkv = jnp.einsum('nfc,oc->nfo', x, Wqkv)
        q, k, v = jnp.split(qkv, 3, axis=-1)
        q = q.reshape(n, f, H, D)
        k = k.reshape(n, f, H, D)
        v = v.reshape(n, f, H, D)
        q = jax.nn.elu(q) + 1.0
        k = jax.nn.elu(k) + 1.0
        kv = jnp.einsum('nshd,nshm->nhmd', k, v)
        ksum = jnp.sum(k, axis=1)
        z = 1.0 / (jnp.einsum('nlhd,nhd->nlh', q, ksum) + EPS_ATTN)
        t = jnp.einsum('nlhd,nhmd,nlh->nlhm', q, kv, z)
        t = t.reshape(n, f, c)
        x1 = layer_norm(t + x, ln1_g, ln1_b)
        h = jax.nn.gelu(jnp.einsum('nfc,oc->nfo', x1, W1) + b1, approximate=False)
        y = jnp.einsum('nfc,oc->nfo', h, W2) + b2
        return layer_norm(y + x1, ln2_g, ln2_b)

    def _L0_ffn_ref(x, Wr, br, W1, b1, W2, b2, gamma, beta):
        import math
        import jax, jax.numpy as jnp
        import numpy as np
        CAPACITY_FACTOR = 1.25
        TOP_K = 2
        LN_EPS = 1e-05

        def _layer_norm(x, gamma, beta):
            mu = jnp.mean(x, axis=-1, keepdims=True)
            var = jnp.var(x, axis=-1, keepdims=True)
            return (x - mu) * jax.lax.rsqrt(var + LN_EPS) * gamma + beta
        B, S, D = x.shape
        E = Wr.shape[1]
        N = B * S
        K = TOP_K
        logits = jnp.mean(x, axis=1) @ Wr + br
        routing_weights = jax.nn.softmax(logits, axis=-1)
        capacity = float(math.ceil(N * CAPACITY_FACTOR / E))
        expected_loads = routing_weights.sum(axis=0) * (N / B)
        scale = jnp.where(expected_loads > capacity, capacity / expected_loads, 1.0)
        routing_weights = jax.nn.softmax(routing_weights * scale, axis=-1)
        rw_tok = jnp.broadcast_to(routing_weights[:, None, :], (B, S, E)).reshape(N, E)
        top_w, top_i = jax.lax.top_k(rw_tok, K)
        top_w = jax.nn.softmax(top_w, axis=-1)
        xf = x.reshape(N, D)
        h = jax.nn.gelu(jnp.einsum('nd,edf->enf', xf, W1) + b1[:, None, :], approximate=False)
        y = jnp.einsum('enf,efd->end', h, W2) + b2[:, None, :]
        w_dense = jnp.zeros((N, E), x.dtype).at[jnp.arange(N)[:, None], top_i].add(top_w)
        out = jnp.einsum('ne,end->nd', w_dense, y).reshape(B, S, D)
        out = _layer_norm(out + x, gamma, beta)
        return out
    xn = _layernorm(x, axis=-1)
    x = x + _L0_gnn_ref(xn, src, dst, edge_weight, L0_gnn_W, L0_gnn_b) + _L0_mix_ref(xn[None], L0_mix_Wqkv, L0_mix_ln1_g, L0_mix_ln1_b, L0_mix_W1, L0_mix_b1, L0_mix_W2, L0_mix_b2, L0_mix_ln2_g, L0_mix_ln2_b)[0]
    x = x + _L0_ffn_ref(_layernorm(x, axis=-1)[None], L0_ffn_Wr, L0_ffn_br, L0_ffn_W1, L0_ffn_b1, L0_ffn_W2, L0_ffn_b2, L0_ffn_gamma, L0_ffn_beta)[0]
    return x

_drawn_inputs = setup_inputs


def setup_inputs(seed=0):
    import zlib

    import numpy as np

    out = dict(_drawn_inputs(seed))
    spreads = {'L0_gnn_b': (0.0, 0.362),
     'L0_mix_ln1_g': (1.0, 0.2),
     'L0_mix_ln1_b': (0.0, 0.374),
     'L0_mix_ln2_g': (1.0, 0.2),
     'L0_mix_ln2_b': (0.0, 0.389),
     'L0_ffn_br': (0.0, 0.1),
     'L0_ffn_b1': (0.0, 0.8),
     'L0_ffn_b2': (0.0, 0.702),
     'L0_ffn_gamma': (1.0, 0.2),
     'L0_ffn_beta': (0.0, 0.446)}
    factors = {'L0_mix_Wqkv': 8.0, 'L0_mix_b1': 24.791, 'L0_mix_b2': 7.294, 'L0_ffn_Wr': 8.0}
    for name, (base, spread) in spreads.items():
        noise = np.random.default_rng([zlib.crc32(name.encode()), seed]).standard_normal(out[name].shape)
        drawn = base * np.exp(spread * noise) if base else spread * noise
        out[name] = jnp.asarray(drawn.astype(out[name].dtype))
    for name, factor in factors.items():
        out[name] = (out[name] * factor).astype(out[name].dtype)
    return out
```

```python
import concourse.bass as bass
from concourse import mybir
from contextlib import ExitStack, contextmanager


def gps_layer_program(nc, x, row, col, weight, gnn_wT, gnn_b, qkv_wT, ln1_g, ln1_b, mix_w1T, mix_b1,
                      mix_w2T, mix_b2, ln2_g, ln2_b, router_w, router_b, exp_w1, exp_b1, exp_w2, exp_b2,
                      ffn_g, ffn_b, out, xg_dram):
    f32, bf16, i32, u32 = mybir.dt.float32, mybir.dt.bfloat16, mybir.dt.int32, mybir.dt.uint32
    ALU, ACT, AX = mybir.AluOpType, mybir.ActivationFunctionType, mybir.AxisListType

    P = 128
    N, C = out.shape
    TILES = x.shape[0] // P
    PAIRS = TILES // 2
    LAST = N - (TILES - 1) * P
    H, HD = 8, C // 8
    HH = H // 2
    CC = C // P
    EPS_ATTN, EPS_LN = 1e-6, 1e-5
    NE, FF = exp_w1.shape[0], exp_w1.shape[2]
    FJ = FF // P
    TOPK = 2
    CAPACITY = float(-(-N * 5 // (4 * NE)))

    EK = row.shape[1]
    GC = 13
    NG = EK // GC
    LC = 64
    assert NG * GC == EK and TILES + GC + (TILES * (P - 1)) // P <= LC
    DZ = 12
    COLS = -(-(EK + TILES - 1) // DZ) * DZ
    DOZENS = COLS // DZ
    assert DOZENS == 3 * PAIRS + 1 and COLS <= 512
    VE = P + HH
    BLK = 4 * P
    NBLK = N // BLK

    ctx = ExitStack()
    with ctx:
        def sb(name, shape, dt=f32):
            return scope.enter_context(nc.sbuf_tensor(name, shape, dt))

        def sem(name):
            return ctx.enter_context(nc.semaphore(name))

        scope = ctx
        X = sb("X", [P, TILES * C])
        XN = sb("XN", [P, TILES * C])
        XS = sb("XS", [P, 2, C])
        XT = sb("XT", [P, CC, 2, P])
        XGS = sb("XGS", [P, 2, C])
        ST = sb("ST", [P, TILES * 6])
        MV = sb("MV", [P, TILES, 2])
        SD = sb("SD", [P, TILES])
        RS = sb("RS", [P, TILES])
        NM = sb("NM", [P, TILES])
        QKVW = sb("QKVW", [P, CC, 3 * C])
        GW = sb("GW", [P, CC, C])
        W1 = sb("W1", [P, CC, C])
        W2 = sb("W2", [P, CC, C])
        ROWC = sb("ROWC", [P, 7, C])
        L1G, L1B, B2R, L2G, L2B, FG, FB = (ROWC[:, n, :] for n in range(7))
        GNB = sb("GNB", [P, C])
        B1C = sb("B1C", [P, CC])
        carrier = sb("carrier", [P, 1])
        eps_ln = sb("eps_ln", [P, 1])
        ident = sb("ident", [P, P])
        iota = sb("iota", [P, P])
        iota_i = sb("iota_i", [P, COLS], i32)
        iota_c = sb("iota_c", [P, COLS])
        ones = sb("ones", [P, P])
        onesb = sb("onesb", [P, P], bf16)
        from_here = sb("from_here", [P, P], bf16)
        row0 = sb("row0", [P, P], bf16)
        zeros = sb("zeros", [P, P])
        local_p = sb("local_p", [P, 1])
        local_i = sb("local_i", [P, 1], i32)
        hmask = sb("hmask", [P, VE])

        SW = sb("SW", [P, COLS])
        SPI = sb("SPI", [P, COLS], i32)
        SLI = sb("SLI", [P, COLS], i32)
        SLO = sb("SLO", [P, COLS])
        SIX = sb("SIX", [P, COLS], i32)
        RW = sb("RW", [P, CC, NE])
        RB = sb("RB", [1, NE])
        BID = sb("BID", [1, COLS], i32)
        VX = sb("VX", [P, 2, CC, VE])
        mhalf = sb("mhalf", [P, 4])

        scope = ctx.enter_context(ExitStack())
        EROW = sb("EROW", [P, EK], i32)
        ECOL = sb("ECOL", [P, EK], i32)
        EW = sb("EW", [P, EK])
        EBI = sb("EBI", [P, EK], i32)
        EBF = sb("EBF", [P, EK], bf16)
        ELO = sb("ELO", [P, EK], i32)
        EPCI = sb("EPCI", [P, EK], i32)
        EPC = sb("EPC", [P, EK])
        SLOT = sb("SLOT", [P, EK])
        SLOTI = EBI
        TMPI = sb("TMPI", [P, EK], i32)
        LANE = sb("LANE", [P, EK])
        LCOL = sb("LCOL", [P, EK])
        JMAP = sb("JMAP", [P, NG])
        sort_scope = scope
        scope = ctx.enter_context(ExitStack())
        RESTART = sb("RESTART", [P, EK], bf16)
        OH = sb("OH", [P, TILES, EK], bf16)
        SC = sb("SC", [P, TILES, EK], bf16)
        NT = TILES * NG
        CNT = sb("CNT", [P, TILES, NG])
        Q1 = sb("Q1", [P, TILES, NG])
        Q0 = sb("Q0", [P, TILES, NG])
        RSB = sb("RSB", [P, TILES, NG])
        Q1I = sb("Q1I", [P, TILES, NG], i32)
        Q0I = sb("Q0I", [P, TILES, NG], i32)
        QLI = sb("QLI", [P, TILES, NG], i32)
        F0, F1 = Q0, Q1
        TCH = sb("TCH", [P, NG, TILES])
        LINC = sb("LINC", [P, NG, TILES])
        LOFF = sb("LOFF", [P, NG, TILES])
        RSG = sb("RSG", [P, NG, TILES])
        TAB0 = sb("TAB0", [P, NG, TILES], bf16)
        TAB1 = sb("TAB1", [P, NG, TILES], bf16)
        DC = sb("DC", [P, NG, TILES])
        DD = LINC
        NBI = sb("NBI", [P, TILES], i32)
        NBF = sb("NBF", [P, TILES])
        CBI = sb("CBI", [P, TILES])
        CB = sb("CB", [P, TILES])
        CBD = sb("CBD", [P, TILES])
        CBP = sb("CBP", [P, 1])
        CMP = sb("CMP", [P, COLS])
        PRD = sb("PRD", [P, TILES, GC])
        scope.close()
        scope = sort_scope
        AS = sb("AS", [P, 2, GC, P])
        OI = sb("OI", [P, 2, GC, P])
        GS = sb("GS", [P, 2, P])
        OJ = sb("OJ", [P, 2, COLS])
        scope.close()
        QT = sb("QT", [P, CC, TILES * P])
        IDXS = sb("IDXS", [P, 2, DZ // 2], i32)
        RING = sb("RING", [P, DZ, C])
        SEL = sb("SEL", [P, 2, P])

        NK = sb("NK", [P, 2, C])
        EXK = sb("EXK", [P, 2, C])
        KS = sb("KS", [P, 2, C])
        NQ = sb("NQ", [P, CC, 2 * P])
        QR = sb("QR", [P, CC, 2 * P])
        KR = sb("KR", [P, 2, C])
        EQ = sb("EQ", [P, CC, 2 * P])
        KVM = sb("KVM", [P, CC, VE])
        QS = sb("QS", [P, 2, CC, P])
        DEN = sb("DEN", [P, 2, H])
        RZ = sb("RZ", [P, 2, H])
        TX = sb("TX", [P, 2, C])
        TX2 = sb("TX2", [P, 2, C])
        X1 = sb("X1", [P, 2, C])
        ST2 = sb("ST2", [P, 2, 6])
        MV2 = sb("MV2", [P, 2, 2])
        SD2 = sb("SD2", [P, 2])
        RS2 = sb("RS2", [P, 2])
        HS = sb("HS", [P, CC, 2, P])
        MEAN = sb("MEAN", [P, CC])
        R = sb("R", [1, 12, NE])
        RI = sb("RI", [1, NE], u32)
        WB = sb("WB", [P, TOPK])
        FW1 = sb("FW1", [P, TOPK, CC, FF])
        FW2 = sb("FW2", [P, TOPK * FJ, C])
        FB1 = sb("FB1", [P, TOPK, FJ])
        FB2 = sb("FB2", [P, TOPK, C])
        B2C = sb("B2C", [P, C])
        HF = sb("HF", [P, TOPK * FJ, BLK])
        Y = sb("Y", [P, 4, C])
        YO = sb("YO", [P, 4, C])
        ST3 = sb("ST3", [P, 4, 6])
        MV3 = sb("MV3", [P, 4, 2])
        VE3 = sb("VE3", [P, 4])
        RS3 = sb("RS3", [P, 4])

        bank = [ctx.enter_context(nc.psum_tensor(f"bank{n}", [P, 512], f32)) for n in range(8)]

        x_in = sem("x_in")
        w_in = sem("w_in")
        e_in = sem("e_in")
        pool_const = sem("pool_const")
        dve_const = sem("dve_const")
        stats_done = sem("stats_done")
        aggr_done = sem("aggr_done")
        std_ready = sem("std_ready")
        rstd_ready = sem("rstd_ready")
        xs_ready = [sem(f"xs_ready{s}") for s in range(2)]
        xn_kept = [sem(f"xn_kept{s}") for s in range(2)]
        tp_done = [sem(f"tp_done{s}") for s in range(2)]
        xt_ready = [sem(f"xt_ready{s}") for s in range(2)]
        g_done = [sem(f"g_done{s}") for s in range(2)]
        xg_evac = [sem(f"xg_evac{s}") for s in range(2)]
        xg_out = [sem(f"xg_out{s}") for s in range(2)]
        dve_step = sem("dve_step")
        act_step = sem("act_step")
        pool_step = sem("pool_step")
        counted = sem("counted")
        totals_done = sem("totals_done")
        tables_ready = sem("tables_ready")
        rank_done = [sem(f"rank_done{s}") for s in range(2)]
        rank_read = [sem(f"rank_read{s}") for s in range(2)]
        bid_cmp = sem("bid_cmp")
        bid_sum = sem("bid_sum")
        bid_ready = sem("bid_ready")
        ops_ready = [sem(f"ops_ready{s}") for s in range(2)]
        grp_done = [sem(f"grp_done{s}") for s in range(2)]
        gs_ready = [sem(f"gs_ready{s}") for s in range(2)]
        oj_ready = [sem(f"oj_ready{s}") for s in range(2)]
        placed = [sem(f"placed{s}") for s in range(2)]
        table_done = sem("table_done")
        slots_ready = sem("slots_ready")
        idx_first = sem("idx_first")
        idx_staged = [sem(f"idx_staged{h}") for h in range(2)]
        gathered = [sem(f"gathered{r}") for r in range(DZ)]
        sel_ready = [sem(f"sel_ready{s}") for s in range(2)]
        chunk_mm = [sem(f"chunk_mm{s}") for s in range(2)]
        x_added = [sem(f"x_added{s}") for s in range(2)]
        a_xs = [sem(f"a_xs{s}") for s in range(2)]
        a_tp = [sem(f"a_tp{s}") for s in range(2)]
        a_xt = [sem(f"a_xt{s}") for s in range(2)]
        kv_done = [sem(f"kv_done{s}") for s in range(2)]
        nk_ready = [sem(f"nk_ready{s}") for s in range(2)]
        ek_ready = [sem(f"ek_ready{s}") for s in range(2)]
        vx_ready = [sem(f"vx_ready{s}") for s in range(2)]
        ks_ready = [sem(f"ks_ready{s}") for s in range(2)]
        kvacc_done = [sem(f"kvacc_done{s}") for s in range(2)]
        q_done = sem("q_done")
        nq_ready = sem("nq_ready")
        eq_ready = sem("eq_ready")
        qt_ready = sem("qt_ready")
        kv_summed = sem("kv_summed")
        kvm_ready = sem("kvm_ready")
        qs_ready = [sem(f"qs_ready{s}") for s in range(2)]
        t_done = [sem(f"t_done{s}") for s in range(2)]
        var1 = sem("var1")
        sd1 = sem("sd1")
        x1_ready = [sem(f"x1_ready{s}") for s in range(2)]
        x1tp = sem("x1tp")
        x1t = sem("x1t")
        h_done = sem("h_done")
        hs_ready = sem("hs_ready")
        y_done = [sem(f"y_done{s}") for s in range(2)]
        var2 = sem("var2")
        sd2 = sem("sd2")
        b_done = sem("b_done")
        f_stats = sem("f_stats")
        f_aggr = sem("f_aggr")
        f_sd = sem("f_sd")
        f_rstd = sem("f_rstd")
        f_xs = [sem(f"f_xs{s}") for s in range(2)]
        f_kept = [sem(f"f_kept{s}") for s in range(2)]
        f_tp = [sem(f"f_tp{s}") for s in range(2)]
        f_xt = [sem(f"f_xt{s}") for s in range(2)]
        mean_done = sem("mean_done")
        mean_ready = sem("mean_ready")
        logits_done = sem("logits_done")
        r_shift = sem("r_shift")
        r_exp = sem("r_exp")
        topi_ready = sem("topi_ready")
        topw_ready = sem("topw_ready")
        wb_done = sem("wb_done")
        exp_in = sem("exp_in")
        w2_scaled = sem("w2_scaled")
        up_done = [sem(f"up_done{s}") for s in range(2)]
        gelu_done = [sem(f"gelu_done{s}") for s in range(2)]
        down_done = [sem(f"down_done{s}") for s in range(2)]
        y_read = [sem(f"y_read{s}") for s in range(2)]
        v3_ready = sem("v3_ready")
        rs3_ready = sem("rs3_ready")
        yo_ready = [sem(f"yo_ready{s}") for s in range(4)]
        out_done = [sem(f"out_done{s}") for s in range(4)]

        block = ctx.enter_context(nc.Block())

        def tile(t):
            return bass.ds(t * C, C)

        def toks(t, n=P):
            return bass.ds(t * P, n)

        class Chain:

            def __init__(self, eng, s):
                self.eng, self.s, self.n, self.local = eng, s, 0, 0

            def mark(self, ins):
                ins.then_inc(self.s, 1)
                self.n = self.n + 1
                self.local += 1

            def settle(self):
                self.eng.wait_ge(self.s, self.n)

            def link(self, ins):
                self.mark(ins)
                self.settle()

            @contextmanager
            def loop(self, trips, per):
                base = self.n
                with self.eng.Fori(0, trips) as i:
                    self.n, self.local = i * per + base, 0
                    yield i
                    assert self.local == per, (self.local, per)
                self.n = base + trips * per

        @block.sync
        def _(sp):
            sp.dma_start(EROW[:, :], row).then_inc(e_in, 16)
            sp.dma_start(ECOL[:, :], col).then_inc(e_in, 16)
            sp.dma_start(EW[:, :], weight).then_inc(e_in, 16)
            sp.dma_start(X[:, :].rearrange("p (t c) -> p t c", c=C),
                         x.rearrange("(t p) c -> p t c", p=P)).then_inc(x_in, 16)
            sp.dma_start(GW[:, :, :], gnn_wT.rearrange("(c p) o -> p c o", p=P)).then_inc(w_in, 16)
            sp.dma_start(QKVW[:, :, :], qkv_wT.rearrange("(c p) o -> p c o", p=P)).then_inc(w_in, 16)
            sp.dma_start(W1[:, :, :], mix_w1T.rearrange("(c p) o -> p c o", p=P)).then_inc(w_in, 16)
            sp.dma_start(W2[:, :, :], mix_w2T.rearrange("(c p) o -> p c o", p=P)).then_inc(w_in, 16)
            for dst, src in ((L1G, ln1_g), (L1B, ln1_b), (B2R, mix_b2), (L2G, ln2_g), (L2B, ln2_b),
                             (FG, ffn_g), (FB, ffn_b), (GNB[:, :], gnn_b)):
                sp.dma_start(dst, src.to_broadcast([P, C])).then_inc(w_in, 16)
            sp.dma_start(B1C[:, :], mix_b1).then_inc(w_in, 16)
            sp.dma_start(RW[:, :, :], router_w.rearrange("(c p) o -> p c o", p=P)).then_inc(w_in, 16)
            sp.dma_start(RB[:, :], router_b).then_inc(w_in, 16)

            def store_xg(i, slots):
                for s in slots:
                    sp.wait_ge(xg_evac[s], i + 1)
                    sp.dma_start(xg_dram[bass.ds((2 * i + s) * P, P), :], XGS[:, s, :]).then_inc(xg_out[s], 16)

            with sp.Fori(0, PAIRS) as i:
                store_xg(i, (0, 1))
            store_xg(PAIRS, (0,))

            sp.wait_ge(topi_ready, 1)
            for e in range(TOPK):
                v = sp.value_load(RI[0:1, e:e + 1], min_val=0, max_val=NE - 1)
                sp.dma_start(FW1[:, e, :, :], exp_w1[bass.ds(v, 1), :, :].rearrange("e (c p) f -> p (e c) f", p=P)).then_inc(exp_in, 16)
                sp.dma_start(FW2[:, e * FJ:(e + 1) * FJ, :], exp_w2[bass.ds(v, 1), :, :].rearrange("e (j p) d -> p (e j) d", p=P)).then_inc(exp_in, 16)
                sp.dma_start(FB1[:, e, :], exp_b1[bass.ds(v, 1), :, :].rearrange("e p j -> p (e j)")).then_inc(exp_in, 16)
                sp.dma_start(FB2[:, e, :], exp_b2[bass.ds(v, 1), :].to_broadcast([P, C])).then_inc(exp_in, 16)

            def store_out(b, tiles, rows=P):
                for s in tiles:
                    sp.wait_ge(yo_ready[s], b + 1)
                    sp.dma_start(out[bass.ds((4 * b + s) * P, rows), :], YO[0:rows, s, :]).then_inc(out_done[s], 16)

            with sp.Fori(0, NBLK) as b:
                store_out(b, range(4))
            store_out(NBLK, (0,), LAST)
            for s in range(4):
                sp.wait_ge(out_done[s], 16 * (NBLK + (s == 0)))

        @block.gpsimd
        def _(pool):
            chain = Chain(pool, pool_step)
            for m in (ident, ones, zeros, onesb, from_here, row0, hmask):
                chain.mark(pool.memset(m[:, :], {"ident": 0.0, "zeros": 0.0, "from_here": -1.0}.get(m.name, 1.0)))
            chain.mark(pool.memset(RESTART[:, :], 1.0))
            chain.mark(pool.memset(RSB[:, :, :], 1.0))
            chain.mark(pool.memset(RSG[:, :, :], 1.0))
            chain.mark(pool.memset(eps_ln[:, :], EPS_LN))
            chain.mark(pool.memset(mhalf[:, :], -0.5))
            chain.mark(pool.memset(VX[:, :, :, :], 1.0))
            chain.settle()
            chain.mark(pool.affine_select(out=ident[:, :], in_=ident[:, :], compare_op=ALU.not_equal, fill=1.0,
                                          base=0, pattern=[[-1, P]], channel_multiplier=1))
            chain.mark(pool.affine_select(out=from_here[:, :], in_=from_here[:, :], compare_op=ALU.is_ge, fill=0.0,
                                          base=0, pattern=[[-1, P]], channel_multiplier=1))
            chain.mark(pool.affine_select(out=row0[:, :], in_=row0[:, :], compare_op=ALU.is_ge, fill=0.0,
                                          base=0, pattern=[[0, P]], channel_multiplier=-1))
            for base, cm, hs in ((0, 1, -HD), (HD - 1, -1, HD)):
                chain.link(pool.affine_select(out=hmask[:, 0:P].rearrange("p (h d) -> p h d", d=HD),
                                              in_=hmask[:, 0:P].rearrange("p (h d) -> p h d", d=HD),
                                              compare_op=ALU.is_ge, fill=0.0, base=base,
                                              pattern=[[hs, HH], [0, HD]], channel_multiplier=cm))
                chain.link(pool.affine_select(out=hmask[:, P:VE], in_=hmask[:, P:VE],
                                              compare_op=ALU.is_ge, fill=0.0, base=base,
                                              pattern=[[hs, HH]], channel_multiplier=cm))
            chain.mark(pool.memset(RESTART[:, :].rearrange("p (g k) -> p g k", k=GC)[:, :, 0:1], 0.0))
            chain.mark(pool.memset(RSB[:, :, 0:1], 0.0))
            chain.mark(pool.memset(RSG[:, :, 0:1], 0.0))
            chain.mark(pool.iota(iota_i[:, :], pattern=[[1, COLS]], base=0, channel_multiplier=0))
            chain.mark(pool.iota(local_i[:, :], pattern=[[0, 1]], base=0, channel_multiplier=1))
            chain.settle()
            pool.tensor_copy(iota_c[:, :], iota_i[:, :]).then_inc(pool_const, 1)
            pool.tensor_copy(iota[:, :], iota_i[:, 0:P]).then_inc(pool_const, 1)

            def keep_xn(i, slots, ready, kept):
                for s in slots:
                    pool.wait_ge(ready[s], i + 1)
                    pool.tensor_copy(XN[:, tile(2 * i + s)], XS[:, s, :]).then_inc(kept[s], 1)

            with pool.Fori(0, PAIRS) as i:
                keep_xn(i, (0, 1), xs_ready, xn_kept)
            keep_xn(PAIRS, (0,), xs_ready, xn_kept)

            def gather(d):
                first = isinstance(d, int)
                for h in range(2):
                    if not first:
                        pool.wait_ge(chunk_mm[1], d * (DZ // 2) - (DZ // 2 - 3 * (h + 1)))
                        for r in range(h * 6, h * 6 + 6):
                            pool.wait_ge(gathered[r], d * 16)
                    copy = pool.tensor_copy(IDXS[:, h, :], SIX[:, bass.ds(d * DZ + 6 * h, 6)])
                    if first:
                        copy.then_inc(idx_first, 1)
                        pool.wait_ge(idx_first, h + 1)
                    else:
                        copy.then_inc(idx_staged[h], 16)
                        pool.wait_ge(slots_ready, 1)
                        pool.wait_ge(idx_staged[h], d * 16)
                    for k in range(6):
                        r = 6 * h + k
                        pool.indirect_dma_start(RING[:, r, :], None, xg_dram,
                                                bass.IndirectOffsetOnAxis(ap=IDXS[:, h, k:k + 1], axis=0)
                                                ).then_inc(gathered[r], 16)

            pool.wait_ge(slots_ready, 1)
            pool.wait_ge(xg_out[0], 16 * (PAIRS + 1))
            pool.wait_ge(xg_out[1], 16 * PAIRS)
            gather(0)
            with pool.Fori(1, DOZENS) as d:
                gather(d)

            with pool.Fori(0, PAIRS) as i:
                keep_xn(i, (0, 1), f_xs, f_kept)
            keep_xn(PAIRS, (0,), f_xs, f_kept)

            def rstd3(b):
                pool.wait_ge(v3_ready, b + 1)
                pool.tensor_tensor(RS3[:, :], VE3[:, :], mhalf[:, :], ALU.pow).then_inc(rs3_ready, 1)

            with pool.Fori(0, NBLK) as b:
                rstd3(b)
            rstd3(NBLK)

        @block.scalar
        def _(act):
            act.wait_ge(pool_const, 2)
            act.wait_ge(aggr_done, 1)
            act.activation(SD[:, :], MV[:, :, 1], ACT.Sqrt, bias=eps_ln[:, 0:1]).then_inc(std_ready, 1)
            act.wait_ge(rstd_ready, 1)

            def norm_tiles(i, slots):
                for s in slots:
                    t = 2 * i + s
                    act.wait_ge(tp_done[s], i)
                    act.wait_ge(xn_kept[s], i)
                    act.activation(XS[:, s, :], X[:, tile(t)], ACT.Identity, bias=NM[:, bass.ds(t, 1)],
                                   scale=RS[:, bass.ds(t, 1)]).then_inc(xs_ready[s], 1)
                for s in slots:
                    act.wait_ge(tp_done[s], i + 1)
                    act.wait_ge(g_done[s], i)
                    act.copy(XT[:, :, s, :], bank[3 * s][:, 0:C].rearrange("p (c n) -> p c n", n=P)).then_inc(xt_ready[s], 1)
                for s in slots:
                    act.wait_ge(g_done[s], i + 1)
                    act.wait_ge(xg_out[s], i * 16)
                    act.copy(XGS[:, s, :], bank[1 + s][:, 0:C]).then_inc(xg_evac[s], 1)

            with act.Fori(0, PAIRS) as i:
                norm_tiles(i, (0, 1))
            norm_tiles(PAIRS, (0,))

            with act.Fori(0, NG // 2) as g:
                for s in range(2):
                    act.wait_ge(grp_done[s], g + 1)
                    act.wait_ge(placed[s], g)
                    act.copy(GS[:, s, :], bank[4 + s][:, 0:P]).then_inc(gs_ready[s], 1)

            for s in range(2):
                act.wait_ge(xn_kept[s], PAIRS + (s == 0))
                act.wait_ge(g_done[s], PAIRS + (s == 0))

            def loop_a(i, slots):
                for s in slots:
                    act.wait_ge(a_tp[s], i)
                    act.copy(XS[:, s, :], XN[:, tile(2 * i + s)]).then_inc(a_xs[s], 1)
                for s in slots:
                    act.wait_ge(a_tp[s], i + 1)
                    act.wait_ge(q_done, i)
                    act.copy(XT[:, :, s, :], bank[s][:, 0:C].rearrange("p (c n) -> p c n", n=P)).then_inc(a_xt[s], 1)
                for s in slots:
                    act.wait_ge(kv_done[s], i + 1)
                    act.wait_ge(ks_ready[s], i)
                    act.activation(NK[:, s, :], bank[2 + s][:, 0:C], ACT.Relu, scale=-1.0).then_inc(nk_ready[s], 1)
                    act.activation(KR[:, s, :], bank[2 + s][:, 0:C], ACT.Relu)
                    act.wait_ge(kvacc_done[s], i)
                    act.copy(VX[:, s, :, 0:P], bank[2 + s][:, C:2 * C].rearrange("p (c n) -> p c n", n=P)).then_inc(vx_ready[s], 1)
                    act.wait_ge(nk_ready[s], i + 1)
                    act.activation(EXK[:, s, :], NK[:, s, :], ACT.Exp, scale=-1.0).then_inc(ek_ready[s], 1)
                n = len(slots) * P
                q = bank[5][:, :].rearrange("p (c n) -> p c n", c=CC)[:, :, 0:n]
                act.wait_ge(q_done, i + 1)
                act.wait_ge(qt_ready, i)
                act.activation(NQ[:, :, 0:n], q, ACT.Relu, scale=-1.0).then_inc(nq_ready, 1)
                act.activation(QR[:, :, 0:n], q, ACT.Relu)
                act.wait_ge(nq_ready, i + 1)
                act.activation(EQ[:, :, 0:n], NQ[:, :, 0:n], ACT.Exp, scale=-1.0).then_inc(eq_ready, 1)

            with act.Fori(0, PAIRS) as i:
                loop_a(i, (0, 1))
            loop_a(PAIRS, (0,))

            def loop_b(i, slots):
                n = len(slots) * P
                for s in slots:
                    act.wait_ge(t_done[s], i)
                    act.wait_ge(qt_ready, PAIRS + 1)
                    act.copy(QS[:, s, :, :], QT[:, :, toks(2 * i + s)]).then_inc(qs_ready[s], 1)
                act.wait_ge(var1, i + 1)
                act.activation(SD2[:, 0:len(slots)], MV2[:, 0:len(slots), 1], ACT.Sqrt, bias=eps_ln[:, 0:1]).then_inc(sd1, 1)
                act.wait_ge(x1tp, i + 1)
                act.wait_ge(h_done, i)
                act.copy(XT[:, :, 0:len(slots), :].rearrange("p c s n -> p s c n"),
                         bank[0][:, 0:len(slots) * C].rearrange("p (s c n) -> p s c n", n=P, c=CC)).then_inc(x1t, 1)
                act.wait_ge(h_done, i + 1)
                for s in slots:
                    act.wait_ge(y_done[s], i)
                for c in range(CC):
                    ins = act.activation(HS[:, c, 0:len(slots), :],
                                         bank[5][:, c * 2 * P:c * 2 * P + n].rearrange("p (s n) -> p s n", n=P),
                                         ACT.Gelu, bias=B1C[:, c:c + 1])
                    ins.then_inc(hs_ready, 1)
                act.wait_ge(var2, i + 1)
                act.activation(SD2[:, 0:len(slots)], MV2[:, 0:len(slots), 1], ACT.Sqrt, bias=eps_ln[:, 0:1]).then_inc(sd2, 1)

            with act.Fori(0, PAIRS) as i:
                loop_b(i, (0, 1))
            loop_b(PAIRS, (0,))

            act.wait_ge(f_aggr, 1)
            act.activation(SD[:, :], MV[:, :, 1], ACT.Sqrt, bias=eps_ln[:, 0:1]).then_inc(f_sd, 1)
            act.wait_ge(f_rstd, 1)

            def ffn_norm(i, slots):
                for s in slots:
                    t = 2 * i + s
                    act.wait_ge(f_tp[s], i)
                    act.wait_ge(f_kept[s], i)
                    act.activation(XS[:, s, :], X[:, tile(t)], ACT.Identity, bias=NM[:, bass.ds(t, 1)],
                                   scale=RS[:, bass.ds(t, 1)]).then_inc(f_xs[s], 1)
                for s in slots:
                    act.wait_ge(f_tp[s], i + 1)
                    act.copy(QT[:, :, toks(2 * i + s)],
                             bank[s][:, 0:C].rearrange("p (c n) -> p c n", n=P)).then_inc(f_xt[s], 1)

            with act.Fori(0, PAIRS) as i:
                ffn_norm(i, (0, 1))
            ffn_norm(PAIRS, (0,))

            for n, width in enumerate((NE, NE, TOPK)):
                act.wait_ge(r_shift, n + 1)
                act.activation(R[0:1, 11, 0:width], R[0:1, 10, 0:width], ACT.Exp).then_inc(r_exp, 1)

            act.wait_ge(exp_in, 16 * 4 * TOPK)
            def up(b, width):
                for n in range(TOPK * FJ):
                    s = n % 2
                    act.wait_ge(up_done[s], b * (TOPK * FJ // 2) + (n // 2 + 1))
                    if n == 0:
                        act.wait_ge(down_done[0], b * 2)
                        act.wait_ge(down_done[1], b * 2)
                    act.activation(HF[:, n, 0:width], bank[1 + s][:, 0:width], ACT.Gelu,
                                   bias=FB1[:, n // FJ, n % FJ:n % FJ + 1]).then_inc(gelu_done[s], 1)

            with act.Fori(0, NBLK) as b:
                up(b, BLK)
            up(NBLK, P)

        @block.vector
        def _(dve):
            chain = Chain(dve, dve_step)
            V = nc.vector
            def bcast(ap, shape):
                return ap.to_broadcast(shape)

            def settle_for_aggr():
                chain.settle()
                V.memset(carrier[0:1, 0:1], 0.0)

            def mean_and_variance():
                st = ST[:, :].rearrange("p (t k) -> p k t", k=6)
                chain.mark(V.tensor_tensor(SD[:, :], st[:, 1, :], st[:, 4, :], ALU.add))
                chain.mark(V.tensor_tensor(RS[:, :], st[:, 1, :], st[:, 4, :], ALU.subtract))
                chain.mark(V.tensor_tensor(NM[:, :], st[:, 2, :], st[:, 5, :], ALU.add))
                chain.settle()
                chain.mark(V.tensor_scalar(MV[:, :, 0], SD[:, :], 0.5, None, ALU.mult))
                chain.mark(V.scalar_tensor_tensor(out=RS[:, :], in0=RS[:, :], scalar=0.25, in1=RS[:, :], op0=ALU.mult, op1=ALU.mult))
                chain.settle()
                return V.scalar_tensor_tensor(out=MV[:, :, 1], in0=NM[:, :], scalar=1.0 / C, in1=RS[:, :], op0=ALU.mult, op1=ALU.add)

            dve.wait_ge(x_in, 16)
            with dve.Fori(0, TILES) as t:
                V.bn_stats(ST[:, bass.ds(t * 6, 6)], X[:, tile(t)]).then_inc(stats_done, 1)
            dve.wait_ge(stats_done, TILES)
            mean_and_variance().then_inc(aggr_done, 1)
            dve.wait_ge(std_ready, 1)
            chain.link(V.reciprocal(RS[:, :], SD[:, :]))
            V.scalar_tensor_tensor(out=NM[:, :], in0=MV[:, :, 0], scalar=-1.0, in1=RS[:, :],
                                   op0=ALU.mult, op1=ALU.mult).then_inc(rstd_ready, 1)

            dve.wait_ge(e_in, 48)
            chain.mark(V.tensor_scalar(EBI[:, :], EROW[:, :], 7, None, ALU.arith_shift_right))
            chain.mark(V.tensor_scalar(ELO[:, :], EROW[:, :], P - 1, None, ALU.bitwise_and))
            chain.mark(V.tensor_scalar(EPCI[:, :], ECOL[:, :], 7, None, ALU.arith_shift_left))
            chain.settle()
            chain.mark(V.tensor_copy(EBF[:, :], EBI[:, :]))
            chain.link(V.tensor_tensor(TMPI[:, :], EPCI[:, :], ELO[:, :], ALU.bitwise_or))
            chain.link(V.tensor_copy(EPC[:, :], TMPI[:, :]))

            dve.wait_ge(pool_const, 2)
            with chain.loop(TILES, 1) as b:
                chain.mark(V.tensor_scalar(OH[:, bass.ds(b, 1), :].rearrange("p a k -> p (a k)"), EBF[:, :],
                                           iota[:, bass.ds(b, 1)], None, ALU.is_equal))
            chain.settle()
            with dve.Fori(0, TILES) as b:
                V.tensor_tensor_scan(SC[:, bass.ds(b, 1), :].rearrange("p a k -> p (a k)"), RESTART[:, :],
                                     OH[:, bass.ds(b, 1), :].rearrange("p a k -> p (a k)"), 0.0,
                                     ALU.mult, ALU.add).then_inc(counted, 1)
            dve.wait_ge(totals_done, 1)
            HB = TILES // 2
            chain.mark(V.tensor_copy(CNT[:, 0:HB, :], bank[4][:, 0:HB * NG].rearrange("p (b g) -> p b g", g=NG)))
            chain.link(V.tensor_copy(CNT[:, HB:TILES, :], bank[5][:, 0:(TILES - HB) * NG].rearrange("p (b g) -> p b g", g=NG)))
            flat = lambda m: m[:, :, :].rearrange("p a b -> p (a b)")
            gb = lambda m: m[:, :, :].rearrange("p b g -> p g b")
            chain.link(V.tensor_tensor_scan(flat(Q1), flat(RSB), flat(CNT), 0.0, ALU.mult, ALU.add))
            chain.mark(V.tensor_tensor(flat(Q0), flat(Q1), flat(CNT), ALU.subtract))
            chain.mark(V.tensor_copy(flat(Q1I), flat(Q1)))
            chain.mark(V.tensor_scalar(NBF[:, :], Q1[:, :, NG - 1], float(P - 1), None, ALU.add))
            chain.settle()
            chain.mark(V.tensor_copy(flat(Q0I), flat(Q0)))
            chain.mark(V.tensor_copy(NBI[:, :], NBF[:, :]))
            chain.settle()
            chain.mark(V.tensor_scalar(flat(QLI), flat(Q0I), P - 1, None, ALU.bitwise_and))
            chain.mark(V.tensor_scalar(flat(Q0I), flat(Q0I), 7, None, ALU.arith_shift_right))
            chain.mark(V.tensor_scalar(flat(Q1I), flat(Q1I), 7, None, ALU.arith_shift_right))
            chain.mark(V.tensor_scalar(NBI[:, :], NBI[:, :], 7, None, ALU.arith_shift_right))
            chain.settle()
            chain.mark(V.tensor_copy(flat(F0), flat(Q0I)))
            chain.mark(V.tensor_copy(flat(F1), flat(Q1I)))
            chain.mark(V.tensor_copy(TAB0[:, :, :], gb(QLI)))
            chain.mark(V.tensor_copy(NBF[:, :], NBI[:, :]))
            chain.settle()
            chain.mark(V.tensor_tensor(flat(F1), flat(F1), flat(F0), ALU.subtract))
            chain.mark(V.tensor_tensor_scan(CBI[:, :], ones[:, 0:TILES], NBF[:, :], 0.0, ALU.mult, ALU.add))
            chain.settle()
            chain.mark(V.tensor_scalar(TCH[:, :, :], gb(F1), 1.0, None, ALU.add))
            chain.mark(V.tensor_tensor(CB[:, :], CBI[:, :], NBF[:, :], ALU.subtract))
            chain.settle()
            chain.mark(V.tensor_tensor(CBD[:, :], CB[:, :], ident[:, 0:TILES], ALU.mult))
            chain.link(V.tensor_tensor_scan(flat(LINC), flat(RSG), flat(TCH), 0.0, ALU.mult, ALU.add))
            chain.mark(V.tensor_reduce(CBP[:, :], CBD[:, :], AX.X, ALU.add))
            chain.mark(V.tensor_tensor(flat(LOFF), flat(LINC), flat(TCH), ALU.subtract))
            chain.mark(V.tensor_tensor(DC[:, :, :], gb(F0), CB[:, :].rearrange("p (o b) -> p o b", o=1).to_broadcast([P, NG, TILES]), ALU.add))
            chain.settle()
            V.tensor_scalar(flat(TAB1), flat(LOFF), float(P), None, ALU.mult).then_inc(tables_ready, 1)
            V.tensor_scalar(CMP[:, :], iota_c[:, :], CBP[:, 0:1], None, ALU.is_ge).then_inc(bid_cmp, 1)
            chain.link(V.tensor_tensor(flat(DC), flat(DC), flat(LOFF), ALU.subtract))
            chain.mark(V.tensor_copy(DD[:, :, 0:1], DC[:, :, 0:1]))
            chain.mark(V.tensor_tensor(DD[:, :, 1:TILES], DC[:, :, 1:TILES], DC[:, :, 0:TILES - 1], ALU.subtract))
            chain.mark(V.tensor_scalar(local_i[:, :], local_i[:, :], LC - 1, None, ALU.bitwise_and))
            chain.settle()
            chain.link(V.tensor_copy(local_p[:, :], local_i[:, :]))
            chain.link(V.scalar_tensor_tensor(out=flat(DC), in0=flat(LOFF), scalar=local_p[:, 0:1], in1=flat(DD),
                                              op0=ALU.is_le, op1=ALU.mult))
            chain.link(V.tensor_reduce(JMAP[:, :], DC[:, :, :], AX.X, ALU.add))
            chain.link(V.tensor_scalar(JMAP[:, :], JMAP[:, :], local_p[:, 0:1], None, ALU.add))
            dve.wait_ge(bid_sum, 1)
            V.tensor_scalar(BID[0:1, :], bank[6][0:1, 0:COLS], -1.0, float(C), ALU.add, ALU.mult).then_inc(bid_ready, 1)
            dve.wait_ge(bid_ready, 1)

            def slot_rank(g, s):
                dve.wait_ge(rank_done[s], g + 1)
                G = 2 * g + s
                ohg = OH[:, :, bass.ds(G * GC, GC)]
                V.tensor_tensor(PRD[:, :, :], bank[4 + s][:, 0:TILES * GC].rearrange("p (b k) -> p b k", k=GC),
                                ohg, ALU.mult).then_inc(rank_read[s], 1)
                dve.wait_ge(rank_read[s], g + 1)
                chain.link(V.tensor_reduce(SLOT[:, bass.ds(G * GC, GC)], PRD[:, :, :].rearrange("p b k -> p k b"),
                                           AX.X, ALU.add))

            with chain.loop(NG // 2, 2) as g:
                slot_rank(g, 0)
                slot_rank(g, 1)
            chain.link(V.tensor_copy(SLOTI[:, :], SLOT[:, :]))
            chain.mark(V.tensor_scalar(TMPI[:, :], SLOTI[:, :], 7, None, ALU.arith_shift_right))
            chain.mark(V.tensor_scalar(SLOTI[:, :], SLOTI[:, :], P - 1, None, ALU.bitwise_and))
            chain.settle()
            chain.mark(V.tensor_copy(LCOL[:, :], TMPI[:, :]))
            chain.mark(V.tensor_copy(LANE[:, :], SLOTI[:, :]))
            chain.settle()

            def group_operands(g, s):
                dve.wait_ge(grp_done[s], g)
                G = 2 * g + s
                for k in range(GC):
                    at = bass.ds(G * GC + k, 1)
                    V.tensor_scalar(AS[:, s, k, 0:LC], iota[:, 0:LC], LCOL[:, at], EW[:, at], ALU.is_equal, ALU.mult)
                    V.tensor_scalar(AS[:, s, k, LC:2 * LC], iota[:, 0:LC], LCOL[:, at], EPC[:, at], ALU.is_equal, ALU.mult)
                    ins = V.tensor_scalar(OI[:, s, k, :], iota[:, :], LANE[:, at], None, ALU.is_equal)
                ins.then_inc(ops_ready[s], 1)
                dve.wait_ge(placed[s], g)
                V.tensor_scalar(OJ[:, s, :], iota_c[:, :], JMAP[:, bass.ds(G, 1)], None, ALU.is_equal).then_inc(oj_ready[s], 1)

            with dve.Fori(0, NG // 2) as g:
                group_operands(g, 0)
                group_operands(g, 1)

            dve.wait_ge(table_done, 1)
            chain.mark(V.tensor_copy(SW[:, :], bank[6][:, 0:COLS]))
            chain.link(V.tensor_copy(SPI[:, :], bank[7][:, 0:COLS]))
            chain.mark(V.tensor_scalar(SLI[:, :], SPI[:, :], P - 1, None, ALU.bitwise_and))
            V.tensor_scalar(SIX[:, :], SPI[:, :], 7, None, ALU.arith_shift_right).then_inc(slots_ready, 1)
            chain.settle()
            chain.link(V.tensor_copy(SLO[:, :], SLI[:, :]))
            chain.link(V.tensor_tensor(L2B, L2B, GNB[:, :], ALU.add))

            def half_dozen(d, h):
                base = [dve.value_load(BID[0:1, bass.ds(d * DZ + 6 * h + k, 1)], min_val=0, max_val=(TILES - 1) * C)
                        for k in range(6)]

                def select(k):
                    r = 6 * h + k
                    s = r % 2
                    at = bass.ds(d * DZ + r, 1)
                    dve.wait_ge(chunk_mm[s], d * (DZ // 2) + r // 2)
                    V.tensor_scalar(SEL[:, s, :], iota[:, :], SLO[:, at], SW[:, at], ALU.is_equal, ALU.mult).then_inc(sel_ready[s], 1)

                def add(k):
                    r = 6 * h + k
                    s = r % 2
                    dve.wait_ge(chunk_mm[s], d * (DZ // 2) + (r // 2 + 1))
                    dve.wait_ge(x_added[1 - s], d * (DZ // 2) + (r + 1) // 2)
                    xt = X[:, bass.ds(base[k], C)]
                    V.tensor_tensor(xt, bank[6 + s][:, 0:C], xt, ALU.add).then_inc(x_added[s], 1)

                for k in range(6):
                    select(k)
                    if k:
                        add(k - 1)
                add(5)

            def a_feature(i, slots):
                for s in slots:
                    dve.wait_ge(ek_ready[s], i + 1)
                    dve.wait_ge(kvacc_done[s], i)
                    V.tensor_tensor(KS[:, s, :], KR[:, s, :], EXK[:, s, :], ALU.add).then_inc(ks_ready[s], 1)
                n = len(slots) * P
                dve.wait_ge(eq_ready, i + 1)
                V.tensor_tensor(QT[:, :, toks(2 * i, n)], QR[:, :, 0:n], EQ[:, :, 0:n], ALU.add).then_inc(qt_ready, 1)

            with dve.Fori(0, PAIRS) as i:
                half_dozen(i, 0)
                a_feature(i, (0, 1))
                half_dozen(i, 1)
            a_feature(PAIRS, (0,))

            dve.wait_ge(kv_summed, 1)
            for c in range(CC):
                ins = V.tensor_tensor(KVM[:, c, :], bank[4][:, c * VE:(c + 1) * VE], hmask[:, :], ALU.mult)
                ins.then_inc(kvm_ready, 1)

            def links(steps, carried=False):
                for step in steps:
                    for ins in step:
                        chain.mark(ins())
                    if carried and step is steps[-1]:
                        settle_for_aggr()
                    else:
                        chain.settle()

            def b_attend(i, slots):
                per_s = lambda f: [lambda s=s: f(s) for s in slots]
                for s in slots:
                    dve.wait_ge(t_done[s], i + 1)
                ps = lambda s: bank[1 + s][:, 0:CC * VE].rearrange("p (c n) -> p c n", n=VE)
                links([
                    per_s(lambda s: V.tensor_scalar(DEN[:, s, :].rearrange("p (c h) -> p c h", c=CC), ps(s)[:, :, P:VE], EPS_ATTN, None, ALU.add)),
                    per_s(lambda s: V.reciprocal(RZ[:, s, :], DEN[:, s, :])),
                    [lambda s=s, c=c: V.tensor_tensor(
                        TX[:, s, c * P:(c + 1) * P].rearrange("p (h d) -> p h d", d=HD),
                        ps(s)[:, c, 0:P].rearrange("p (h d) -> p h d", d=HD),
                        RZ[:, s, c * HH:(c + 1) * HH].rearrange("p (h o) -> p h o", o=1).to_broadcast([P, HH, HD]), ALU.mult)
                        for s in slots for c in range(CC)],
                    per_s(lambda s: V.tensor_tensor(TX[:, s, :], TX[:, s, :], XN[:, tile(2 * i + s)], ALU.add)),
                    per_s(lambda s: V.bn_stats(ST2[:, s, :], TX[:, s, :])),
                ], carried=True)
                for s in slots:
                    ins = V.bn_aggr(MV2[:, s, :], ST2[:, s, :])
                    if s == slots[-1]:
                        ins.then_inc(var1, 1)

            def b_norm(src, dst, gain, bias, slots, last):
                per_s = lambda f: [lambda s=s: f(s) for s in slots]
                n = len(slots)
                links([
                    [lambda: V.reciprocal(RS2[:, 0:n], SD2[:, 0:n])],
                    per_s(lambda s: V.tensor_scalar(TX2[:, s, :], src[:, s, :], MV2[:, s, 0:1], RS2[:, s:s + 1], ALU.subtract, ALU.mult)),
                    per_s(lambda s: V.tensor_tensor(TX2[:, s, :], TX2[:, s, :], gain, ALU.mult)),
                ])
                for s in slots:
                    last(s, V.tensor_tensor(dst[:, s, :], TX2[:, s, :], bias, ALU.add))

            def b_x1(i, slots):
                dve.wait_ge(sd1, i + 1)
                b_norm(TX, X1, L1G, L1B, slots, lambda s, ins: ins.then_inc(x1_ready[s], 1))

            def b_out(i, slots):
                per_s = lambda f: [lambda s=s: f(s) for s in slots]
                for s in slots:
                    dve.wait_ge(y_done[s], i + 1)
                    dve.wait_ge(x1_ready[s], i + 1)
                links([
                    per_s(lambda s: V.tensor_tensor(TX[:, s, :], bank[3 + s][:, 0:C], X1[:, s, :], ALU.add)),
                    per_s(lambda s: V.tensor_tensor(TX[:, s, :], TX[:, s, :], B2R, ALU.add)),
                    per_s(lambda s: V.bn_stats(ST2[:, s, :], TX[:, s, :])),
                ], carried=True)
                for s in slots:
                    ins = V.bn_aggr(MV2[:, s, :], ST2[:, s, :])
                    if s == slots[-1]:
                        ins.then_inc(var2, 1)

            def b_update(i, slots, rounds):
                dve.wait_ge(sd2, i + 1)
                b_norm(TX, TX2, L2G, L2B, slots, lambda s, ins: chain.mark(ins))
                chain.settle()
                for s in range(2):
                    dve.wait_ge(x_added[s], rounds * (DZ // 2))
                for s in slots:
                    xt = X[:, tile(2 * i + s)]
                    chain.mark(V.tensor_tensor(xt, xt, TX2[:, s, :], ALU.add))
                chain.settle()

            with chain.loop(PAIRS, 1 * 0 + 2 * 2 + 4 + 2 + 2 + 1 + 2 + 2 + 2 + 2 + 2 + 1 + 2 + 2 + 2 + 2) as i:
                d = i * 2 + PAIRS
                b_attend(i, (0, 1))
                half_dozen(d, 0)
                b_x1(i, (0, 1))
                half_dozen(d, 1)
                b_out(i, (0, 1))
                half_dozen(d + 1, 0)
                half_dozen(d + 1, 1)
                b_update(i, (0, 1), d + 2)
            b_attend(PAIRS, (0,))
            b_x1(PAIRS, (0,))
            half_dozen(DOZENS - 1, 0)
            b_out(PAIRS, (0,))
            half_dozen(DOZENS - 1, 1)
            b_update(PAIRS, (0,), DOZENS)

            with dve.Fori(0, TILES) as t:
                V.bn_stats(ST[:, bass.ds(t * 6, 6)], X[:, tile(t)]).then_inc(f_stats, 1)
            dve.wait_ge(f_stats, TILES)
            mean_and_variance().then_inc(f_aggr, 1)
            dve.wait_ge(f_sd, 1)
            chain.link(V.reciprocal(RS[:, :], SD[:, :]))
            V.scalar_tensor_tensor(out=NM[:, :], in0=MV[:, :, 0], scalar=-1.0, in1=RS[:, :],
                                   op0=ALU.mult, op1=ALU.mult).then_inc(f_rstd, 1)

            dve.wait_ge(mean_done, 1)
            V.tensor_scalar(MEAN[:, :], bank[3][:, 0:CC], 1.0 / N, None, ALU.mult).then_inc(mean_ready, 1)
            dve.wait_ge(logits_done, 1)
            chain.link(V.tensor_tensor(R[0:1, 0, :], bank[4][0:1, 0:NE], RB[:, :], ALU.add))

            def softmax(src, dst, width, n):
                chain.link(V.tensor_reduce(R[0:1, 1, 0:1], src, AX.X, ALU.max))
                V.tensor_scalar(R[0:1, 10, 0:width], src, R[0:1, 1, 0:1], None, ALU.subtract).then_inc(r_shift, 1)
                dve.wait_ge(r_exp, n)
                chain.link(V.tensor_reduce(R[0:1, 1, 1:2], R[0:1, 11, 0:width], AX.X, ALU.add))
                chain.link(V.reciprocal(R[0:1, 1, 2:3], R[0:1, 1, 1:2]))
                return V.tensor_scalar(dst, R[0:1, 11, 0:width], R[0:1, 1, 2:3], None, ALU.mult)

            chain.link(softmax(R[0:1, 0, :], R[0:1, 2, :], NE, 1))
            chain.link(V.tensor_scalar(R[0:1, 3, :], R[0:1, 2, :], float(N), 1.0, ALU.mult, ALU.max))
            chain.link(V.reciprocal(R[0:1, 4, :], R[0:1, 3, :]))
            chain.link(V.tensor_scalar(R[0:1, 5, :], R[0:1, 4, :], CAPACITY, 1.0, ALU.mult, ALU.min))
            chain.link(V.tensor_tensor(R[0:1, 6, :], R[0:1, 2, :], R[0:1, 5, :], ALU.mult))
            chain.link(softmax(R[0:1, 6, :], R[0:1, 7, :], NE, 2))
            chain.link(V.max(R[0:1, 8, :], R[0:1, 7, :]))
            V.max_index(RI[0:1, :], R[0:1, 8, :], R[0:1, 7, :]).then_inc(topi_ready, 1)
            softmax(R[0:1, 8, 0:TOPK], R[0:1, 9, 0:TOPK], TOPK, 3).then_inc(topw_ready, 1)
            dve.wait_ge(wb_done, 1)
            chain.link(V.tensor_copy(WB[:, :], bank[5][:, 0:TOPK]))
            dve.wait_ge(exp_in, 16 * 4 * TOPK)
            for e in range(TOPK):
                chain.mark(V.tensor_scalar(FW2[:, e * FJ:(e + 1) * FJ, :], FW2[:, e * FJ:(e + 1) * FJ, :], WB[:, e:e + 1], None, ALU.mult))
            chain.link(V.tensor_scalar(B2C[:, :], FB2[:, 0, :], WB[:, 0:1], None, ALU.mult))
            V.scalar_tensor_tensor(out=B2C[:, :], in0=FB2[:, 1, :], scalar=WB[:, 1:2], in1=B2C[:, :],
                                   op0=ALU.mult, op1=ALU.add).then_inc(w2_scaled, 1)
            dve.wait_ge(w2_scaled, 1)

            def ffn_out(b, tiles):
                for s in tiles:
                    u = s % 2
                    dve.wait_ge(down_done[u], b * 2 + (s // 2 + 1))
                    V.tensor_tensor(Y[:, s, :], bank[4 + u][:, 0:C], XN[:, tile(4 * b + s)], ALU.add).then_inc(y_read[u], 1)
                    dve.wait_ge(y_read[u], b * 2 + (s // 2 + 1))
                    chain.link(V.tensor_tensor(Y[:, s, :], Y[:, s, :], B2C[:, :], ALU.add))
                    chain.mark(V.bn_stats(ST3[:, s, :], Y[:, s, :]))
                    settle_for_aggr()
                    chain.mark(V.bn_aggr(MV3[:, s, :], ST3[:, s, :]))
                chain.settle()
                dve.wait_ge(rs3_ready, b)
                V.tensor_scalar(VE3[:, :], MV3[:, :, 1], EPS_LN, None, ALU.add).then_inc(v3_ready, 1)
                dve.wait_ge(rs3_ready, b + 1)
                for s in tiles:
                    chain.link(V.tensor_scalar(Y[:, s, :], Y[:, s, :], MV3[:, s, 0:1], RS3[:, s:s + 1], ALU.subtract, ALU.mult))
                    chain.link(V.tensor_tensor(Y[:, s, :], Y[:, s, :], FG, ALU.mult))
                    chain.link(V.tensor_tensor(Y[:, s, :], Y[:, s, :], FB, ALU.add))
                    dve.wait_ge(out_done[s], b * 16)
                    V.tensor_tensor(YO[:, s, :], Y[:, s, :], X[:, tile(4 * b + s)], ALU.add).then_inc(yo_ready[s], 1)

            with chain.loop(NBLK, 4 * 6) as b:
                ffn_out(b, range(4))
            ffn_out(NBLK, (0,))

        @block.tensor
        def _(pe):
            T = nc.tensor
            pe.wait_ge(w_in, 16 * 15)
            pe.wait_ge(pool_const, 2)

            def transpose_tile(into, src):
                for c in range(CC):
                    ins = T.transpose(into[:, c * P:(c + 1) * P], src[:, c * P:(c + 1) * P], ident[:, :])
                return ins

            def xg_tiles(i, slots):
                for s in slots:
                    pe.wait_ge(xs_ready[s], i + 1)
                    pe.wait_ge(xt_ready[s], i)
                    transpose_tile(bank[3 * s], XS[:, s, :]).then_inc(tp_done[s], 1)
                for s in slots:
                    pe.wait_ge(xt_ready[s], i + 1)
                    pe.wait_ge(xg_evac[s], i)
                    for c in range(CC):
                        ins = T.matmul(bank[1 + s][:, 0:C], XT[:, c, s, :], GW[:, c, :], start=(c == 0), stop=(c == CC - 1))
                    ins.then_inc(g_done[s], 1)

            with pe.Fori(0, PAIRS) as i:
                xg_tiles(i, (0, 1))
            xg_tiles(PAIRS, (0,))

            HB = TILES // 2
            pe.wait_ge(counted, TILES)
            last_k = SC[:, :, :].rearrange("p b (g k) -> p b g k", k=GC)[:, :, :, GC - 1]
            T.matmul(bank[4][:, 0:HB * NG], onesb[:, :], last_k[:, 0:HB, :], start=True, stop=True)
            T.matmul(bank[5][:, 0:(TILES - HB) * NG], onesb[:, :], last_k[:, HB:TILES, :], start=True, stop=True).then_inc(totals_done, 1)
            pe.wait_ge(bid_cmp, 1)
            T.matmul(bank[6][0:1, 0:COLS], ones[0:TILES, 0:1], CMP[0:TILES, :], start=True, stop=True).then_inc(bid_sum, 1)

            pe.wait_ge(tables_ready, 1)

            def rank(g, s):
                G = 2 * g + s
                pe.wait_ge(rank_read[s], g)
                at = bass.ds(G * GC, GC)
                ps = bank[4 + s][:, 0:TILES * GC]
                tab = lambda m: m[:, bass.ds(G, 1), :].rearrange("p g (b o) -> p (g b) o", o=1).to_broadcast([P, TILES, GC])
                T.matmul(ps, onesb[:, :], SC[:, :, at], start=True, stop=False)
                T.matmul(ps, from_here[:, :], OH[:, :, at], start=False, stop=False)
                T.matmul(ps, row0[:, :], tab(TAB0), start=False, stop=False)
                T.matmul(ps, row0[:, :], tab(TAB1), start=False, stop=True).then_inc(rank_done[s], 1)

            with pe.Fori(0, NG // 2) as g:
                rank(g, 0)
                rank(g, 1)

            pe.wait_ge(bid_ready, 1)
            T.matmul(bank[6][:, 0:COLS], zeros[:, :], iota_c[:, :], start=True, stop=False)
            T.matmul(bank[7][:, 0:COLS], zeros[:, :], iota_c[:, :], start=True, stop=False)

            def group(g, s):
                pe.wait_ge(ops_ready[s], g + 1)
                pe.wait_ge(gs_ready[s], g)
                for k in range(GC):
                    ins = T.matmul(bank[4 + s][:, 0:P], AS[:, s, k, :], OI[:, s, k, :], start=(k == 0), stop=(k == GC - 1))
                ins.then_inc(grp_done[s], 1)

            def place(g, s):
                pe.wait_ge(gs_ready[s], g + 1)
                pe.wait_ge(oj_ready[s], g + 1)
                T.matmul(bank[6][:, 0:COLS], GS[0:LC, s, :], OJ[0:LC, s, :], start=False, stop=False, skip_group_check=True)
                T.matmul(bank[7][:, 0:COLS], GS[LC:2 * LC, s, :], OJ[LC:2 * LC, s, :], start=False, stop=False, skip_group_check=True).then_inc(placed[s], 1)

            for s in range(2):
                pe.wait_ge(rank_read[s], NG // 2)
            with pe.Fori(0, NG // 2) as g:
                group(g, 0)
                group(g, 1)
                place(g, 0)
                place(g, 1)
            T.matmul(bank[6][:, 0:COLS], zeros[:, :], iota_c[:, :], start=False, stop=True)
            T.matmul(bank[7][:, 0:COLS], zeros[:, :], iota_c[:, :], start=False, stop=True).then_inc(table_done, 1)

            def half_dozen(d, h):
                for k in range(6):
                    r = 6 * h + k
                    s = r % 2
                    pe.wait_ge(sel_ready[s], d * (DZ // 2) + (r // 2 + 1))
                    pe.wait_ge(x_added[s], d * (DZ // 2) + r // 2)
                    pe.wait_ge(gathered[r], d * 16 + 16)
                    T.matmul(bank[6 + s][:, 0:C], SEL[:, s, :], RING[:, r, :], start=True, stop=True).then_inc(chunk_mm[s], 1)

            pe.wait_ge(slots_ready, 1)
            T.matmul(bank[4][:, 0:CC * VE], zeros[:, :], iota_c[:, 0:CC * VE], start=True, stop=False)

            def a_project(i, slots):
                for s in slots:
                    pe.wait_ge(a_xs[s], i + 1)
                    pe.wait_ge(a_xt[s], i)
                    transpose_tile(bank[s], XS[:, s, :]).then_inc(a_tp[s], 1)
                for s in slots:
                    pe.wait_ge(a_xt[s], i + 1)
                    pe.wait_ge(vx_ready[s], i)
                    for c in range(CC):
                        ins = T.matmul(bank[2 + s][:, :], XT[:, c, s, :], QKVW[:, c, C:3 * C], start=(c == 0), stop=(c == CC - 1))
                    ins.then_inc(kv_done[s], 1)
                pe.wait_ge(eq_ready, i)
                n = len(slots) * P
                for h in range(CC):
                    for c in range(CC):
                        ins = T.matmul(bank[5][:, h * 2 * P:h * 2 * P + n], QKVW[:, c, h * P:(h + 1) * P],
                                       XT[:, c, 0:len(slots), :], start=(c == 0), stop=(c == CC - 1))
                ins.then_inc(q_done, 1)

            def a_outer(i, slots, rows=P):
                for s in slots:
                    pe.wait_ge(ks_ready[s], i + 1)
                    pe.wait_ge(vx_ready[s], i + 1)
                    for c in range(CC):
                        ins = T.matmul(bank[4][:, c * VE:(c + 1) * VE], KS[0:rows, s, c * P:(c + 1) * P], VX[0:rows, s, c, :],
                                       start=False, stop=False, skip_group_check=True)
                    ins.then_inc(kvacc_done[s], 1)

            with pe.Fori(0, PAIRS) as i:
                a_project(i, (0, 1))
                half_dozen(i, 0)
                a_outer(i, (0, 1))
                half_dozen(i, 1)
            a_project(PAIRS, (0,))
            a_outer(PAIRS, (0,), LAST)
            T.matmul(bank[4][:, 0:CC * VE], zeros[:, :], iota_c[:, 0:CC * VE], start=False, stop=True).then_inc(kv_summed, 1)

            pe.wait_ge(kvm_ready, CC)

            def b_attend(i, slots):
                for s in slots:
                    pe.wait_ge(qs_ready[s], i + 1)
                    pe.wait_ge(x1_ready[s], i)
                    for c in range(CC):
                        ins = T.matmul(bank[1 + s][:, c * VE:(c + 1) * VE], QS[:, s, c, :], KVM[:, c, :], start=True, stop=True)
                    ins.then_inc(t_done[s], 1)

            def b_transpose(i, slots):
                pe.wait_ge(x1t, i)
                for s in slots:
                    pe.wait_ge(x1_ready[s], i + 1)
                    ins = transpose_tile(bank[0][:, s * C:(s + 1) * C], X1[:, s, :])
                ins.then_inc(x1tp, 1)

            def b_hidden(i, slots):
                n = len(slots) * P
                pe.wait_ge(x1t, i + 1)
                pe.wait_ge(hs_ready, i * CC)
                for h in range(CC):
                    for c in range(CC):
                        ins = T.matmul(bank[5][:, h * 2 * P:h * 2 * P + n], W1[:, c, h * P:(h + 1) * P],
                                       XT[:, c, 0:len(slots), :], start=(c == 0), stop=(c == CC - 1))
                ins.then_inc(h_done, 1)

            def b_project(i, slots):
                pe.wait_ge(hs_ready, i * CC + CC)
                pe.wait_ge(var2, i)
                for s in slots:
                    for h in range(CC):
                        ins = T.matmul(bank[3 + s][:, 0:C], HS[:, h, s, :], W2[:, h, :], start=(h == 0), stop=(h == CC - 1))
                    ins.then_inc(y_done[s], 1)

            with pe.Fori(0, PAIRS) as i:
                d = i * 2 + PAIRS
                b_attend(i, (0, 1))
                half_dozen(d, 0)
                b_transpose(i, (0, 1))
                half_dozen(d, 1)
                b_hidden(i, (0, 1))
                b_project(i, (0, 1))
                half_dozen(d + 1, 0)
                half_dozen(d + 1, 1)
            b_attend(PAIRS, (0,))
            b_transpose(PAIRS, (0,))
            half_dozen(DOZENS - 1, 0)
            b_hidden(PAIRS, (0,))
            b_project(PAIRS, (0,))
            half_dozen(DOZENS - 1, 1)

            pe.wait_ge(f_rstd, 1)
            T.matmul(bank[3][:, 0:CC], zeros[:, :], iota_c[:, 0:CC], start=True, stop=False)

            def ffn_in(i, slots, rows=P):
                for s in slots:
                    pe.wait_ge(f_xs[s], i + 1)
                    pe.wait_ge(f_xt[s], i)
                    for c in range(CC):
                        T.matmul(bank[3][:, c:c + 1], XS[0:rows, s, c * P:(c + 1) * P], ones[0:rows, 0:1],
                                 start=False, stop=False, skip_group_check=True)
                    transpose_tile(bank[s], XS[:, s, :]).then_inc(f_tp[s], 1)

            with pe.Fori(0, PAIRS) as i:
                ffn_in(i, (0, 1))
            ffn_in(PAIRS, (0,), LAST)
            T.matmul(bank[3][:, 0:CC], zeros[:, :], iota_c[:, 0:CC], start=False, stop=True).then_inc(mean_done, 1)
            pe.wait_ge(mean_ready, 1)
            for c in range(CC):
                ins = T.matmul(bank[4][0:1, 0:NE], MEAN[:, c:c + 1], RW[:, c, :], start=(c == 0), stop=(c == CC - 1))
            ins.then_inc(logits_done, 1)
            pe.wait_ge(topw_ready, 1)
            T.matmul(bank[5][:, 0:TOPK], ones[0:1, :], R[0:1, 9, 0:TOPK], start=True, stop=True).then_inc(wb_done, 1)
            pe.wait_ge(exp_in, 16 * 4 * TOPK)
            for s in range(2):
                pe.wait_ge(f_xt[s], PAIRS + (s == 0))

            def up(b, width):
                for n in range(TOPK * FJ):
                    s = n % 2
                    e, j = divmod(n, FJ)
                    pe.wait_ge(gelu_done[s], b * (TOPK * FJ // 2) + n // 2)
                    for c in range(CC):
                        ins = T.matmul(bank[1 + s][:, 0:width], FW1[:, e, c, j * P:(j + 1) * P],
                                       QT[:, c, bass.ds(b * BLK, width)], start=(c == 0), stop=(c == CC - 1))
                    ins.then_inc(up_done[s], 1)

            def down(b, tiles):
                for s in range(2):
                    pe.wait_ge(gelu_done[s], b * (TOPK * FJ // 2) + TOPK * FJ // 2)
                for t in tiles:
                    u = t % 2
                    pe.wait_ge(y_read[u], b * 2 + t // 2)
                    for n in range(TOPK * FJ):
                        ins = T.matmul(bank[4 + u][:, 0:C], HF[:, n, t * P:(t + 1) * P], FW2[:, n, :],
                                       start=(n == 0), stop=(n == TOPK * FJ - 1))
                    ins.then_inc(down_done[u], 1)

            pe.wait_ge(w2_scaled, 1)
            with pe.Fori(0, NBLK) as b:
                up(b, BLK)
                down(b, range(4))
            up(NBLK, P)
            down(NBLK, (0,))


def kernel(**inputs):
    import numpy as _np
    import concourse.bacc as _bacc
    from concourse import mybir as _mybir
    from concourse.bass_utils import run_bass_kernel_spmd as _run

    get = lambda n: _np.asarray(inputs[n])
    x = get("x")
    n, c = x.shape
    tiles = -(-n // 128)
    n_edges = get("src").shape[0]
    chunks = -(-n_edges // (128 * 13)) * 13

    def edges(a):
        flat = _np.zeros(128 * chunks, a.dtype)
        flat[:n_edges] = a
        return flat.reshape(128, chunks)

    xp = _np.zeros((tiles * 128, c), x.dtype)
    xp[:n] = x
    b1 = get("L0_ffn_b1")
    ne, ff = b1.shape
    rowv = lambda name: get(name).reshape(1, -1)
    laid = {
        "x": xp, "row": edges(get("src")), "col": edges(get("dst")), "weight": edges(get("edge_weight")),
        "gnn_wT": get("L0_gnn_W").T, "gnn_b": rowv("L0_gnn_b"), "qkv_wT": get("L0_mix_Wqkv").T,
        "ln1_g": rowv("L0_mix_ln1_g"), "ln1_b": rowv("L0_mix_ln1_b"), "mix_w1T": get("L0_mix_W1").T,
        "mix_b1": get("L0_mix_b1").reshape(-1, 128).T, "mix_w2T": get("L0_mix_W2").T, "mix_b2": rowv("L0_mix_b2"),
        "ln2_g": rowv("L0_mix_ln2_g"), "ln2_b": rowv("L0_mix_ln2_b"),
        "router_w": get("L0_ffn_Wr"), "router_b": rowv("L0_ffn_br"), "exp_w1": get("L0_ffn_W1"),
        "exp_b1": b1.reshape(ne, ff // 128, 128).transpose(0, 2, 1), "exp_w2": get("L0_ffn_W2"), "exp_b2": get("L0_ffn_b2"),
        "ffn_g": rowv("L0_ffn_gamma"), "ffn_b": rowv("L0_ffn_beta"),
    }
    nc = _bacc.Bacc("TRN2", target_bir_lowering=False, num_devices=1)
    arrays, args = {}, []
    for name, a in laid.items():
        a = _np.ascontiguousarray(a)
        arrays[f"in_{name}"] = a
        args.append(nc.dram_tensor(f"in_{name}", a.shape, _mybir.dt.from_np(a.dtype), kind="ExternalInput").ap())
    f32 = _mybir.dt.float32
    args.append(nc.dram_tensor("out_0", (n, c), f32, kind="ExternalOutput").ap())
    args.append(nc.dram_tensor("xg_rows", (tiles * 128, c), f32, kind="Internal").ap())
    gps_layer_program(nc, *args)
    r = _run(nc, [arrays], core_ids=[0])
    return r.results[0]["out_0"]
```

```python
import concourse.bass as bass
from concourse import mybir
from contextlib import ExitStack, contextmanager


def gps_layer_program(nc, x, row, col, weight, gnn_wT, gnn_b, qkv_wT, ln1_g, ln1_b, mix_w1T, mix_b1,
                      mix_w2T, mix_b2, ln2_g, ln2_b, router_w, router_b, exp_w1, exp_b1, exp_w2, exp_b2,
                      ffn_g, ffn_b, out, xg_dram):
    f32, bf16, i32, u32 = mybir.dt.float32, mybir.dt.bfloat16, mybir.dt.int32, mybir.dt.uint32
    ALU, ACT, AX = mybir.AluOpType, mybir.ActivationFunctionType, mybir.AxisListType

    P = 128
    N, C = out.shape
    TILES = x.shape[0] // P
    PAIRS = TILES // 2
    LAST = N - (TILES - 1) * P
    H, HD = 8, C // 8
    HH = H // 2
    CC = C // P
    EPS_ATTN, EPS_LN = 1e-6, 1e-5
    NE, FF = exp_w1.shape[0], exp_w1.shape[2]
    FJ = FF // P
    TOPK = 2
    CAPACITY = float(-(-N * 5 // (4 * NE)))

    EK = row.shape[1]
    GC = 13
    NG = EK // GC
    LC = 64
    assert NG * GC == EK and NG % 4 == 0 and TILES + GC + (TILES * (P - 1)) // P <= LC
    HAND = 6
    HANDS = 3
    RC = HANDS * HAND
    ROUNDS = 2 * PAIRS
    COLS = -(-(EK + TILES - 1) // HAND) * HAND
    TAIL = COLS // HAND - ROUNDS * HANDS
    assert TAIL == 2 and COLS <= 512
    VE = P + HH
    BLK = 4 * P
    NBLK = N // BLK

    ctx = ExitStack()
    with ctx:
        def sb(name, shape, dt=f32):
            return scope.enter_context(nc.sbuf_tensor(name, shape, dt))

        def sem(name):
            return ctx.enter_context(nc.semaphore(name))

        scope = ctx
        X = sb("X", [P, TILES * C])
        XN = sb("XN", [P, TILES * C])
        XS = sb("XS", [P, 2, C])
        XT = sb("XT", [P, CC, 2, P])
        XGS = sb("XGS", [P, 2, C])
        ST = sb("ST", [P, TILES * 6])
        MV = sb("MV", [P, TILES, 2])
        SD = sb("SD", [P, TILES])
        RS = sb("RS", [P, TILES])
        NM = sb("NM", [P, TILES])
        QKVW = sb("QKVW", [P, CC, 3 * C])
        GW = sb("GW", [P, CC, C])
        W1 = sb("W1", [P, CC, C])
        W2 = sb("W2", [P, CC, C])
        ROWC = sb("ROWC", [P, 7, C])
        L1G, L1B, B2R, L2G, L2B, FG, FB = (ROWC[:, n, :] for n in range(7))
        GNB = sb("GNB", [P, C])
        B1C = sb("B1C", [P, CC])
        carrier = sb("carrier", [P, 1])
        eps_ln = sb("eps_ln", [P, 1])
        ident = sb("ident", [P, P])
        iota = sb("iota", [P, P])
        iota_i = sb("iota_i", [P, COLS], i32)
        iota_c = sb("iota_c", [P, COLS])
        ones = sb("ones", [P, P])
        onesb = sb("onesb", [P, P], bf16)
        from_here = sb("from_here", [P, P], bf16)
        row0 = sb("row0", [P, P], bf16)
        zeros = sb("zeros", [P, P])
        local_p = sb("local_p", [P, 1])
        local_i = sb("local_i", [P, 1], i32)
        hmask = sb("hmask", [P, VE])

        SW = sb("SW", [P, COLS])
        SPI = sb("SPI", [P, COLS], i32)
        SLI = sb("SLI", [P, COLS], i32)
        SLO = sb("SLO", [P, COLS])
        SIX = sb("SIX", [P, COLS], i32)
        RW = sb("RW", [P, CC, NE])
        RB = sb("RB", [1, NE])
        BID = sb("BID", [1, ROUNDS + 1, -(-RC // 4) * 4], i32)
        VX = sb("VX", [P, 2, CC, VE])
        mhalf = sb("mhalf", [P, 4])

        scope = ctx.enter_context(ExitStack())
        EROW = sb("EROW", [P, EK], i32)
        ECOL = sb("ECOL", [P, EK], i32)
        EW = sb("EW", [P, EK])
        EBI = sb("EBI", [P, EK], i32)
        EBF = sb("EBF", [P, EK], bf16)
        ELO = sb("ELO", [P, EK], i32)
        EPCI = sb("EPCI", [P, EK], i32)
        EPC = sb("EPC", [P, EK])
        SLOT = sb("SLOT", [P, EK])
        SLOTI = EBI
        TMPI = sb("TMPI", [P, EK], i32)
        LANE = sb("LANE", [P, EK])
        LCOL = sb("LCOL", [P, EK])
        JMAP = sb("JMAP", [P, NG])
        JPAIR = sb("JPAIR", [P, NG // 2])
        sort_scope = scope
        scope = ctx.enter_context(ExitStack())
        RESTART = sb("RESTART", [P, EK], bf16)
        OH = sb("OH", [P, TILES, EK], bf16)
        SC = sb("SC", [P, TILES, EK], bf16)
        NT = TILES * NG
        CNT = sb("CNT", [P, TILES, NG])
        Q1 = sb("Q1", [P, TILES, NG])
        Q0 = sb("Q0", [P, TILES, NG])
        RSB = sb("RSB", [P, TILES, NG])
        Q1I = sb("Q1I", [P, TILES, NG], i32)
        Q0I = sb("Q0I", [P, TILES, NG], i32)
        QLI = sb("QLI", [P, TILES, NG], i32)
        F0, F1 = Q0, Q1
        TCH = sb("TCH", [P, NG, TILES])
        LINC = sb("LINC", [P, NG, TILES])
        LOFF = sb("LOFF", [P, NG, TILES])
        RSG = sb("RSG", [P, NG, TILES])
        TAB0 = sb("TAB0", [P, NG, TILES], bf16)
        TAB1 = sb("TAB1", [P, NG, TILES], bf16)
        DC = sb("DC", [P, NG, TILES])
        DD = LINC
        NBI = sb("NBI", [P, TILES], i32)
        NBF = sb("NBF", [P, TILES])
        CBI = sb("CBI", [P, TILES])
        CB = sb("CB", [P, TILES])
        CBD = sb("CBD", [P, TILES])
        CBP = sb("CBP", [P, 1])
        CMP = sb("CMP", [P, COLS])
        PRD = sb("PRD", [P, 2, TILES, GC])
        scope.close()
        scope = sort_scope
        LH = sb("LH", [P, 2, GC, LC])
        AS = sb("AS", [P, 4, GC, P])
        OI = sb("OI", [P, 4, GC, P])
        LD = sb("LD", [P, GC, P])
        GSW = sb("GSW", [P, 2, P])
        GSP = sb("GSP", [P, 2, P])
        OJ = sb("OJ", [P, 2, COLS])
        scope.close()
        QT = sb("QT", [P, CC, TILES * P])
        scope = ctx.enter_context(ExitStack())
        IDXS = sb("IDXS", [P, HANDS, HAND], i32)
        RING = sb("RING", [P, RC, C])
        SEL = sb("SEL", [P, HAND, P])

        NK = sb("NK", [P, 2, C])
        EXK = sb("EXK", [P, 2, C])
        KS = sb("KS", [P, 2, C])
        NQ = sb("NQ", [P, CC, 2 * P])
        QR = sb("QR", [P, CC, 2 * P])
        KR = sb("KR", [P, 2, C])
        EQ = sb("EQ", [P, CC, 2 * P])
        KVM = sb("KVM", [P, CC, VE])
        QS = sb("QS", [P, 2, CC, P])
        DEN = sb("DEN", [P, 2, H])
        RZ = sb("RZ", [P, 2, H])
        TX = sb("TX", [P, 2, C])
        TY = sb("TY", [P, 2, C])
        TN = sb("TN", [P, 2, C])
        X1 = sb("X1", [P, 2, C])
        ST2 = sb("ST2", [P, 2, 2, 6])
        MV2 = sb("MV2", [P, 2, 2, 2])
        SD2 = sb("SD2", [P, 2, 2])
        RS2 = sb("RS2", [P, 2, 2])
        HS = sb("HS", [P, CC, 2, P])
        scope.close()
        scope = ctx
        MEAN = sb("MEAN", [P, CC])
        R = sb("R", [1, 12, NE])
        RI = sb("RI", [1, NE], u32)
        WB = sb("WB", [P, TOPK])
        FW1 = sb("FW1", [P, TOPK, CC, FF])
        FW2 = sb("FW2", [P, TOPK * FJ, C])
        FB1 = sb("FB1", [P, TOPK, FJ])
        FB2 = sb("FB2", [P, TOPK, C])
        B2C = sb("B2C", [P, C])
        HF = sb("HF", [P, TOPK * FJ, BLK])
        Y = sb("Y", [P, 4, C])
        YO = sb("YO", [P, 4, C])
        ST3 = sb("ST3", [P, 4, 6])
        MV3 = sb("MV3", [P, 4, 2])
        VE3 = sb("VE3", [P, 4])
        RS3 = sb("RS3", [P, 4])

        bank = [ctx.enter_context(nc.psum_tensor(f"bank{n}", [P, 512], f32)) for n in range(8)]

        x_in = sem("x_in")
        w_in = sem("w_in")
        gw_in = sem("gw_in")
        e_in = sem("e_in")
        iota_ready = sem("iota_ready")
        pool_const = sem("pool_const")
        dve_const = sem("dve_const")
        stats_done = sem("stats_done")
        aggr_done = sem("aggr_done")
        std_ready = sem("std_ready")
        rstd_ready = sem("rstd_ready")
        xs_ready = [sem(f"xs_ready{s}") for s in range(2)]
        xn_kept = [sem(f"xn_kept{s}") for s in range(2)]
        tp_done = [sem(f"tp_done{s}") for s in range(2)]
        xt_ready = [sem(f"xt_ready{s}") for s in range(2)]
        g_done = [sem(f"g_done{s}") for s in range(2)]
        xg_evac = [sem(f"xg_evac{s}") for s in range(2)]
        xg_out = [sem(f"xg_out{s}") for s in range(2)]
        dve_step = sem("dve_step")
        act_step = sem("act_step")
        pool_step = sem("pool_step")
        counted = sem("counted")
        totals_done = sem("totals_done")
        tables_ready = sem("tables_ready")
        rank_done = [sem(f"rank_done{s}") for s in range(2)]
        rank_read = [sem(f"rank_read{s}") for s in range(2)]
        bid_cmp = sem("bid_cmp")
        bid_sum = sem("bid_sum")
        bid_ready = sem("bid_ready")
        as_ready = [sem(f"as_ready{s}") for s in range(4)]
        oi_ready = [sem(f"oi_ready{s}") for s in range(4)]
        grp_done = [sem(f"grp_done{s}") for s in range(4)]
        gs_ready = [sem(f"gs_ready{j}") for j in range(2)]
        oj_ready = [sem(f"oj_ready{j}") for j in range(2)]
        placed = [sem(f"placed{j}") for j in range(2)]
        lanes_ready = sem("lanes_ready")
        table_done = sem("table_done")
        slots_ready = sem("slots_ready")
        idx_first = sem("idx_first")
        x_biased = sem("x_biased")
        idx_staged = [sem(f"idx_staged{h}") for h in range(HANDS)]
        gathered = [sem(f"gathered{h}") for h in range(HANDS)]
        sel_ready = [sem(f"sel_ready{s}") for s in range(2)]
        chunk_mm = [sem(f"chunk_mm{s}") for s in range(2)]
        x_added = [sem(f"x_added{s}") for s in range(2)]
        a_xs = [sem(f"a_xs{s}") for s in range(2)]
        a_tp = [sem(f"a_tp{s}") for s in range(2)]
        a_xt = [sem(f"a_xt{s}") for s in range(2)]
        kv_done = [sem(f"kv_done{s}") for s in range(2)]
        nk_ready = [sem(f"nk_ready{s}") for s in range(2)]
        ek_ready = [sem(f"ek_ready{s}") for s in range(2)]
        vx_ready = [sem(f"vx_ready{s}") for s in range(2)]
        ks_ready = [sem(f"ks_ready{s}") for s in range(2)]
        kvacc_done = [sem(f"kvacc_done{s}") for s in range(2)]
        q_done = sem("q_done")
        nq_ready = sem("nq_ready")
        eq_ready = sem("eq_ready")
        qt_ready = sem("qt_ready")
        kv_summed = sem("kv_summed")
        kvm_ready = sem("kvm_ready")
        qs_ready = [sem(f"qs_ready{s}") for s in range(2)]
        t_done = [sem(f"t_done{s}") for s in range(2)]
        var1 = sem("var1")
        sd1 = sem("sd1")
        x1_ready = [sem(f"x1_ready{s}") for s in range(2)]
        x1tp = sem("x1tp")
        x1t = sem("x1t")
        h_done = sem("h_done")
        hs_ready = sem("hs_ready")
        y_done = [sem(f"y_done{s}") for s in range(2)]
        var2 = sem("var2")
        sd2 = sem("sd2")
        b_done = sem("b_done")
        f_stats = sem("f_stats")
        f_aggr = sem("f_aggr")
        f_sd = sem("f_sd")
        f_rstd = sem("f_rstd")
        f_xs = [sem(f"f_xs{s}") for s in range(2)]
        f_kept = [sem(f"f_kept{s}") for s in range(2)]
        f_tp = [sem(f"f_tp{s}") for s in range(2)]
        f_xt = [sem(f"f_xt{s}") for s in range(2)]
        mean_done = sem("mean_done")
        mean_ready = sem("mean_ready")
        logits_done = sem("logits_done")
        r_shift = sem("r_shift")
        r_exp = sem("r_exp")
        topi_ready = sem("topi_ready")
        topw_ready = sem("topw_ready")
        wb_done = sem("wb_done")
        exp_in = sem("exp_in")
        w2_scaled = sem("w2_scaled")
        up_done = [sem(f"up_done{s}") for s in range(2)]
        gelu_done = [sem(f"gelu_done{s}") for s in range(2)]
        down_done = [sem(f"down_done{s}") for s in range(2)]
        y_read = [sem(f"y_read{s}") for s in range(2)]
        v3_ready = sem("v3_ready")
        rs3_ready = sem("rs3_ready")
        yo_ready = [sem(f"yo_ready{s}") for s in range(4)]
        out_done = [sem(f"out_done{s}") for s in range(4)]

        WEIGHTS_IN = 16 * 14

        block = ctx.enter_context(nc.Block())

        def tile(t):
            return bass.ds(t * C, C)

        def toks(t, n=P):
            return bass.ds(t * P, n)

        class Chain:

            def __init__(self, eng, s):
                self.eng, self.s, self.n, self.local = eng, s, 0, 0

            def mark(self, ins):
                ins.then_inc(self.s, 1)
                self.n = self.n + 1
                self.local += 1

            def settle(self):
                self.eng.wait_ge(self.s, self.n)

            def link(self, ins):
                self.mark(ins)
                self.settle()

            @contextmanager
            def loop(self, trips, per, first=0):
                base = self.n
                with self.eng.Fori(first, first + trips) as i:
                    self.n, self.local = i * per + (base - first * per), 0
                    yield i
                    assert self.local == per, (self.local, per)
                self.n = base + trips * per

        @block.sync
        def _(sp):
            sp.dma_start(EROW[:, :], row).then_inc(e_in, 16)
            sp.dma_start(ECOL[:, :], col).then_inc(e_in, 16)
            sp.dma_start(EW[:, :], weight).then_inc(e_in, 16)
            sp.dma_start(X[:, :].rearrange("p (t c) -> p t c", c=C),
                         x.rearrange("(t p) c -> p t c", p=P)).then_inc(x_in, 16)
            sp.dma_start(GW[:, :, :], gnn_wT.rearrange("(c p) o -> p c o", p=P)).then_inc(gw_in, 16)
            sp.dma_start(QKVW[:, :, :], qkv_wT.rearrange("(c p) o -> p c o", p=P)).then_inc(w_in, 16)
            sp.dma_start(W1[:, :, :], mix_w1T.rearrange("(c p) o -> p c o", p=P)).then_inc(w_in, 16)
            sp.dma_start(W2[:, :, :], mix_w2T.rearrange("(c p) o -> p c o", p=P)).then_inc(w_in, 16)
            for dst, src in ((L1G, ln1_g), (L1B, ln1_b), (B2R, mix_b2), (L2G, ln2_g), (L2B, ln2_b),
                             (FG, ffn_g), (FB, ffn_b), (GNB[:, :], gnn_b)):
                sp.dma_start(dst, src.to_broadcast([P, C])).then_inc(w_in, 16)
            sp.dma_start(B1C[:, :], mix_b1).then_inc(w_in, 16)
            sp.dma_start(RW[:, :, :], router_w.rearrange("(c p) o -> p c o", p=P)).then_inc(w_in, 16)
            sp.dma_start(RB[:, :], router_b).then_inc(w_in, 16)

            def store_xg(i, slots):
                for s in slots:
                    sp.wait_ge(xg_evac[s], i + 1)
                    sp.dma_start(xg_dram[bass.ds((2 * i + s) * P, P), :], XGS[:, s, :]).then_inc(xg_out[s], 16)

            with sp.Fori(0, PAIRS) as i:
                store_xg(i, (0, 1))
            store_xg(PAIRS, (0,))

            sp.wait_ge(topi_ready, 1)
            for e in range(TOPK):
                v = sp.value_load(RI[0:1, e:e + 1], min_val=0, max_val=NE - 1)
                sp.dma_start(FW1[:, e, :, :], exp_w1[bass.ds(v, 1), :, :].rearrange("e (c p) f -> p (e c) f", p=P)).then_inc(exp_in, 16)
                sp.dma_start(FW2[:, e * FJ:(e + 1) * FJ, :], exp_w2[bass.ds(v, 1), :, :].rearrange("e (j p) d -> p (e j) d", p=P)).then_inc(exp_in, 16)
                sp.dma_start(FB1[:, e, :], exp_b1[bass.ds(v, 1), :, :].rearrange("e p j -> p (e j)")).then_inc(exp_in, 16)
                sp.dma_start(FB2[:, e, :], exp_b2[bass.ds(v, 1), :].to_broadcast([P, C])).then_inc(exp_in, 16)

            def store_out(b, tiles, rows=P):
                for s in tiles:
                    sp.wait_ge(yo_ready[s], b + 1)
                    sp.dma_start(out[bass.ds((4 * b + s) * P, rows), :], YO[0:rows, s, :]).then_inc(out_done[s], 16)

            with sp.Fori(0, NBLK) as b:
                store_out(b, range(4))
            store_out(NBLK, (0,), LAST)
            for s in range(4):
                sp.wait_ge(out_done[s], 16 * (NBLK + (s == 0)))

        @block.gpsimd
        def _(pool):
            chain = Chain(pool, pool_step)
            chain.mark(pool.iota(iota_i[:, :], pattern=[[1, COLS]], base=0, channel_multiplier=0))
            chain.mark(pool.iota(local_i[:, :], pattern=[[0, 1]], base=0, channel_multiplier=1))
            chain.settle()
            pool.tensor_copy(iota[:, :], iota_i[:, 0:P]).then_inc(iota_ready, 1)
            for m in (ident, ones, zeros, onesb, from_here, row0, hmask):
                chain.mark(pool.memset(m[:, :], {"ident": 0.0, "zeros": 0.0, "from_here": -1.0}.get(m.name, 1.0)))
            chain.mark(pool.memset(RESTART[:, :], 1.0))
            chain.mark(pool.memset(RSB[:, :, :], 1.0))
            chain.mark(pool.memset(RSG[:, :, :], 1.0))
            chain.mark(pool.memset(eps_ln[:, :], EPS_LN))
            chain.mark(pool.memset(mhalf[:, :], -0.5))
            chain.mark(pool.memset(VX[:, :, :, :], 1.0))
            chain.settle()
            chain.mark(pool.affine_select(out=ident[:, :], in_=ident[:, :], compare_op=ALU.not_equal, fill=1.0,
                                          base=0, pattern=[[-1, P]], channel_multiplier=1))
            chain.mark(pool.affine_select(out=from_here[:, :], in_=from_here[:, :], compare_op=ALU.is_ge, fill=0.0,
                                          base=0, pattern=[[-1, P]], channel_multiplier=1))
            chain.mark(pool.affine_select(out=row0[:, :], in_=row0[:, :], compare_op=ALU.is_ge, fill=0.0,
                                          base=0, pattern=[[0, P]], channel_multiplier=-1))
            for base, cm, hs in ((0, 1, -HD), (HD - 1, -1, HD)):
                chain.link(pool.affine_select(out=hmask[:, 0:P].rearrange("p (h d) -> p h d", d=HD),
                                              in_=hmask[:, 0:P].rearrange("p (h d) -> p h d", d=HD),
                                              compare_op=ALU.is_ge, fill=0.0, base=base,
                                              pattern=[[hs, HH], [0, HD]], channel_multiplier=cm))
                chain.link(pool.affine_select(out=hmask[:, P:VE], in_=hmask[:, P:VE],
                                              compare_op=ALU.is_ge, fill=0.0, base=base,
                                              pattern=[[hs, HH]], channel_multiplier=cm))
            chain.mark(pool.memset(RESTART[:, :].rearrange("p (g k) -> p g k", k=GC)[:, :, 0:1], 0.0))
            chain.mark(pool.memset(RSB[:, :, 0:1], 0.0))
            chain.mark(pool.memset(RSG[:, :, 0:1], 0.0))
            chain.settle()
            pool.tensor_copy(iota_c[:, :], iota_i[:, :]).then_inc(pool_const, 1)

            def keep_xn(i, slots, ready, kept):
                for s in slots:
                    pool.wait_ge(ready[s], i + 1)
                    pool.tensor_copy(XN[:, tile(2 * i + s)], XS[:, s, :]).then_inc(kept[s], 1)

            with pool.Fori(0, PAIRS) as i:
                keep_xn(i, (0, 1), xs_ready, xn_kept)
            keep_xn(PAIRS, (0,), xs_ready, xn_kept)

            for t in range(2):
                pool.wait_ge(xs_ready[t], PAIRS + (t == 0))
            pool.wait_ge(w_in, WEIGHTS_IN)
            chain.link(pool.tensor_tensor(L2B, L2B, GNB[:, :], ALU.add))
            with pool.Fori(0, TILES) as t:
                pool.tensor_tensor(X[:, tile(t)], X[:, tile(t)], L2B, ALU.add).then_inc(x_biased, 1)

            GATHERED = 16 * HAND

            def stage(r, h):
                first = isinstance(r, int) and r == 0
                if not first:
                    pool.wait_ge(chunk_mm[1], r * (RC // 2) - (RC // 2 - (h + 1) * (HAND // 2)))
                    pool.wait_ge(gathered[h], r * GATHERED)
                pool.tensor_copy(IDXS[:, h, :], SIX[:, bass.ds(r * RC + h * HAND, HAND)]
                                 ).then_inc(idx_first if first else idx_staged[h], 1 if first else GATHERED)

            def gather(r, h):
                first = isinstance(r, int) and r == 0
                if first:
                    pool.wait_ge(idx_first, h + 1)
                else:
                    pool.wait_ge(slots_ready, 1)
                    pool.wait_ge(idx_staged[h], r * GATHERED)
                for k in range(HAND):
                    pool.indirect_dma_start(RING[:, h * HAND + k, :], None, xg_dram,
                                            bass.IndirectOffsetOnAxis(ap=IDXS[:, h, k:k + 1], axis=0)
                                            ).then_inc(gathered[h], 16)

            pool.wait_ge(slots_ready, 1)
            pool.wait_ge(xg_out[0], 16 * (PAIRS + 1))
            pool.wait_ge(xg_out[1], 16 * PAIRS)
            for h in range(HANDS):
                stage(0, h)
            for h in range(HANDS):
                gather(0, h)
            with pool.Fori(1, ROUNDS) as r:
                for h in range(HANDS):
                    stage(r, h)
                    gather(r, h)
            for h in range(TAIL):
                stage(ROUNDS, h)
                gather(ROUNDS, h)

            with pool.Fori(0, PAIRS) as i:
                keep_xn(i, (0, 1), f_xs, f_kept)
            keep_xn(PAIRS, (0,), f_xs, f_kept)

            def rstd3(b):
                pool.wait_ge(v3_ready, b + 1)
                pool.tensor_tensor(RS3[:, :], VE3[:, :], mhalf[:, :], ALU.pow).then_inc(rs3_ready, 1)

            with pool.Fori(0, NBLK) as b:
                rstd3(b)
            rstd3(NBLK)

        @block.scalar
        def _(act):
            act.wait_ge(pool_const, 1)
            act.wait_ge(aggr_done, 1)
            act.activation(SD[:, :], MV[:, :, 1], ACT.Sqrt, bias=eps_ln[:, 0:1]).then_inc(std_ready, 1)
            act.wait_ge(rstd_ready, 1)

            def normalise(i, s):
                act.wait_ge(tp_done[s], i)
                act.wait_ge(xn_kept[s], i)
                act.activation(XS[:, s, :], X[:, tile(2 * i + s)], ACT.Identity, bias=NM[:, bass.ds(2 * i + s, 1)],
                               scale=RS[:, bass.ds(2 * i + s, 1)]).then_inc(xs_ready[s], 1)

            def xg_tiles(i, slots, following):
                for s in slots:
                    act.wait_ge(tp_done[s], i + 1)
                    act.wait_ge(g_done[s], i)
                    act.copy(XT[:, :, s, :], bank[3 * s][:, 0:C].rearrange("p (c n) -> p c n", n=P)).then_inc(xt_ready[s], 1)
                    if s in following:
                        normalise(i + 1, s)
                for s in slots:
                    act.wait_ge(g_done[s], i + 1)
                    act.wait_ge(xg_out[s], i * 16)
                    act.copy(XGS[:, s, :], bank[1 + s][:, 0:C]).then_inc(xg_evac[s], 1)

            normalise(0, 0)
            normalise(0, 1)
            with act.Fori(0, PAIRS - 1) as i:
                xg_tiles(i, (0, 1), (0, 1))
            xg_tiles(PAIRS - 1, (0, 1), (0,))
            xg_tiles(PAIRS, (0,), ())

            chain = Chain(act, act_step)
            act.wait_ge(lanes_ready, 1)

            def lanes(i, s):
                act.wait_ge(grp_done[s], i)
                act.wait_ge(oi_ready[2 - s], i + s // 2)
                for k in range(GC):
                    ins = act.activation(LD[:, k, :], iota[:, :], ACT.Abs, scale=-1.0, bias=LANE[:, bass.ds((4 * i + s) * GC + k, 1)])
                chain.link(ins)
                act.activation(OI[:, s, :, :], LD[:, :, :], ACT.Relu, scale=-1.0, bias=ones[:, 0:1]).then_inc(oi_ready[s], 1)

            def evacuate(i, j):
                act.wait_ge(placed[j], i)
                for u in range(2):
                    s = 2 * j + u
                    act.wait_ge(grp_done[s], i + 1)
                    act.copy(GSW[u * LC:(u + 1) * LC, j, :], bank[s][0:LC, 0:P])
                    ins = act.copy(GSP[u * LC:(u + 1) * LC, j, :], bank[s][LC:2 * LC, 0:P])
                ins.then_inc(gs_ready[j], 1)

            def sort_step(i, before=True):
                lanes(i, 0)
                if before:
                    evacuate(i - 1, 1)
                lanes(i, 2)
                evacuate(i, 0)

            sort_step(0, before=False)
            with chain.loop(NG // 4 - 1, 2, first=1) as i:
                sort_step(i)
            evacuate(NG // 4 - 1, 1)

            for s in range(2):
                act.wait_ge(xn_kept[s], PAIRS + (s == 0))
                act.wait_ge(g_done[s], PAIRS + (s == 0))

            def loop_a(i, slots):
                for s in slots:
                    act.wait_ge(a_tp[s], i)
                    act.copy(XS[:, s, :], XN[:, tile(2 * i + s)]).then_inc(a_xs[s], 1)
                for s in slots:
                    act.wait_ge(a_tp[s], i + 1)
                    act.wait_ge(q_done, i)
                    act.copy(XT[:, :, s, :], bank[s][:, 0:C].rearrange("p (c n) -> p c n", n=P)).then_inc(a_xt[s], 1)
                for s in slots:
                    act.wait_ge(kv_done[s], i + 1)
                    act.wait_ge(ks_ready[s], i)
                    act.activation(NK[:, s, :], bank[2 + s][:, 0:C], ACT.Relu, scale=-1.0).then_inc(nk_ready[s], 1)
                    act.activation(KR[:, s, :], bank[2 + s][:, 0:C], ACT.Relu)
                    act.wait_ge(kvacc_done[s], i)
                    act.copy(VX[:, s, :, 0:P], bank[2 + s][:, C:2 * C].rearrange("p (c n) -> p c n", n=P)).then_inc(vx_ready[s], 1)
                    act.wait_ge(nk_ready[s], i + 1)
                    act.activation(EXK[:, s, :], NK[:, s, :], ACT.Exp, scale=-1.0).then_inc(ek_ready[s], 1)
                n = len(slots) * P
                q = bank[5][:, :].rearrange("p (c n) -> p c n", c=CC)[:, :, 0:n]
                act.wait_ge(q_done, i + 1)
                act.wait_ge(qt_ready, i)
                act.activation(NQ[:, :, 0:n], q, ACT.Relu, scale=-1.0).then_inc(nq_ready, 1)
                act.activation(QR[:, :, 0:n], q, ACT.Relu)
                act.wait_ge(nq_ready, i + 1)
                act.activation(EQ[:, :, 0:n], NQ[:, :, 0:n], ACT.Exp, scale=-1.0).then_inc(eq_ready, 1)

            with act.Fori(0, PAIRS) as i:
                loop_a(i, (0, 1))
            loop_a(PAIRS, (0,))

            def b_query(i, slots):
                for s in slots:
                    act.wait_ge(t_done[s], i)
                    act.wait_ge(qt_ready, PAIRS + 1)
                    act.copy(QS[:, s, :, :], QT[:, :, toks(2 * i + s)]).then_inc(qs_ready[s], 1)

            def b_std(i, slots, m, var, sd):
                act.wait_ge(var, i + 1)
                act.activation(SD2[:, m, 0:len(slots)], MV2[:, m, 0:len(slots), 1], ACT.Sqrt, bias=eps_ln[:, 0:1]).then_inc(sd, 1)

            def b_hidden(i, slots):
                n = len(slots) * P
                act.wait_ge(x1tp, i + 1)
                act.wait_ge(h_done, i)
                act.copy(XT[:, :, 0:len(slots), :].rearrange("p c s n -> p s c n"),
                         bank[0][:, 0:len(slots) * C].rearrange("p (s c n) -> p s c n", n=P, c=CC)).then_inc(x1t, 1)
                act.wait_ge(h_done, i + 1)
                for s in slots:
                    act.wait_ge(y_done[s], i)
                for c in range(CC):
                    ins = act.activation(HS[:, c, 0:len(slots), :],
                                         bank[5][:, c * 2 * P:c * 2 * P + n].rearrange("p (s n) -> p s n", n=P),
                                         ACT.Gelu, bias=B1C[:, c:c + 1])
                    ins.then_inc(hs_ready, 1)

            b_query(0, (0, 1))
            b_std(0, (0, 1), 0, var1, sd1)
            b_hidden(0, (0, 1))
            with act.Fori(1, PAIRS) as i:
                b_query(i, (0, 1))
                b_std(i, (0, 1), 0, var1, sd1)
                b_std(i - 1, (0, 1), 1, var2, sd2)
                b_hidden(i, (0, 1))
            b_query(PAIRS, (0,))
            b_std(PAIRS, (0,), 0, var1, sd1)
            b_std(PAIRS - 1, (0, 1), 1, var2, sd2)
            b_hidden(PAIRS, (0,))
            b_std(PAIRS, (0,), 1, var2, sd2)

            act.wait_ge(f_aggr, 1)
            act.activation(SD[:, :], MV[:, :, 1], ACT.Sqrt, bias=eps_ln[:, 0:1]).then_inc(f_sd, 1)
            act.wait_ge(f_rstd, 1)

            def ffn_norm(i, slots):
                for s in slots:
                    t = 2 * i + s
                    act.wait_ge(f_tp[s], i)
                    act.wait_ge(f_kept[s], i)
                    act.activation(XS[:, s, :], X[:, tile(t)], ACT.Identity, bias=NM[:, bass.ds(t, 1)],
                                   scale=RS[:, bass.ds(t, 1)]).then_inc(f_xs[s], 1)
                for s in slots:
                    act.wait_ge(f_tp[s], i + 1)
                    act.copy(QT[:, :, toks(2 * i + s)],
                             bank[s][:, 0:C].rearrange("p (c n) -> p c n", n=P)).then_inc(f_xt[s], 1)

            with act.Fori(0, PAIRS) as i:
                ffn_norm(i, (0, 1))
            ffn_norm(PAIRS, (0,))

            for n, width in enumerate((NE, NE, TOPK)):
                act.wait_ge(r_shift, n + 1)
                act.activation(R[0:1, 11, 0:width], R[0:1, 10, 0:width], ACT.Exp).then_inc(r_exp, 1)

            act.wait_ge(exp_in, 16 * 4 * TOPK)
            def up(b, width):
                for n in range(TOPK * FJ):
                    s = n % 2
                    act.wait_ge(up_done[s], b * (TOPK * FJ // 2) + (n // 2 + 1))
                    if n == 0:
                        act.wait_ge(down_done[0], b * 2)
                        act.wait_ge(down_done[1], b * 2)
                    act.activation(HF[:, n, 0:width], bank[1 + s][:, 0:width], ACT.Gelu,
                                   bias=FB1[:, n // FJ, n % FJ:n % FJ + 1]).then_inc(gelu_done[s], 1)

            with act.Fori(0, NBLK) as b:
                up(b, BLK)
            up(NBLK, P)

        @block.vector
        def _(dve):
            chain = Chain(dve, dve_step)
            V = nc.vector
            def bcast(ap, shape):
                return ap.to_broadcast(shape)

            def settle_for_aggr():
                chain.settle()
                V.memset(carrier[0:1, 0:1], 0.0)

            def mean_and_variance():
                st = ST[:, :].rearrange("p (t k) -> p k t", k=6)
                chain.mark(V.tensor_tensor(SD[:, :], st[:, 1, :], st[:, 4, :], ALU.add))
                chain.mark(V.tensor_tensor(RS[:, :], st[:, 1, :], st[:, 4, :], ALU.subtract))
                chain.mark(V.tensor_tensor(NM[:, :], st[:, 2, :], st[:, 5, :], ALU.add))
                chain.settle()
                chain.mark(V.tensor_scalar(MV[:, :, 0], SD[:, :], 0.5, None, ALU.mult))
                chain.mark(V.scalar_tensor_tensor(out=RS[:, :], in0=RS[:, :], scalar=0.25, in1=RS[:, :], op0=ALU.mult, op1=ALU.mult))
                chain.settle()
                return V.scalar_tensor_tensor(out=MV[:, :, 1], in0=NM[:, :], scalar=1.0 / C, in1=RS[:, :], op0=ALU.mult, op1=ALU.add)

            UN = 5
            assert TILES % UN == 0

            def statistics(done):
                with dve.Fori(0, TILES // UN) as n:
                    for m in range(UN):
                        t = n * UN + m
                        V.bn_stats(ST[:, bass.ds(t * 6, 6)], X[:, tile(t)]).then_inc(done, 1)
                dve.wait_ge(done, TILES)

            dve.wait_ge(e_in, 48)
            chain.mark(V.tensor_scalar(EBI[:, :], EROW[:, :], 7, None, ALU.arith_shift_right))
            chain.mark(V.tensor_scalar(ELO[:, :], EROW[:, :], P - 1, None, ALU.bitwise_and))
            chain.mark(V.tensor_scalar(EPCI[:, :], ECOL[:, :], 7, None, ALU.arith_shift_left))
            chain.settle()
            chain.mark(V.tensor_copy(EBF[:, :], EBI[:, :]))
            chain.link(V.tensor_tensor(TMPI[:, :], EPCI[:, :], ELO[:, :], ALU.bitwise_or))
            chain.link(V.tensor_copy(EPC[:, :], TMPI[:, :]))

            dve.wait_ge(iota_ready, 1)
            with chain.loop(TILES // UN, UN) as n:
                for m in range(UN):
                    b = n * UN + m
                    chain.mark(V.tensor_scalar(OH[:, bass.ds(b, 1), :].rearrange("p a k -> p (a k)"), EBF[:, :],
                                               iota[:, bass.ds(b, 1)], None, ALU.is_equal))

            dve.wait_ge(x_in, 16)
            statistics(stats_done)
            mean_and_variance().then_inc(aggr_done, 1)

            chain.settle()
            dve.wait_ge(pool_const, 1)

            def running_counts(b):
                V.tensor_tensor_scan(SC[:, bass.ds(b, 1), :].rearrange("p a k -> p (a k)"), RESTART[:, :],
                                     OH[:, bass.ds(b, 1), :].rearrange("p a k -> p (a k)"), 0.0,
                                     ALU.mult, ALU.add).then_inc(counted, 1)

            for b in range(UN):
                running_counts(b)
            dve.wait_ge(std_ready, 1)
            chain.link(V.reciprocal(RS[:, :], SD[:, :]))
            V.scalar_tensor_tensor(out=NM[:, :], in0=MV[:, :, 0], scalar=-1.0, in1=RS[:, :],
                                   op0=ALU.mult, op1=ALU.mult).then_inc(rstd_ready, 1)
            with dve.Fori(1, TILES // UN) as n:
                for m in range(UN):
                    running_counts(n * UN + m)
            dve.wait_ge(totals_done, 1)
            HB = TILES // 2
            chain.mark(V.tensor_copy(CNT[:, 0:HB, :], bank[4][:, 0:HB * NG].rearrange("p (b g) -> p b g", g=NG)))
            chain.link(V.tensor_copy(CNT[:, HB:TILES, :], bank[5][:, 0:(TILES - HB) * NG].rearrange("p (b g) -> p b g", g=NG)))
            flat = lambda m: m[:, :, :].rearrange("p a b -> p (a b)")
            gb = lambda m: m[:, :, :].rearrange("p b g -> p g b")
            chain.link(V.tensor_tensor_scan(flat(Q1), flat(RSB), flat(CNT), 0.0, ALU.mult, ALU.add))
            chain.mark(V.tensor_tensor(flat(Q0), flat(Q1), flat(CNT), ALU.subtract))
            chain.mark(V.tensor_copy(flat(Q1I), flat(Q1)))
            chain.mark(V.tensor_scalar(NBF[:, :], Q1[:, :, NG - 1], float(P - 1), None, ALU.add))
            chain.settle()
            chain.mark(V.tensor_copy(flat(Q0I), flat(Q0)))
            chain.mark(V.tensor_copy(NBI[:, :], NBF[:, :]))
            chain.settle()
            chain.mark(V.tensor_scalar(flat(QLI), flat(Q0I), P - 1, None, ALU.bitwise_and))
            chain.mark(V.tensor_scalar(flat(Q0I), flat(Q0I), 7, None, ALU.arith_shift_right))
            chain.mark(V.tensor_scalar(flat(Q1I), flat(Q1I), 7, None, ALU.arith_shift_right))
            chain.mark(V.tensor_scalar(NBI[:, :], NBI[:, :], 7, None, ALU.arith_shift_right))
            chain.settle()
            chain.mark(V.tensor_copy(flat(F0), flat(Q0I)))
            chain.mark(V.tensor_copy(flat(F1), flat(Q1I)))
            chain.mark(V.tensor_copy(TAB0[:, :, :], gb(QLI)))
            chain.mark(V.tensor_copy(NBF[:, :], NBI[:, :]))
            chain.settle()
            chain.mark(V.tensor_tensor(flat(F1), flat(F1), flat(F0), ALU.subtract))
            chain.mark(V.tensor_tensor_scan(CBI[:, :], ones[:, 0:TILES], NBF[:, :], 0.0, ALU.mult, ALU.add))
            chain.settle()
            chain.mark(V.tensor_scalar(TCH[:, :, :], gb(F1), 1.0, None, ALU.add))
            chain.mark(V.tensor_tensor(CB[:, :], CBI[:, :], NBF[:, :], ALU.subtract))
            chain.settle()
            chain.mark(V.tensor_tensor(CBD[:, :], CB[:, :], ident[:, 0:TILES], ALU.mult))
            chain.link(V.tensor_tensor_scan(flat(LINC), flat(RSG), flat(TCH), 0.0, ALU.mult, ALU.add))
            chain.mark(V.tensor_reduce(CBP[:, :], CBD[:, :], AX.X, ALU.add))
            chain.mark(V.tensor_tensor(flat(LOFF), flat(LINC), flat(TCH), ALU.subtract))
            chain.mark(V.tensor_tensor(DC[:, :, :], gb(F0), CB[:, :].rearrange("p (o b) -> p o b", o=1).to_broadcast([P, NG, TILES]), ALU.add))
            chain.settle()
            V.tensor_scalar(flat(TAB1), flat(LOFF), float(P), None, ALU.mult).then_inc(tables_ready, 1)
            V.tensor_scalar(CMP[:, :], iota_c[:, :], CBP[:, 0:1], None, ALU.is_ge).then_inc(bid_cmp, 1)
            chain.link(V.tensor_tensor(flat(DC), flat(DC), flat(LOFF), ALU.subtract))
            chain.mark(V.tensor_copy(DD[:, :, 0:1], DC[:, :, 0:1]))
            chain.mark(V.tensor_tensor(DD[:, :, 1:TILES], DC[:, :, 1:TILES], DC[:, :, 0:TILES - 1], ALU.subtract))
            chain.mark(V.tensor_scalar(local_i[:, :], local_i[:, :], LC - 1, None, ALU.bitwise_and))
            chain.settle()
            chain.link(V.tensor_copy(local_p[:, :], local_i[:, :]))
            chain.link(V.scalar_tensor_tensor(out=flat(DC), in0=flat(LOFF), scalar=local_p[:, 0:1], in1=flat(DD),
                                              op0=ALU.is_le, op1=ALU.mult))
            chain.link(V.tensor_reduce(JMAP[:, :], DC[:, :, :], AX.X, ALU.add))
            chain.link(V.tensor_scalar(JMAP[:, :], JMAP[:, :], local_p[:, 0:1], None, ALU.add))
            for u in range(2):
                of_u = JMAP[u * LC:(u + 1) * LC, :].rearrange("p (g u) -> p g u", u=2)[:, :, u]
                chain.mark(V.tensor_copy(JPAIR[u * LC:(u + 1) * LC, :], of_u))
            dve.wait_ge(bid_sum, 1)
            whole = ROUNDS * RC
            chain.link(V.tensor_scalar(BID[0:1, 0:ROUNDS, 0:RC], bank[6][0:1, 0:whole].rearrange("p (r c) -> p r c", c=RC),
                                       -1.0, float(C), ALU.add, ALU.mult))
            V.tensor_scalar(BID[0:1, ROUNDS, 0:COLS - whole], bank[6][0:1, whole:COLS],
                            -1.0, float(C), ALU.add, ALU.mult).then_inc(bid_ready, 1)
            dve.wait_ge(bid_ready, 1)

            def slot_rank(g):
                at = lambda s: bass.ds((2 * g + s) * GC, GC)
                so_far = chain.n
                for s in range(2):
                    dve.wait_ge(rank_done[s], g + 1)
                    dve.wait_ge(dve_step, so_far - 1 + s)
                    V.tensor_tensor(PRD[:, s, :, :], bank[4 + s][:, 0:TILES * GC].rearrange("p (b k) -> p b k", k=GC),
                                    OH[:, :, at(s)], ALU.mult).then_inc(rank_read[s], 1)
                for s in range(2):
                    dve.wait_ge(rank_read[s], g + 1)
                    chain.mark(V.tensor_reduce(SLOT[:, at(s)], PRD[:, s, :, :].rearrange("p b k -> p k b"), AX.X, ALU.add))

            with chain.loop(NG // 2, 2) as g:
                slot_rank(g)
            chain.settle()
            chain.link(V.tensor_copy(SLOTI[:, :], SLOT[:, :]))
            chain.mark(V.tensor_scalar(TMPI[:, :], SLOTI[:, :], 7, None, ALU.arith_shift_right))
            chain.mark(V.tensor_scalar(SLOTI[:, :], SLOTI[:, :], P - 1, None, ALU.bitwise_and))
            chain.settle()
            chain.mark(V.tensor_copy(LCOL[:, :], TMPI[:, :]))
            V.tensor_copy(LANE[:, :], SLOTI[:, :]).then_inc(lanes_ready, 1)
            chain.settle()
            dve.wait_ge(lanes_ready, 1)

            def per_chunk(m, i, s, n):
                return m[:, bass.ds((4 * i + s) * GC, GC)].rearrange("p (k o) -> p k o", o=1).to_broadcast([P, GC, n])

            def per_row(n):
                return iota[:, 0:n].rearrange("p (o m) -> p o m", o=1).to_broadcast([P, GC, n])

            def pair_operands(i, j):
                for u in range(2):
                    dve.wait_ge(as_ready[2 * (1 - j) + u], i + j)
                    chain.mark(V.tensor_tensor(LH[:, u, :, :], per_row(LC), per_chunk(LCOL, i, 2 * j + u, LC), ALU.is_equal))
                dve.wait_ge(grp_done[2 * j + 1], i)
                V.tensor_tensor(OI[:, 2 * j + 1, :, :], per_row(P), per_chunk(LANE, i, 2 * j + 1, P), ALU.is_equal
                                ).then_inc(oi_ready[2 * j + 1], 1)
                dve.wait_ge(grp_done[2 * j], i)
                chain.settle()
                for u in range(2):
                    s = 2 * j + u
                    chain.mark(V.tensor_tensor(AS[:, s, :, 0:LC], LH[:, u, :, :], per_chunk(EW, i, s, LC), ALU.mult))
                    V.tensor_tensor(AS[:, s, :, LC:2 * LC], LH[:, u, :, :], per_chunk(EPC, i, s, LC), ALU.mult).then_inc(as_ready[s], 1)
                dve.wait_ge(placed[j], i)
                V.tensor_scalar(OJ[:, j, :], iota_c[:, :], JPAIR[:, bass.ds(2 * i + j, 1)], None, ALU.is_equal).then_inc(oj_ready[j], 1)

            with chain.loop(NG // 4, 8) as i:
                pair_operands(i, 0)
                pair_operands(i, 1)

            dve.wait_ge(table_done, 1)
            chain.mark(V.tensor_copy(SW[:, :], bank[6][:, 0:COLS]))
            chain.link(V.tensor_copy(SPI[:, :], bank[7][:, 0:COLS]))
            chain.mark(V.tensor_scalar(SLI[:, :], SPI[:, :], P - 1, None, ALU.bitwise_and))
            V.tensor_scalar(SIX[:, :], SPI[:, :], 7, None, ALU.arith_shift_right).then_inc(slots_ready, 1)
            chain.settle()
            chain.link(V.tensor_copy(SLO[:, :], SLI[:, :]))

            def targets(r, cols=RC):
                _, base = nc.values_load_multi_w_load_instructions(
                    BID[0:1, bass.ds(r, 1), 0:cols].rearrange("p a c -> p (a c)"), engines=[mybir.EngineType.DVE],
                    min_val=0, max_val=(TILES - 1) * C,
                    skip_runtime_bounds_check_because="BID counts the buckets whose first column is at or before the "
                    "column, less one: the first bucket starts at column 0, so it lies in 0 .. TILES - 1, times C")
                return base

            def nth(r, h, k):
                return r * (RC // 2) + (h * (HAND // 2) + k // 2)

            def select(r, h, k):
                at = bass.ds(r * RC + (h * HAND + k), 1)
                V.tensor_scalar(SEL[:, k, :], iota[:, :], SLO[:, at], SW[:, at], ALU.is_equal, ALU.mult).then_inc(sel_ready[k % 2], 1)

            def add(base, r, h, k):
                s = k % 2
                dve.wait_ge(chunk_mm[s], nth(r, h, k) + 1)
                dve.wait_ge(x_added[1 - s], nth(r, h, k + s) )
                xt = X[:, bass.ds(base[h * HAND + k], C)]
                V.tensor_tensor(xt, bank[6 + s][:, 0:C], xt, ALU.add).then_inc(x_added[s], 1)

            def hand(base, r, h, ks=range(HAND), final=False):
                for k in ks:
                    add(base, r, h, k)
                    if not final:
                        select(r, h + 1, k)

            for k in range(HAND):
                select(0, 0, k)
            dve.wait_ge(x_biased, TILES)

            def a_feature(i, slots):
                for s in slots:
                    dve.wait_ge(ek_ready[s], i + 1)
                    dve.wait_ge(kvacc_done[s], i)
                    V.tensor_tensor(KS[:, s, :], KR[:, s, :], EXK[:, s, :], ALU.add).then_inc(ks_ready[s], 1)
                n = len(slots) * P
                dve.wait_ge(eq_ready, i + 1)
                V.tensor_tensor(QT[:, :, toks(2 * i, n)], QR[:, :, 0:n], EQ[:, :, 0:n], ALU.add).then_inc(qt_ready, 1)

            with dve.Fori(0, PAIRS) as i:
                base = targets(i)
                hand(base, i, 0)
                hand(base, i, 1)
                a_feature(i, (0, 1))
                hand(base, i, 2)
            a_feature(PAIRS, (0,))

            dve.wait_ge(kv_summed, 1)
            for c in range(CC):
                ins = V.tensor_tensor(KVM[:, c, :], bank[4][:, c * VE:(c + 1) * VE], hmask[:, :], ALU.mult)
                ins.then_inc(kvm_ready, 1)

            def links(steps, carried=False):
                for step in steps:
                    for ins in step:
                        chain.mark(ins())
                    if carried and step is steps[-1]:
                        settle_for_aggr()
                    else:
                        chain.settle()

            def aggregate(m, slots, var):
                for s in slots:
                    ins = V.bn_aggr(MV2[:, m, s, :], ST2[:, m, s, :])
                ins.then_inc(var, 1)

            def b_attend(i, slots):
                per_s = lambda f: [lambda s=s: f(s) for s in slots]
                for s in slots:
                    dve.wait_ge(t_done[s], i + 1)
                ps = lambda s: bank[1 + s][:, 0:CC * VE].rearrange("p (c n) -> p c n", n=VE)
                links([
                    per_s(lambda s: V.tensor_scalar(DEN[:, s, :].rearrange("p (c h) -> p c h", c=CC), ps(s)[:, :, P:VE], EPS_ATTN, None, ALU.add)),
                    per_s(lambda s: V.reciprocal(RZ[:, s, :], DEN[:, s, :])),
                    [lambda s=s, c=c: V.tensor_tensor(
                        TX[:, s, c * P:(c + 1) * P].rearrange("p (h d) -> p h d", d=HD),
                        ps(s)[:, c, 0:P].rearrange("p (h d) -> p h d", d=HD),
                        RZ[:, s, c * HH:(c + 1) * HH].rearrange("p (h o) -> p h o", o=1).to_broadcast([P, HH, HD]), ALU.mult)
                        for s in slots for c in range(CC)],
                    per_s(lambda s: V.tensor_tensor(TX[:, s, :], TX[:, s, :], XN[:, tile(2 * i + s)], ALU.add)),
                    per_s(lambda s: V.bn_stats(ST2[:, 0, s, :], TX[:, s, :])),
                ], carried=True)
                aggregate(0, slots, var1)

            def b_scale(src, gain, m, slots):
                per_s = lambda f: [lambda s=s: f(s) for s in slots]
                n = len(slots)
                links([
                    [lambda: V.reciprocal(RS2[:, m, 0:n], SD2[:, m, 0:n])] +
                    per_s(lambda s: V.scalar_tensor_tensor(out=TN[:, s, :], in0=src[:, s, :], scalar=MV2[:, m, s, 0:1],
                                                           in1=gain, op0=ALU.subtract, op1=ALU.mult)),
                ])

            def b_x1(i, slots):
                dve.wait_ge(sd1, i + 1)
                b_scale(TX, L1G, 0, slots)
                for s in slots:
                    V.scalar_tensor_tensor(out=X1[:, s, :], in0=TN[:, s, :], scalar=RS2[:, 0, s:s + 1], in1=L1B,
                                           op0=ALU.mult, op1=ALU.add).then_inc(x1_ready[s], 1)

            def b_out(i, slots):
                per_s = lambda f: [lambda s=s: f(s) for s in slots]
                for s in slots:
                    dve.wait_ge(y_done[s], i + 1)
                    dve.wait_ge(x1_ready[s], i + 1)
                links([
                    per_s(lambda s: V.tensor_tensor(TY[:, s, :], bank[3 + s][:, 0:C], X1[:, s, :], ALU.add)),
                    per_s(lambda s: V.tensor_tensor(TY[:, s, :], TY[:, s, :], B2R, ALU.add)),
                    per_s(lambda s: V.bn_stats(ST2[:, 1, s, :], TY[:, s, :])),
                ], carried=True)
                aggregate(1, slots, var2)

            def b_update(i, slots, r, h):
                dve.wait_ge(sd2, i + 1)
                b_scale(TY, L2G, 1, slots)
                for s in range(2):
                    dve.wait_ge(x_added[s], nth(r, h + 1, 0))
                for s in slots:
                    xt = X[:, tile(2 * i + s)]
                    chain.mark(V.scalar_tensor_tensor(out=xt, in0=TN[:, s, :], scalar=RS2[:, 1, s:s + 1], in1=xt,
                                                      op0=ALU.mult, op1=ALU.add))
                chain.settle()

            b_attend_n, b_x1_n, b_out_n, b_update_n = 10 + 2, 1 + 2, 6, 1 + 2 + 2
            base = targets(PAIRS)
            hand(base, PAIRS, 0)
            b_attend(0, (0, 1))
            hand(base, PAIRS, 1)
            b_x1(0, (0, 1))
            hand(base, PAIRS, 2)
            with chain.loop(PAIRS - 1, b_attend_n + b_x1_n + b_out_n + b_update_n, first=1) as i:
                r = i + PAIRS
                base = targets(r)
                hand(base, r, 0)
                b_attend(i, (0, 1))
                hand(base, r, 1, range(0, 3))
                b_out(i - 1, (0, 1))
                hand(base, r, 1, range(3, 6))
                b_x1(i, (0, 1))
                hand(base, r, 2)
                b_update(i - 1, (0, 1), r, 2)
            base = targets(ROUNDS, TAIL * HAND)
            hand(base, ROUNDS, 0)
            b_attend(PAIRS, (0,))
            b_out(PAIRS - 1, (0, 1))
            b_x1(PAIRS, (0,))
            hand(base, ROUNDS, 1, final=True)
            b_update(PAIRS - 1, (0, 1), ROUNDS, 1)
            b_out(PAIRS, (0,))
            b_update(PAIRS, (0,), ROUNDS, 1)

            statistics(f_stats)
            mean_and_variance().then_inc(f_aggr, 1)
            dve.wait_ge(f_sd, 1)
            chain.link(V.reciprocal(RS[:, :], SD[:, :]))
            V.scalar_tensor_tensor(out=NM[:, :], in0=MV[:, :, 0], scalar=-1.0, in1=RS[:, :],
                                   op0=ALU.mult, op1=ALU.mult).then_inc(f_rstd, 1)

            dve.wait_ge(mean_done, 1)
            V.tensor_scalar(MEAN[:, :], bank[3][:, 0:CC], 1.0 / N, None, ALU.mult).then_inc(mean_ready, 1)
            dve.wait_ge(logits_done, 1)
            chain.link(V.tensor_tensor(R[0:1, 0, :], bank[4][0:1, 0:NE], RB[:, :], ALU.add))

            def softmax(src, dst, width, n):
                chain.link(V.tensor_reduce(R[0:1, 1, 0:1], src, AX.X, ALU.max))
                V.tensor_scalar(R[0:1, 10, 0:width], src, R[0:1, 1, 0:1], None, ALU.subtract).then_inc(r_shift, 1)
                dve.wait_ge(r_exp, n)
                chain.link(V.tensor_reduce(R[0:1, 1, 1:2], R[0:1, 11, 0:width], AX.X, ALU.add))
                chain.link(V.reciprocal(R[0:1, 1, 2:3], R[0:1, 1, 1:2]))
                return V.tensor_scalar(dst, R[0:1, 11, 0:width], R[0:1, 1, 2:3], None, ALU.mult)

            chain.link(softmax(R[0:1, 0, :], R[0:1, 2, :], NE, 1))
            chain.link(V.tensor_scalar(R[0:1, 3, :], R[0:1, 2, :], float(N), 1.0, ALU.mult, ALU.max))
            chain.link(V.reciprocal(R[0:1, 4, :], R[0:1, 3, :]))
            chain.link(V.tensor_scalar(R[0:1, 5, :], R[0:1, 4, :], CAPACITY, 1.0, ALU.mult, ALU.min))
            chain.link(V.tensor_tensor(R[0:1, 6, :], R[0:1, 2, :], R[0:1, 5, :], ALU.mult))
            chain.link(softmax(R[0:1, 6, :], R[0:1, 7, :], NE, 2))
            chain.link(V.max(R[0:1, 8, :], R[0:1, 7, :]))
            V.max_index(RI[0:1, :], R[0:1, 8, :], R[0:1, 7, :]).then_inc(topi_ready, 1)
            softmax(R[0:1, 8, 0:TOPK], R[0:1, 9, 0:TOPK], TOPK, 3).then_inc(topw_ready, 1)
            dve.wait_ge(wb_done, 1)
            chain.link(V.tensor_copy(WB[:, :], bank[5][:, 0:TOPK]))
            dve.wait_ge(exp_in, 16 * 4 * TOPK)
            for e in range(TOPK):
                chain.mark(V.tensor_scalar(FW2[:, e * FJ:(e + 1) * FJ, :], FW2[:, e * FJ:(e + 1) * FJ, :], WB[:, e:e + 1], None, ALU.mult))
            chain.link(V.tensor_scalar(B2C[:, :], FB2[:, 0, :], WB[:, 0:1], None, ALU.mult))
            V.scalar_tensor_tensor(out=B2C[:, :], in0=FB2[:, 1, :], scalar=WB[:, 1:2], in1=B2C[:, :],
                                   op0=ALU.mult, op1=ALU.add).then_inc(w2_scaled, 1)
            dve.wait_ge(w2_scaled, 1)

            def ffn_out(b, tiles):
                for s in tiles:
                    u = s % 2
                    dve.wait_ge(down_done[u], b * 2 + (s // 2 + 1))
                    V.tensor_tensor(Y[:, s, :], bank[4 + u][:, 0:C], XN[:, tile(4 * b + s)], ALU.add).then_inc(y_read[u], 1)
                    dve.wait_ge(y_read[u], b * 2 + (s // 2 + 1))
                    chain.link(V.tensor_tensor(Y[:, s, :], Y[:, s, :], B2C[:, :], ALU.add))
                    chain.mark(V.bn_stats(ST3[:, s, :], Y[:, s, :]))
                    settle_for_aggr()
                    chain.mark(V.bn_aggr(MV3[:, s, :], ST3[:, s, :]))
                chain.settle()
                dve.wait_ge(rs3_ready, b)
                V.tensor_scalar(VE3[:, :], MV3[:, :, 1], EPS_LN, None, ALU.add).then_inc(v3_ready, 1)
                dve.wait_ge(rs3_ready, b + 1)
                for s in tiles:
                    chain.link(V.tensor_scalar(Y[:, s, :], Y[:, s, :], MV3[:, s, 0:1], RS3[:, s:s + 1], ALU.subtract, ALU.mult))
                    chain.link(V.tensor_tensor(Y[:, s, :], Y[:, s, :], FG, ALU.mult))
                    chain.link(V.tensor_tensor(Y[:, s, :], Y[:, s, :], FB, ALU.add))
                    dve.wait_ge(out_done[s], b * 16)
                    V.tensor_tensor(YO[:, s, :], Y[:, s, :], X[:, tile(4 * b + s)], ALU.add).then_inc(yo_ready[s], 1)

            with chain.loop(NBLK, 4 * 6) as b:
                ffn_out(b, range(4))
            ffn_out(NBLK, (0,))

        @block.tensor
        def _(pe):
            T = nc.tensor
            pe.wait_ge(gw_in, 16)
            pe.wait_ge(pool_const, 1)

            def transpose_tile(into, src):
                for c in range(CC):
                    ins = T.transpose(into[:, c * P:(c + 1) * P], src[:, c * P:(c + 1) * P], ident[:, :])
                return ins

            def transpose_xn(i, s):
                pe.wait_ge(xs_ready[s], i + 1)
                pe.wait_ge(xt_ready[s], i)
                transpose_tile(bank[3 * s], XS[:, s, :]).then_inc(tp_done[s], 1)

            def xg_tiles(i, slots, following):
                for s in slots:
                    pe.wait_ge(xt_ready[s], i + 1)
                    pe.wait_ge(xg_evac[s], i)
                    for c in range(CC):
                        ins = T.matmul(bank[1 + s][:, 0:C], XT[:, c, s, :], GW[:, c, :], start=(c == 0), stop=(c == CC - 1))
                    ins.then_inc(g_done[s], 1)
                    if s in following:
                        transpose_xn(i + 1, s)

            BEFORE = PAIRS // 3
            transpose_xn(0, 0)
            transpose_xn(0, 1)
            with pe.Fori(0, BEFORE) as i:
                xg_tiles(i, (0, 1), (0, 1))

            HB = TILES // 2
            pe.wait_ge(counted, TILES)
            last_k = SC[:, :, :].rearrange("p b (g k) -> p b g k", k=GC)[:, :, :, GC - 1]
            T.matmul(bank[4][:, 0:HB * NG], onesb[:, :], last_k[:, 0:HB, :], start=True, stop=True)
            T.matmul(bank[5][:, 0:(TILES - HB) * NG], onesb[:, :], last_k[:, HB:TILES, :], start=True, stop=True).then_inc(totals_done, 1)

            with pe.Fori(BEFORE, PAIRS - 1) as i:
                xg_tiles(i, (0, 1), (0, 1))
            xg_tiles(PAIRS - 1, (0, 1), (0,))
            xg_tiles(PAIRS, (0,), ())

            pe.wait_ge(bid_cmp, 1)
            T.matmul(bank[6][0:1, 0:COLS], ones[0:TILES, 0:1], CMP[0:TILES, :], start=True, stop=True).then_inc(bid_sum, 1)

            pe.wait_ge(tables_ready, 1)

            def rank(g, s):
                G = 2 * g + s
                pe.wait_ge(rank_read[s], g)
                at = bass.ds(G * GC, GC)
                ps = bank[4 + s][:, 0:TILES * GC]
                tab = lambda m: m[:, bass.ds(G, 1), :].rearrange("p g (b o) -> p (g b) o", o=1).to_broadcast([P, TILES, GC])
                T.matmul(ps, onesb[:, :], SC[:, :, at], start=True, stop=False)
                T.matmul(ps, from_here[:, :], OH[:, :, at], start=False, stop=False)
                T.matmul(ps, row0[:, :], tab(TAB0), start=False, stop=False)
                T.matmul(ps, row0[:, :], tab(TAB1), start=False, stop=True).then_inc(rank_done[s], 1)

            with pe.Fori(0, NG // 2) as g:
                rank(g, 0)
                rank(g, 1)

            pe.wait_ge(bid_ready, 1)
            T.matmul(bank[6][:, 0:COLS], zeros[:, :], iota_c[:, :], start=True, stop=False)
            T.matmul(bank[7][:, 0:COLS], zeros[:, :], iota_c[:, :], start=True, stop=False)

            def group(i, s):
                pe.wait_ge(as_ready[s], i + 1)
                pe.wait_ge(oi_ready[s], i + 1)
                pe.wait_ge(gs_ready[s // 2], i)
                for k in range(GC):
                    ins = T.matmul(bank[s][:, 0:P], AS[:, s, k, :], OI[:, s, k, :], start=(k == 0), stop=(k == GC - 1))
                ins.then_inc(grp_done[s], 1)

            def place(i, j):
                pe.wait_ge(gs_ready[j], i + 1)
                pe.wait_ge(oj_ready[j], i + 1)
                T.matmul(bank[6][:, 0:COLS], GSW[:, j, :], OJ[:, j, :], start=False, stop=False, skip_group_check=True)
                T.matmul(bank[7][:, 0:COLS], GSP[:, j, :], OJ[:, j, :], start=False, stop=False, skip_group_check=True).then_inc(placed[j], 1)

            def sort_step(i, before=True):
                group(i, 0)
                group(i, 1)
                if before:
                    place(i - 1, 1)
                group(i, 2)
                group(i, 3)
                place(i, 0)

            sort_step(0, before=False)
            with pe.Fori(1, NG // 4) as i:
                sort_step(i)
            place(NG // 4 - 1, 1)
            T.matmul(bank[6][:, 0:COLS], zeros[:, :], iota_c[:, :], start=False, stop=True)
            T.matmul(bank[7][:, 0:COLS], zeros[:, :], iota_c[:, :], start=False, stop=True).then_inc(table_done, 1)

            def hand(r, h, ks=range(HAND)):
                for k in ks:
                    s = k % 2
                    n = r * (RC // 2) + (h * (HAND // 2) + k // 2)
                    pe.wait_ge(sel_ready[s], n + 1)
                    pe.wait_ge(x_added[s], n)
                    if k == ks[0]:
                        pe.wait_ge(gathered[h], r * (16 * HAND) + 16 * HAND)
                    T.matmul(bank[6 + s][:, 0:C], SEL[:, k, :], RING[:, h * HAND + k, :], start=True, stop=True).then_inc(chunk_mm[s], 1)

            pe.wait_ge(w_in, WEIGHTS_IN)
            pe.wait_ge(slots_ready, 1)
            T.matmul(bank[4][:, 0:CC * VE], zeros[:, :], iota_c[:, 0:CC * VE], start=True, stop=False)

            def a_transpose(i, slots):
                for s in slots:
                    pe.wait_ge(a_xs[s], i + 1)
                    pe.wait_ge(a_xt[s], i)
                    transpose_tile(bank[s], XS[:, s, :]).then_inc(a_tp[s], 1)

            def a_project(i, slots):
                for s in slots:
                    pe.wait_ge(a_xt[s], i + 1)
                    pe.wait_ge(vx_ready[s], i)
                    for c in range(CC):
                        ins = T.matmul(bank[2 + s][:, :], XT[:, c, s, :], QKVW[:, c, C:3 * C], start=(c == 0), stop=(c == CC - 1))
                    ins.then_inc(kv_done[s], 1)
                pe.wait_ge(eq_ready, i)
                n = len(slots) * P
                for h in range(CC):
                    for c in range(CC):
                        ins = T.matmul(bank[5][:, h * 2 * P:h * 2 * P + n], QKVW[:, c, h * P:(h + 1) * P],
                                       XT[:, c, 0:len(slots), :], start=(c == 0), stop=(c == CC - 1))
                ins.then_inc(q_done, 1)

            def a_outer(i, slots, rows=P):
                for s in slots:
                    pe.wait_ge(ks_ready[s], i + 1)
                    pe.wait_ge(vx_ready[s], i + 1)
                    for c in range(CC):
                        ins = T.matmul(bank[4][:, c * VE:(c + 1) * VE], KS[0:rows, s, c * P:(c + 1) * P], VX[0:rows, s, c, :],
                                       start=False, stop=False, skip_group_check=True)
                    ins.then_inc(kvacc_done[s], 1)

            with pe.Fori(0, PAIRS) as i:
                a_transpose(i, (0, 1))
                hand(i, 0)
                a_project(i, (0, 1))
                hand(i, 1)
                hand(i, 2)
                a_outer(i, (0, 1))
            a_transpose(PAIRS, (0,))
            a_project(PAIRS, (0,))
            a_outer(PAIRS, (0,), LAST)
            T.matmul(bank[4][:, 0:CC * VE], zeros[:, :], iota_c[:, 0:CC * VE], start=False, stop=True).then_inc(kv_summed, 1)

            pe.wait_ge(kvm_ready, CC)

            def b_attend(i, slots):
                for s in slots:
                    pe.wait_ge(qs_ready[s], i + 1)
                    pe.wait_ge(x1_ready[s], i)
                    for c in range(CC):
                        ins = T.matmul(bank[1 + s][:, c * VE:(c + 1) * VE], QS[:, s, c, :], KVM[:, c, :], start=True, stop=True)
                    ins.then_inc(t_done[s], 1)

            def b_transpose(i, slots):
                pe.wait_ge(x1t, i)
                for s in slots:
                    pe.wait_ge(x1_ready[s], i + 1)
                    ins = transpose_tile(bank[0][:, s * C:(s + 1) * C], X1[:, s, :])
                ins.then_inc(x1tp, 1)

            def b_hidden(i, slots):
                n = len(slots) * P
                pe.wait_ge(x1t, i + 1)
                pe.wait_ge(hs_ready, i * CC)
                for h in range(CC):
                    for c in range(CC):
                        ins = T.matmul(bank[5][:, h * 2 * P:h * 2 * P + n], W1[:, c, h * P:(h + 1) * P],
                                       XT[:, c, 0:len(slots), :], start=(c == 0), stop=(c == CC - 1))
                ins.then_inc(h_done, 1)

            def b_project(i, slots):
                pe.wait_ge(hs_ready, i * CC + CC)
                pe.wait_ge(var2, i)
                for s in slots:
                    for h in range(CC):
                        ins = T.matmul(bank[3 + s][:, 0:C], HS[:, h, s, :], W2[:, h, :], start=(h == 0), stop=(h == CC - 1))
                    ins.then_inc(y_done[s], 1)

            b_attend(0, (0, 1))
            hand(PAIRS, 0)
            hand(PAIRS, 1)
            hand(PAIRS, 2, range(0, 2))
            b_transpose(0, (0, 1))
            hand(PAIRS, 2, range(2, 6))
            b_hidden(0, (0, 1))
            with pe.Fori(1, PAIRS) as i:
                r = i + PAIRS
                b_attend(i, (0, 1))
                hand(r, 0)
                b_project(i - 1, (0, 1))
                hand(r, 1)
                hand(r, 2, range(0, 2))
                b_transpose(i, (0, 1))
                hand(r, 2, range(2, 6))
                b_hidden(i, (0, 1))
            b_attend(PAIRS, (0,))
            hand(ROUNDS, 0)
            b_project(PAIRS - 1, (0, 1))
            hand(ROUNDS, 1, range(0, 2))
            b_transpose(PAIRS, (0,))
            hand(ROUNDS, 1, range(2, 6))
            b_hidden(PAIRS, (0,))
            b_project(PAIRS, (0,))

            pe.wait_ge(f_rstd, 1)
            T.matmul(bank[3][:, 0:CC], zeros[:, :], iota_c[:, 0:CC], start=True, stop=False)

            def ffn_in(i, slots, rows=P):
                for s in slots:
                    pe.wait_ge(f_xs[s], i + 1)
                    pe.wait_ge(f_xt[s], i)
                    for c in range(CC):
                        T.matmul(bank[3][:, c:c + 1], XS[0:rows, s, c * P:(c + 1) * P], ones[0:rows, 0:1],
                                 start=False, stop=False, skip_group_check=True)
                    transpose_tile(bank[s], XS[:, s, :]).then_inc(f_tp[s], 1)

            with pe.Fori(0, PAIRS) as i:
                ffn_in(i, (0, 1))
            ffn_in(PAIRS, (0,), LAST)
            T.matmul(bank[3][:, 0:CC], zeros[:, :], iota_c[:, 0:CC], start=False, stop=True).then_inc(mean_done, 1)
            pe.wait_ge(mean_ready, 1)
            for c in range(CC):
                ins = T.matmul(bank[4][0:1, 0:NE], MEAN[:, c:c + 1], RW[:, c, :], start=(c == 0), stop=(c == CC - 1))
            ins.then_inc(logits_done, 1)
            pe.wait_ge(topw_ready, 1)
            T.matmul(bank[5][:, 0:TOPK], ones[0:1, :], R[0:1, 9, 0:TOPK], start=True, stop=True).then_inc(wb_done, 1)
            pe.wait_ge(exp_in, 16 * 4 * TOPK)
            for s in range(2):
                pe.wait_ge(f_xt[s], PAIRS + (s == 0))

            def up(b, width):
                for n in range(TOPK * FJ):
                    s = n % 2
                    e, j = divmod(n, FJ)
                    pe.wait_ge(gelu_done[s], b * (TOPK * FJ // 2) + n // 2)
                    for c in range(CC):
                        ins = T.matmul(bank[1 + s][:, 0:width], FW1[:, e, c, j * P:(j + 1) * P],
                                       QT[:, c, bass.ds(b * BLK, width)], start=(c == 0), stop=(c == CC - 1))
                    ins.then_inc(up_done[s], 1)

            def down(b, tiles):
                for s in range(2):
                    pe.wait_ge(gelu_done[s], b * (TOPK * FJ // 2) + TOPK * FJ // 2)
                for t in tiles:
                    u = t % 2
                    pe.wait_ge(y_read[u], b * 2 + t // 2)
                    for n in range(TOPK * FJ):
                        ins = T.matmul(bank[4 + u][:, 0:C], HF[:, n, t * P:(t + 1) * P], FW2[:, n, :],
                                       start=(n == 0), stop=(n == TOPK * FJ - 1))
                    ins.then_inc(down_done[u], 1)

            pe.wait_ge(w2_scaled, 1)
            with pe.Fori(0, NBLK) as b:
                up(b, BLK)
                down(b, range(4))
            up(NBLK, P)
            down(NBLK, (0,))


def kernel(**inputs):
    import numpy as _np
    import concourse.bacc as _bacc
    from concourse import mybir as _mybir
    from concourse.bass_utils import run_bass_kernel_spmd as _run

    get = lambda n: _np.asarray(inputs[n])
    x = get("x")
    n, c = x.shape
    tiles = -(-n // 128)
    n_edges = get("src").shape[0]
    chunks = -(-n_edges // (128 * 13)) * 13

    def edges(a):
        flat = _np.zeros(128 * chunks, a.dtype)
        flat[:n_edges] = a
        return flat.reshape(128, chunks)

    xp = _np.zeros((tiles * 128, c), x.dtype)
    xp[:n] = x
    b1 = get("L0_ffn_b1")
    ne, ff = b1.shape
    rowv = lambda name: get(name).reshape(1, -1)
    laid = {
        "x": xp, "row": edges(get("src")), "col": edges(get("dst")), "weight": edges(get("edge_weight")),
        "gnn_wT": get("L0_gnn_W").T, "gnn_b": rowv("L0_gnn_b"), "qkv_wT": get("L0_mix_Wqkv").T,
        "ln1_g": rowv("L0_mix_ln1_g"), "ln1_b": rowv("L0_mix_ln1_b"), "mix_w1T": get("L0_mix_W1").T,
        "mix_b1": get("L0_mix_b1").reshape(-1, 128).T, "mix_w2T": get("L0_mix_W2").T, "mix_b2": rowv("L0_mix_b2"),
        "ln2_g": rowv("L0_mix_ln2_g"), "ln2_b": rowv("L0_mix_ln2_b"),
        "router_w": get("L0_ffn_Wr"), "router_b": rowv("L0_ffn_br"), "exp_w1": get("L0_ffn_W1"),
        "exp_b1": b1.reshape(ne, ff // 128, 128).transpose(0, 2, 1), "exp_w2": get("L0_ffn_W2"), "exp_b2": get("L0_ffn_b2"),
        "ffn_g": rowv("L0_ffn_gamma"), "ffn_b": rowv("L0_ffn_beta"),
    }
    nc = _bacc.Bacc("TRN2", target_bir_lowering=False, num_devices=1)
    arrays, args = {}, []
    for name, a in laid.items():
        a = _np.ascontiguousarray(a)
        arrays[f"in_{name}"] = a
        args.append(nc.dram_tensor(f"in_{name}", a.shape, _mybir.dt.from_np(a.dtype), kind="ExternalInput").ap())
    f32 = _mybir.dt.float32
    args.append(nc.dram_tensor("out_0", (n, c), f32, kind="ExternalOutput").ap())
    args.append(nc.dram_tensor("xg_rows", (tiles * 128, c), f32, kind="Internal").ap())
    gps_layer_program(nc, *args)
    r = _run(nc, [arrays], core_ids=[0])
    return r.results[0]["out_0"]
```

```python
import concourse.bass as bass
from concourse import mybir
from contextlib import ExitStack, contextmanager


def gps_layer_program(nc, x, row, col, weight, gnn_wT, gnn_b, qkv_wT, ln1_g, ln1_b, mix_w1T, mix_b1,
                      mix_w2T, mix_b2, ln2_g, ln2_b, router_w, router_b, exp_w1, exp_b1, exp_w2, exp_b2,
                      ffn_g, ffn_b, out, xg_dram):
    f32, bf16, i32, u32 = mybir.dt.float32, mybir.dt.bfloat16, mybir.dt.int32, mybir.dt.uint32
    f32r = mybir.dt.float32r
    ALU, ACT, AX = mybir.AluOpType, mybir.ActivationFunctionType, mybir.AxisListType

    P = 128
    N, C = out.shape
    TILES = x.shape[0] // P
    PAIRS = TILES // 2
    LAST = N - (TILES - 1) * P
    H, HD = 8, C // 8
    HH = H // 2
    CC = C // P
    EPS_ATTN, EPS_LN = 1e-6, 1e-5
    NE, FF = exp_w1.shape[0], exp_w1.shape[2]
    FJ = FF // P
    TOPK = 2
    CAPACITY = float(-(-N * 5 // (4 * NE)))

    EK = row.shape[1]
    GC = 13
    NG = EK // GC
    LC = 64
    assert NG * GC == EK and NG % 4 == 0 and TILES + GC + (TILES * (P - 1)) // P <= LC
    HAND = 6
    HANDS = 3
    RC = HANDS * HAND
    ROUNDS = 2 * PAIRS
    COLS = -(-(EK + TILES - 1) // HAND) * HAND
    TAIL = COLS // HAND - ROUNDS * HANDS
    assert TAIL == 2 and COLS <= 512
    VE = P + HH
    NH = TOPK * FJ
    BLK = 2 * P
    UPS = 4
    NBLK = N // BLK
    EARLY = PAIRS // 2
    assert NBLK == PAIRS and NBLK % 2 == 0 and NH == 8

    ctx = ExitStack()
    with ctx:
        def sb(name, shape, dt=f32):
            return scope.enter_context(nc.sbuf_tensor(name, shape, dt))

        def sem(name):
            return ctx.enter_context(nc.semaphore(name))

        scope = ctx
        X = sb("X", [P, TILES * C])
        XN = sb("XN", [P, TILES * C])
        XS = sb("XS", [P, 2, C])
        ST = sb("ST", [P, TILES * 6])
        MV = sb("MV", [P, TILES, 2])
        SD = sb("SD", [P, TILES])
        RS = sb("RS", [P, TILES])
        NM = sb("NM", [P, TILES])
        ROWC = sb("ROWC", [P, 5, C])
        B2R, L2G, L2B, FG, FB = (ROWC[:, n, :] for n in range(5))
        carrier = sb("carrier", [P, 1])
        eps_ln = sb("eps_ln", [P, 1])
        ident = sb("ident", [P, P])
        iota = sb("iota", [P, P])
        iota_c = sb("iota_c", [P, COLS])
        ones = sb("ones", [P, P])
        onesb = sb("onesb", [P, P], bf16)
        from_here = sb("from_here", [P, P], bf16)
        row0 = sb("row0", [P, P], bf16)
        zeros = sb("zeros", [P, P])

        RW = sb("RW", [P, CC, NE])
        RB = sb("RB", [1, NE])
        mhalf = sb("mhalf", [P, 1])

        scope = ctx.enter_context(ExitStack())
        until_ffn = scope
        XT = sb("XT", [P, CC, 2, P])
        XGS = sb("XGS", [P, 2, 2, C])
        QKVW = sb("QKVW", [P, CC, 3 * C])
        GW = sb("GW", [P, CC, C])
        W1 = sb("W1", [P, CC, C])
        W2 = sb("W2", [P, CC, C])
        L1G = sb("L1G", [P, CC])
        L1B = sb("L1B", [P, CC])
        GNB = sb("GNB", [P, C])
        B1C = sb("B1C", [P, CC])
        iota_i = sb("iota_i", [P, COLS], i32)
        local_p = sb("local_p", [P, 1])
        local_i = sb("local_i", [P, 1], i32)
        hmask = sb("hmask", [P, VE])
        SW = sb("SW", [P, COLS])
        SPI = sb("SPI", [P, COLS], i32)
        SLI = sb("SLI", [P, COLS], i32)
        SLO = sb("SLO", [P, COLS])
        SIX = sb("SIX", [P, COLS], i32)
        BID = sb("BID", [1, ROUNDS + 1, -(-RC // 4) * 4], i32)
        VX = sb("VX", [P, 2, CC, VE])

        scope = ctx.enter_context(ExitStack())
        EROW = sb("EROW", [P, EK], i32)
        ECOL = sb("ECOL", [P, EK], i32)
        EW = sb("EW", [P, EK])
        EBI = sb("EBI", [P, EK], i32)
        EBF = sb("EBF", [P, EK], bf16)
        ELO = sb("ELO", [P, EK], i32)
        EPCI = sb("EPCI", [P, EK], i32)
        EPC = sb("EPC", [P, EK])
        SLOT = sb("SLOT", [P, EK])
        SLOTI = EBI
        TMPI = sb("TMPI", [P, EK], i32)
        LANE = sb("LANE", [P, EK])
        LCOL = sb("LCOL", [P, EK])
        JMAP = sb("JMAP", [P, NG])
        JPAIR = sb("JPAIR", [P, NG // 2])
        sort_scope = scope
        scope = ctx.enter_context(ExitStack())
        RESTART = sb("RESTART", [P, EK], bf16)
        OH = sb("OH", [P, TILES, EK], bf16)
        SC = sb("SC", [P, TILES, EK], bf16)
        NT = TILES * NG
        CNT = sb("CNT", [P, TILES, NG])
        Q1 = sb("Q1", [P, TILES, NG])
        Q0 = sb("Q0", [P, TILES, NG])
        RSB = sb("RSB", [P, TILES, NG])
        Q1I = sb("Q1I", [P, TILES, NG], i32)
        Q0I = sb("Q0I", [P, TILES, NG], i32)
        QLI = sb("QLI", [P, TILES, NG], i32)
        F0, F1 = Q0, Q1
        TCH = sb("TCH", [P, NG, TILES])
        LINC = sb("LINC", [P, NG, TILES])
        LOFF = sb("LOFF", [P, NG, TILES])
        RSG = sb("RSG", [P, NG, TILES])
        TAB0 = sb("TAB0", [P, NG, TILES], bf16)
        TAB1 = sb("TAB1", [P, NG, TILES], bf16)
        DC = sb("DC", [P, NG, TILES])
        DD = LINC
        NBI = sb("NBI", [P, TILES], i32)
        NBF = sb("NBF", [P, TILES])
        CBI = sb("CBI", [P, TILES])
        CB = sb("CB", [P, TILES])
        CBD = sb("CBD", [P, TILES])
        CBP = sb("CBP", [P, 1])
        CMP = sb("CMP", [P, COLS])
        PRD = sb("PRD", [P, 2, TILES, GC])
        scope.close()
        scope = sort_scope
        LH = sb("LH", [P, 4, GC, LC])
        AS = sb("AS", [P, 4, GC, P])
        OI = sb("OI", [P, 4, GC, P])
        LD = sb("LD", [P, GC, P])
        GSW = sb("GSW", [P, 2, P])
        GSP = sb("GSP", [P, 2, P])
        OJ = sb("OJ", [P, 2, COLS])
        scope.close()
        scope = until_ffn
        QT = sb("QT", [P, CC, TILES * P])
        IDXS = sb("IDXS", [P, HANDS, HAND], i32)
        RING = sb("RING", [P, RC, C])
        SEL = sb("SEL", [P, HAND, P])

        NK = sb("NK", [P, 2, C])
        EXK = sb("EXK", [P, 2, C])
        KS = sb("KS", [P, 2, C])
        NQ = sb("NQ", [P, CC, 2 * P])
        QR = sb("QR", [P, CC, 2 * P])
        KR = sb("KR", [P, 2, C])
        EQ = sb("EQ", [P, CC, 2 * P])
        KVM = sb("KVM", [P, CC, VE])
        QS = sb("QS", [P, 2, CC, P])
        DEN = sb("DEN", [P, 2, H])
        RZ = sb("RZ", [P, 2, H])
        TX = sb("TX", [P, 2, C])
        TN = sb("TN", [P, 2, C])
        NM2 = sb("NM2", [P, 2])
        ST2 = sb("ST2", [P, 2, 2, 6])
        MV2 = sb("MV2", [P, 2, 2, 2])
        SD2 = sb("SD2", [P, 2, 2])
        RS2 = sb("RS2", [P, 2, 2])
        HS = sb("HS", [P, CC, 2, P])
        scope.close()
        scope = ctx
        QH = sb("QH", [P, CC, TILES * P], f32r)
        QL = sb("QL", [P, CC, TILES * P], f32r)
        MEANR = sb("MEANR", [1, C])
        MEAN = sb("MEAN", [P, CC])
        R = sb("R", [1, 12, NE])
        RI = sb("RI", [1, NE], u32)
        WB = sb("WB", [P, TOPK])
        W1H = sb("W1H", [P, TOPK, CC, FF], f32r)
        W1L = sb("W1L", [P, TOPK, CC, FF], f32r)
        W2H = sb("W2H", [P, NH, C], f32r)
        W2L = sb("W2L", [P, NH, C], f32r)
        FB1 = sb("FB1", [P, TOPK, FJ])
        FB2 = sb("FB2", [P, TOPK, C])
        B2C = sb("B2C", [P, C])
        HF = sb("HF", [P, UPS, BLK])
        Y = sb("Y", [P, 2, C])
        YN = sb("YN", [P, 2, C])
        YO = sb("YO", [P, 2, C])
        ST3 = sb("ST3", [P, 2, 6])
        MV3 = sb("MV3", [P, 2, 2])
        VE3 = sb("VE3", [P, 2])
        RS3 = sb("RS3", [P, 2])
        scope = ctx.enter_context(ExitStack())
        QF = sb("QF", [P, CC, TILES * P])
        FW1 = sb("FW1", [P, TOPK, CC, FF])
        FW2 = sb("FW2", [P, NH, C])
        scope.close()
        scope = ctx
        HFH = sb("HFH", [P, 2, NH, BLK], f32r)
        HFL = sb("HFL", [P, 2, NH, BLK], f32r)

        bank = [ctx.enter_context(nc.psum_tensor(f"bank{n}", [P, 512], f32)) for n in range(8)]

        x_in = sem("x_in")
        w_in = sem("w_in")
        gw_in = sem("gw_in")
        e_in = sem("e_in")
        iota_ready = sem("iota_ready")
        pool_const = sem("pool_const")
        dve_const = sem("dve_const")
        stats_done = sem("stats_done")
        aggr_done = sem("aggr_done")
        std_ready = sem("std_ready")
        rstd_ready = sem("rstd_ready")
        xs_ready = [sem(f"xs_ready{s}") for s in range(2)]
        xn_kept = [sem(f"xn_kept{s}") for s in range(2)]
        tp_done = [sem(f"tp_done{s}") for s in range(2)]
        xt_ready = [sem(f"xt_ready{s}") for s in range(2)]
        g_done = [sem(f"g_done{s}") for s in range(2)]
        xg_evac = [sem(f"xg_evac{s}") for s in range(2)]
        xg_out = [sem(f"xg_out{s}") for s in range(2)]
        dve_step = sem("dve_step")
        act_step = sem("act_step")
        pool_step = sem("pool_step")
        counted = sem("counted")
        totals_done = sem("totals_done")
        tables_ready = sem("tables_ready")
        rank_done = [sem(f"rank_done{s}") for s in range(2)]
        rank_read = [sem(f"rank_read{s}") for s in range(2)]
        bid_cmp = sem("bid_cmp")
        bid_sum = sem("bid_sum")
        bid_ready = sem("bid_ready")
        lh_ready = sem("lh_ready")
        as_ready = sem("as_ready")
        ap_ready = sem("ap_ready")
        oi_ready = [sem(f"oi_ready{s}") for s in range(4)]
        grp_done = sem("grp_done")
        gs_ready = [sem(f"gs_ready{j}") for j in range(2)]
        oj_ready = [sem(f"oj_ready{j}") for j in range(2)]
        placed = [sem(f"placed{j}") for j in range(2)]
        lanes_ready = sem("lanes_ready")
        table_done = sem("table_done")
        slots_ready = sem("slots_ready")
        idx_first = sem("idx_first")
        x_biased = sem("x_biased")
        idx_staged = [sem(f"idx_staged{h}") for h in range(HANDS)]
        gathered = [sem(f"gathered{h}") for h in range(HANDS)]
        sel_ready = [sem(f"sel_ready{s}") for s in range(2)]
        chunk_mm = [sem(f"chunk_mm{s}") for s in range(2)]
        x_added = [sem(f"x_added{s}") for s in range(2)]
        a_xs = [sem(f"a_xs{s}") for s in range(2)]
        a_tp = [sem(f"a_tp{s}") for s in range(2)]
        a_xt = [sem(f"a_xt{s}") for s in range(2)]
        kv_done = [sem(f"kv_done{s}") for s in range(2)]
        nk_ready = [sem(f"nk_ready{s}") for s in range(2)]
        ek_ready = [sem(f"ek_ready{s}") for s in range(2)]
        vx_ready = [sem(f"vx_ready{s}") for s in range(2)]
        ks_ready = [sem(f"ks_ready{s}") for s in range(2)]
        kvacc_done = [sem(f"kvacc_done{s}") for s in range(2)]
        q_done = sem("q_done")
        nq_ready = sem("nq_ready")
        eq_ready = sem("eq_ready")
        qt_ready = sem("qt_ready")
        kv_summed = sem("kv_summed")
        kvm_ready = sem("kvm_ready")
        qs_ready = [sem(f"qs_ready{s}") for s in range(2)]
        t_done = [sem(f"t_done{s}") for s in range(2)]
        var1 = sem("var1")
        sd1 = sem("sd1")
        nm1 = sem("nm1")
        x1_ready = [sem(f"x1_ready{s}") for s in range(2)]
        x1tp = sem("x1tp")
        x1t = sem("x1t")
        h_done = sem("h_done")
        hs_ready = sem("hs_ready")
        y_done = [sem(f"y_done{s}") for s in range(2)]
        y_used = [sem(f"y_used{s}") for s in range(2)]
        var2 = sem("var2")
        sd2 = sem("sd2")
        b_done = sem("b_done")
        f_stats = sem("f_stats")
        f_aggr = sem("f_aggr")
        f_sd = sem("f_sd")
        f_rstd = sem("f_rstd")
        f_xs = [sem(f"f_xs{s}") for s in range(2)]
        f_xn = sem("f_xn")
        f_tp = [sem(f"f_tp{s}") for s in range(2)]
        f_xt = [sem(f"f_xt{s}") for s in range(2)]
        mean_done = sem("mean_done")
        mean_ready = sem("mean_ready")
        mean_turned = sem("mean_turned")
        mean_col = sem("mean_col")
        logits_done = sem("logits_done")
        r_shift = sem("r_shift")
        r_exp = sem("r_exp")
        topi_ready = sem("topi_ready")
        topw_ready = sem("topw_ready")
        wb_done = sem("wb_done")
        up_in = sem("up_in")
        down_in = sem("down_in")
        w2_scaled = sem("w2_scaled")
        up_done = sem("up_done")
        gelu_done = sem("gelu_done")
        hl_ready = sem("hl_ready")
        down_done = [sem(f"down_done{s}") for s in range(2)]
        y_read = [sem(f"y_read{s}") for s in range(2)]
        q_split = sem("q_split")
        w1_split = sem("w1_split")
        b2_ready = sem("b2_ready")
        res_ready = sem("res_ready")
        v3_ready = sem("v3_ready")
        rs3_ready = sem("rs3_ready")
        yo_ready = [sem(f"yo_ready{s}") for s in range(2)]
        out_done = [sem(f"out_done{s}") for s in range(2)]

        WEIGHTS_IN = 16 * 14

        block = ctx.enter_context(nc.Block())

        def tile(t):
            return bass.ds(t * C, C)

        def toks(t, n=P):
            return bass.ds(t * P, n)

        def first_of(i):
            return isinstance(i, int) and i == 0

        def per_chunk(m, i, s, n):
            return m[:, bass.ds((4 * i + s) * GC, GC)].rearrange("p (k o) -> p k o", o=1).to_broadcast([P, GC, n])

        def per_row(n):
            return iota[:, 0:n].rearrange("p (o m) -> p o m", o=1).to_broadcast([P, GC, n])

        class Chain:

            def __init__(self, eng, s):
                self.eng, self.s, self.n, self.local = eng, s, 0, 0

            def mark(self, ins):
                ins.then_inc(self.s, 1)
                self.n = self.n + 1
                self.local += 1

            def settle(self):
                self.eng.wait_ge(self.s, self.n)

            def link(self, ins):
                self.mark(ins)
                self.settle()

            @contextmanager
            def loop(self, trips, per, first=0):
                base = self.n
                with self.eng.Fori(first, first + trips) as i:
                    self.n, self.local = i * per + (base - first * per), 0
                    yield i
                    assert self.local == per, (self.local, per)
                self.n = base + trips * per

        @block.sync
        def _(sp):
            sp.dma_start(EROW[:, :], row).then_inc(e_in, 16)
            sp.dma_start(ECOL[:, :], col).then_inc(e_in, 16)
            sp.dma_start(EW[:, :], weight).then_inc(e_in, 16)
            sp.dma_start(X[:, :].rearrange("p (t c) -> p t c", c=C),
                         x.rearrange("(t p) c -> p t c", p=P)).then_inc(x_in, 16)
            sp.dma_start(GW[:, :, :], gnn_wT.rearrange("(c p) o -> p c o", p=P)).then_inc(gw_in, 16)
            sp.dma_start(QKVW[:, :, :], qkv_wT.rearrange("(c p) o -> p c o", p=P)).then_inc(w_in, 16)
            sp.dma_start(W1[:, :, :], mix_w1T.rearrange("(c p) o -> p c o", p=P)).then_inc(w_in, 16)
            sp.dma_start(W2[:, :, :], mix_w2T.rearrange("(c p) o -> p c o", p=P)).then_inc(w_in, 16)
            sp.dma_start(L1G[:, :], ln1_g).then_inc(w_in, 16)
            sp.dma_start(L1B[:, :], ln1_b).then_inc(w_in, 16)
            for dst, src in ((B2R, mix_b2), (L2G, ln2_g), (L2B, ln2_b),
                             (FG, ffn_g), (FB, ffn_b), (GNB[:, :], gnn_b)):
                sp.dma_start(dst, src.to_broadcast([P, C])).then_inc(w_in, 16)
            sp.dma_start(B1C[:, :], mix_b1).then_inc(w_in, 16)
            sp.dma_start(RW[:, :, :], router_w.rearrange("(c p) o -> p c o", p=P)).then_inc(w_in, 16)
            sp.dma_start(RB[:, :], router_b).then_inc(w_in, 16)

            def store_xg(h, q, n=2):
                for s in range(n):
                    sp.wait_ge(xg_evac[s], 2 * h + (q + 1))
                sp.dma_start(xg_dram[bass.ds((4 * h + 2 * q) * P, n * P), :].rearrange("(t p) c -> p t c", p=P),
                             XGS[:, q, 0:n, :]).then_inc(xg_out[q], 16)

            with sp.Fori(0, PAIRS // 2) as h:
                store_xg(h, 0)
                store_xg(h, 1)
            store_xg(PAIRS // 2, 0, n=1)

            sp.wait_ge(topi_ready, 1)
            chosen = []
            for e in range(TOPK):
                v = sp.value_load(RI[0:1, e:e + 1], min_val=0, max_val=NE - 1)
                sp.dma_start(FW1[:, e, :, :], exp_w1[bass.ds(v, 1), :, :].rearrange("e (c p) f -> p (e c) f", p=P)).then_inc(up_in, 16)
                sp.dma_start(FB1[:, e, :], exp_b1[bass.ds(v, 1), :, :].rearrange("e p j -> p (e j)")).then_inc(up_in, 16)
                chosen.append(v)
            for e, v in enumerate(chosen):
                sp.dma_start(FW2[:, e * FJ:(e + 1) * FJ, :], exp_w2[bass.ds(v, 1), :, :].rearrange("e (j p) d -> p (e j) d", p=P)).then_inc(down_in, 16)
                sp.dma_start(FB2[:, e, :], exp_b2[bass.ds(v, 1), :].to_broadcast([P, C])).then_inc(down_in, 16)

            def store_out(b, s, rows=P):
                sp.wait_ge(yo_ready[s], b + 1)
                sp.dma_start(out[bass.ds((2 * b + s) * P, rows), :], YO[0:rows, s, :]).then_inc(out_done[s], 16)

            with sp.Fori(0, NBLK) as b:
                store_out(b, 0)
                store_out(b, 1)
            store_out(NBLK, 0, LAST)
            for s in range(2):
                sp.wait_ge(out_done[s], 16 * (NBLK + (s == 0)))

        @block.gpsimd
        def _(pool):
            chain = Chain(pool, pool_step)
            chain.mark(pool.iota(iota_i[:, :], pattern=[[1, COLS]], base=0, channel_multiplier=0))
            chain.mark(pool.iota(local_i[:, :], pattern=[[0, 1]], base=0, channel_multiplier=1))
            chain.settle()
            pool.tensor_copy(iota[:, :], iota_i[:, 0:P]).then_inc(iota_ready, 1)
            for m in (ident, ones, zeros, onesb, from_here, row0, hmask):
                chain.mark(pool.memset(m[:, :], {"ident": 0.0, "zeros": 0.0, "from_here": -1.0}.get(m.name, 1.0)))
            chain.mark(pool.memset(RESTART[:, :], 1.0))
            chain.mark(pool.memset(RSB[:, :, :], 1.0))
            chain.mark(pool.memset(RSG[:, :, :], 1.0))
            chain.mark(pool.memset(eps_ln[:, :], EPS_LN))
            chain.mark(pool.memset(mhalf[:, :], -0.5))
            chain.mark(pool.memset(VX[:, :, :, :], 1.0))
            chain.settle()
            chain.mark(pool.affine_select(out=ident[:, :], in_=ident[:, :], compare_op=ALU.not_equal, fill=1.0,
                                          base=0, pattern=[[-1, P]], channel_multiplier=1))
            chain.mark(pool.affine_select(out=from_here[:, :], in_=from_here[:, :], compare_op=ALU.is_ge, fill=0.0,
                                          base=0, pattern=[[-1, P]], channel_multiplier=1))
            chain.mark(pool.affine_select(out=row0[:, :], in_=row0[:, :], compare_op=ALU.is_ge, fill=0.0,
                                          base=0, pattern=[[0, P]], channel_multiplier=-1))
            for base, cm, hs in ((0, 1, -HD), (HD - 1, -1, HD)):
                chain.link(pool.affine_select(out=hmask[:, 0:P].rearrange("p (h d) -> p h d", d=HD),
                                              in_=hmask[:, 0:P].rearrange("p (h d) -> p h d", d=HD),
                                              compare_op=ALU.is_ge, fill=0.0, base=base,
                                              pattern=[[hs, HH], [0, HD]], channel_multiplier=cm))
                chain.link(pool.affine_select(out=hmask[:, P:VE], in_=hmask[:, P:VE],
                                              compare_op=ALU.is_ge, fill=0.0, base=base,
                                              pattern=[[hs, HH]], channel_multiplier=cm))
            chain.mark(pool.memset(RESTART[:, :].rearrange("p (g k) -> p g k", k=GC)[:, :, 0:1], 0.0))
            chain.mark(pool.memset(RSB[:, :, 0:1], 0.0))
            chain.mark(pool.memset(RSG[:, :, 0:1], 0.0))
            chain.settle()
            pool.tensor_copy(iota_c[:, :], iota_i[:, :]).then_inc(pool_const, 1)

            def keep_xn(i, slots):
                for s in slots:
                    pool.wait_ge(xs_ready[s], i + 1)
                    pool.tensor_copy(XN[:, tile(2 * i + s)], XS[:, s, :]).then_inc(xn_kept[s], 1)

            with pool.Fori(0, PAIRS) as i:
                keep_xn(i, (0, 1))
            keep_xn(PAIRS, (0,))

            for t in range(2):
                pool.wait_ge(xs_ready[t], PAIRS + (t == 0))
            pool.wait_ge(w_in, WEIGHTS_IN)
            chain.link(pool.tensor_tensor(L2B, L2B, GNB[:, :], ALU.add))
            with pool.Fori(0, TILES) as t:
                pool.tensor_tensor(X[:, tile(t)], X[:, tile(t)], L2B, ALU.add).then_inc(x_biased, 1)

            def columns_and_rows(i):
                for s in range(4):
                    pool.wait_ge(lh_ready, 4 * i + (s + 1))
                    if not first_of(i):
                        pool.wait_ge(grp_done, 4 * i + (s - 3))
                    pool.tensor_tensor(AS[:, s, :, LC:2 * LC], LH[:, s, :, :], per_chunk(EPC, i, s, LC), ALU.mult).then_inc(ap_ready, 1)

            columns_and_rows(0)
            with pool.Fori(1, NG // 4) as i:
                columns_and_rows(i)

            GATHERED = 16 * HAND

            def stage(r, h):
                first = isinstance(r, int) and r == 0
                if not first:
                    pool.wait_ge(chunk_mm[1], r * (RC // 2) - (RC // 2 - (h + 1) * (HAND // 2)))
                    pool.wait_ge(gathered[h], r * GATHERED)
                pool.tensor_copy(IDXS[:, h, :], SIX[:, bass.ds(r * RC + h * HAND, HAND)]
                                 ).then_inc(idx_first if first else idx_staged[h], 1 if first else GATHERED)

            def gather(r, h):
                first = isinstance(r, int) and r == 0
                if first:
                    pool.wait_ge(idx_first, h + 1)
                else:
                    pool.wait_ge(slots_ready, 1)
                    pool.wait_ge(idx_staged[h], r * GATHERED)
                for k in range(HAND):
                    pool.indirect_dma_start(RING[:, h * HAND + k, :], None, xg_dram,
                                            bass.IndirectOffsetOnAxis(ap=IDXS[:, h, k:k + 1], axis=0)
                                            ).then_inc(gathered[h], 16)

            pool.wait_ge(slots_ready, 1)
            pool.wait_ge(xg_out[0], 16 * (PAIRS // 2 + 1))
            pool.wait_ge(xg_out[1], 16 * (PAIRS // 2))
            for h in range(HANDS):
                stage(0, h)
            for h in range(HANDS):
                gather(0, h)
            with pool.Fori(1, ROUNDS) as r:
                for h in range(HANDS):
                    stage(r, h)
                    gather(r, h)
            for h in range(TAIL):
                stage(ROUNDS, h)
                gather(ROUNDS, h)

            def split_input(i, slots):
                for s in slots:
                    pool.wait_ge(f_xt[s], i + 1)
                at = toks(2 * i, len(slots) * P)
                pool.tensor_tensor(QL[:, :, at], QF[:, :, at], QH[:, :, at].bitcast(f32), ALU.subtract).then_inc(q_split, 1)

            with pool.Fori(0, PAIRS) as i:
                split_input(i, (0, 1))
            split_input(PAIRS, (0,))

            def residuals(t):
                pool.tensor_tensor(XN[:, tile(t)], XN[:, tile(t)], B2C[:, :], ALU.add).then_inc(res_ready, 1)
                pool.tensor_tensor(X[:, tile(t)], X[:, tile(t)], FB, ALU.add).then_inc(res_ready, 1)

            def rstd3(n, s):
                pool.wait_ge(v3_ready, n + 1)
                pool.tensor_tensor(RS3[:, s:s + 1], VE3[:, s:s + 1], mhalf[:, :], ALU.pow).then_inc(rs3_ready, 1)

            pool.wait_ge(b2_ready, 1)
            for s in range(2):
                pool.wait_ge(f_xs[s], PAIRS + (s == 0))
            residuals(0)
            residuals(1)
            with pool.Fori(0, PAIRS - 1) as b:
                for s in range(2):
                    residuals(2 * b + (s + 2))
                    rstd3(2 * b + s, s)
            residuals(TILES - 1)
            rstd3(TILES - 3, 0)
            rstd3(TILES - 2, 1)
            rstd3(TILES - 1, 0)

        @block.scalar
        def _(act):
            act.wait_ge(pool_const, 1)
            act.wait_ge(aggr_done, 1)
            act.activation(SD[:, :], MV[:, :, 1], ACT.Sqrt, bias=eps_ln[:, 0:1]).then_inc(std_ready, 1)
            act.wait_ge(rstd_ready, 1)

            def normalise(i, s):
                act.wait_ge(tp_done[s], i)
                act.wait_ge(xn_kept[s], i)
                act.activation(XS[:, s, :], X[:, tile(2 * i + s)], ACT.Identity, bias=NM[:, bass.ds(2 * i + s, 1)],
                               scale=RS[:, bass.ds(2 * i + s, 1)]).then_inc(xs_ready[s], 1)

            def xg_evacuate(h, q, s):
                act.wait_ge(g_done[s], 2 * h + (q + 1))
                act.wait_ge(xg_out[q], h * 16)
                act.copy(XGS[:, q, s, :], bank[1 + s][:, 0:C]).then_inc(xg_evac[s], 1)

            def xg_tiles(i, slots, following, before=None):
                for s in slots:
                    act.wait_ge(tp_done[s], i + 1)
                    act.wait_ge(g_done[s], i)
                    act.copy(XT[:, :, s, :], bank[3 * s][:, 0:C].rearrange("p (c n) -> p c n", n=P)).then_inc(xt_ready[s], 1)
                    if before:
                        xg_evacuate(*before, s)
                    if s in following:
                        normalise(i + 1, s)

            normalise(0, 0)
            normalise(0, 1)
            xg_tiles(0, (0, 1), (0, 1))
            with act.Fori(0, PAIRS // 2 - 1) as h:
                for q in range(2):
                    xg_tiles(2 * h + (q + 1), (0, 1), (0, 1), before=(h, q))
            xg_tiles(PAIRS - 1, (0, 1), (0,), before=(PAIRS // 2 - 1, 0))
            xg_tiles(PAIRS, (0,), (), before=(PAIRS // 2 - 1, 1))
            xg_evacuate(PAIRS // 2 - 1, 1, 1)
            xg_evacuate(PAIRS // 2, 0, 0)

            chain = Chain(act, act_step)
            act.wait_ge(lanes_ready, 1)

            def lanes(i, s):
                if not first_of(i):
                    act.wait_ge(grp_done, 4 * i + (s - 3))
                act.wait_ge(oi_ready[2 - s], i + s // 2)
                for k in range(GC):
                    ins = act.activation(LD[:, k, :], iota[:, :], ACT.Abs, scale=-1.0, bias=LANE[:, bass.ds((4 * i + s) * GC + k, 1)])
                chain.link(ins)
                act.activation(OI[:, s, :, :], LD[:, :, :], ACT.Relu, scale=-1.0, bias=ones[:, 0:1]).then_inc(oi_ready[s], 1)

            def evacuate(i, j):
                act.wait_ge(placed[j], i)
                for u in range(2):
                    s = 2 * j + u
                    act.wait_ge(grp_done, 4 * i + (s + 1))
                    act.copy(GSW[u * LC:(u + 1) * LC, j, :], bank[s][0:LC, 0:P])
                    ins = act.copy(GSP[u * LC:(u + 1) * LC, j, :], bank[s][LC:2 * LC, 0:P])
                ins.then_inc(gs_ready[j], 1)

            def sort_step(i, before=True):
                lanes(i, 0)
                if before:
                    evacuate(i - 1, 1)
                lanes(i, 2)
                evacuate(i, 0)

            sort_step(0, before=False)
            with chain.loop(NG // 4 - 1, 2, first=1) as i:
                sort_step(i)
            evacuate(NG // 4 - 1, 1)

            for s in range(2):
                act.wait_ge(xn_kept[s], PAIRS + (s == 0))
                act.wait_ge(g_done[s], PAIRS + (s == 0))

            def loop_a(i, slots):
                for s in slots:
                    act.wait_ge(a_tp[s], i)
                    act.copy(XS[:, s, :], XN[:, tile(2 * i + s)]).then_inc(a_xs[s], 1)
                for s in slots:
                    act.wait_ge(a_tp[s], i + 1)
                    act.wait_ge(q_done, i)
                    act.copy(XT[:, :, s, :], bank[s][:, 0:C].rearrange("p (c n) -> p c n", n=P)).then_inc(a_xt[s], 1)
                for s in slots:
                    act.wait_ge(kv_done[s], i + 1)
                    act.wait_ge(ks_ready[s], i)
                    act.activation(NK[:, s, :], bank[2 + s][:, 0:C], ACT.Relu, scale=-1.0).then_inc(nk_ready[s], 1)
                    act.activation(KR[:, s, :], bank[2 + s][:, 0:C], ACT.Relu)
                    act.wait_ge(kvacc_done[s], i)
                    act.copy(VX[:, s, :, 0:P], bank[2 + s][:, C:2 * C].rearrange("p (c n) -> p c n", n=P)).then_inc(vx_ready[s], 1)
                    act.wait_ge(nk_ready[s], i + 1)
                    act.activation(EXK[:, s, :], NK[:, s, :], ACT.Exp, scale=-1.0).then_inc(ek_ready[s], 1)
                n = len(slots) * P
                q = bank[5][:, :].rearrange("p (c n) -> p c n", c=CC)[:, :, 0:n]
                act.wait_ge(q_done, i + 1)
                act.wait_ge(qt_ready, i)
                act.activation(NQ[:, :, 0:n], q, ACT.Relu, scale=-1.0).then_inc(nq_ready, 1)
                act.activation(QR[:, :, 0:n], q, ACT.Relu)
                act.wait_ge(nq_ready, i + 1)
                act.activation(EQ[:, :, 0:n], NQ[:, :, 0:n], ACT.Exp, scale=-1.0).then_inc(eq_ready, 1)

            with act.Fori(0, PAIRS) as i:
                loop_a(i, (0, 1))
            loop_a(PAIRS, (0,))

            def b_query(i, slots):
                for s in slots:
                    act.wait_ge(t_done[s], i)
                    act.wait_ge(qt_ready, PAIRS + 1)
                    act.copy(QS[:, s, :, :], QT[:, :, toks(2 * i + s)]).then_inc(qs_ready[s], 1)

            def b_std(i, slots, m, var, sd):
                act.wait_ge(var, i + 1)
                act.activation(SD2[:, m, 0:len(slots)], MV2[:, m, 0:len(slots), 1], ACT.Sqrt, bias=eps_ln[:, 0:1]).then_inc(sd, 1)

            def b_normalise(i, slots):
                act.wait_ge(nm1, i + 1)
                act.wait_ge(x1tp, i)
                for s in slots:
                    act.activation(XS[:, s, :], TX[:, s, :], ACT.Identity, bias=NM2[:, s:s + 1],
                                   scale=RS2[:, 0, s:s + 1]).then_inc(x1_ready[s], 1)

            def b_hidden(i, slots):
                n = len(slots) * P
                act.wait_ge(x1tp, i + 1)
                for s in range(2):
                    act.wait_ge(y_done[s], i)
                turned = bank[0][:, 0:len(slots) * C].rearrange("p (s c n) -> p s c n", n=P, c=CC)
                for c in range(CC):
                    act.activation(XT[:, c, 0:len(slots), :], turned[:, :, c, :], ACT.Identity,
                                   bias=L1B[:, c:c + 1], scale=L1G[:, c:c + 1]).then_inc(x1t, 1)
                act.wait_ge(h_done, i + 1)
                for c in range(CC):
                    ins = act.activation(HS[:, c, 0:len(slots), :],
                                         bank[5][:, c * 2 * P:c * 2 * P + n].rearrange("p (s n) -> p s n", n=P),
                                         ACT.Gelu, bias=B1C[:, c:c + 1])
                    ins.then_inc(hs_ready, 1)

            b_query(0, (0, 1))
            b_query(1, (0, 1))
            b_std(0, (0, 1), 0, var1, sd1)
            b_normalise(0, (0, 1))
            b_hidden(0, (0, 1))
            b_query(2, (0, 1))
            b_std(1, (0, 1), 0, var1, sd1)
            b_normalise(1, (0, 1))
            b_hidden(1, (0, 1))
            with act.Fori(2, PAIRS - 1) as i:
                b_query(i + 1, (0, 1))
                b_std(i, (0, 1), 0, var1, sd1)
                b_std(i - 2, (0, 1), 1, var2, sd2)
                b_normalise(i, (0, 1))
                b_hidden(i, (0, 1))
            b_query(PAIRS, (0,))
            b_std(PAIRS - 1, (0, 1), 0, var1, sd1)
            b_std(PAIRS - 3, (0, 1), 1, var2, sd2)
            b_normalise(PAIRS - 1, (0, 1))
            b_hidden(PAIRS - 1, (0, 1))
            b_std(PAIRS - 2, (0, 1), 1, var2, sd2)
            b_std(PAIRS, (0,), 0, var1, sd1)
            b_std(PAIRS - 1, (0, 1), 1, var2, sd2)
            b_normalise(PAIRS, (0,))
            b_hidden(PAIRS, (0,))
            b_std(PAIRS, (0,), 1, var2, sd2)

            act.wait_ge(f_aggr, 1)
            act.activation(SD[:, :], MV[:, :, 1], ACT.Sqrt, bias=eps_ln[:, 0:1]).then_inc(f_sd, 1)
            act.wait_ge(f_rstd, 1)

            def ffn_normalise(i, s):
                act.wait_ge(f_tp[s], i)
                act.activation(XS[:, s, :], X[:, tile(2 * i + s)], ACT.Identity, bias=NM[:, bass.ds(2 * i + s, 1)],
                               scale=RS[:, bass.ds(2 * i + s, 1)]).then_inc(f_xs[s], 1)

            def ffn_tiles(i, slots, following):
                for s in slots:
                    act.wait_ge(f_tp[s], i + 1)
                    turned = bank[s][:, 0:C].rearrange("p (c n) -> p c n", n=P)
                    act.copy(QH[:, :, toks(2 * i + s)], turned)
                    act.copy(QF[:, :, toks(2 * i + s)], turned).then_inc(f_xt[s], 1)
                    if s in following:
                        ffn_normalise(i + 1, s)

            ffn_normalise(0, 0)
            ffn_normalise(0, 1)
            with act.Fori(0, EARLY) as i:
                ffn_tiles(i, (0, 1), (0, 1))

            for n, width in enumerate((NE, NE, TOPK)):
                act.wait_ge(r_shift, n + 1)
                act.activation(R[0:1, 11, 0:width], R[0:1, 10, 0:width], ACT.Exp).then_inc(r_exp, 1)
                if n < 2:
                    ffn_tiles(EARLY + n, (0, 1), (0, 1))

            with act.Fori(EARLY + 2, PAIRS - 1) as i:
                ffn_tiles(i, (0, 1), (0, 1))
            ffn_tiles(PAIRS - 1, (0, 1), (0,))
            ffn_tiles(PAIRS, (0,), ())

            act.wait_ge(up_in, 16 * 2 * TOPK)

            act.wait_ge(w1_split, 1)
            act.wait_ge(q_split, PAIRS + 1)

            def hidden(b, par, width=BLK):
                for n in range(NH):
                    s = n % UPS
                    act.wait_ge(up_done, b * NH + (n + 1))
                    if not first_of(b) or n >= UPS:
                        act.wait_ge(hl_ready, b * NH + (n + 1 - UPS))
                    if n == 0 and not (isinstance(b, int) and b < 2):
                        act.wait_ge(down_done[0], b - 1)
                        act.wait_ge(down_done[1], b - 1)
                    for into in (HF[:, s, 0:width], HFH[:, par, n, 0:width]):
                        ins = act.activation(into, bank[s][:, 0:width], ACT.Gelu, bias=FB1[:, n // FJ, n % FJ:n % FJ + 1])
                    ins.then_inc(gelu_done, 1)

            hidden(0, 0)
            hidden(1, 1)
            with act.Fori(1, NBLK // 2) as j:
                hidden(2 * j, 0)
                hidden(2 * j + 1, 1)
            hidden(NBLK, 0, P)

        @block.vector
        def _(dve):
            chain = Chain(dve, dve_step)
            V = nc.vector
            def bcast(ap, shape):
                return ap.to_broadcast(shape)

            def settle_for_aggr():
                chain.settle()
                V.memset(carrier[0:1, 0:1], 0.0)

            def mean_and_variance():
                st = ST[:, :].rearrange("p (t k) -> p k t", k=6)
                chain.mark(V.tensor_tensor(SD[:, :], st[:, 1, :], st[:, 4, :], ALU.add))
                chain.mark(V.tensor_tensor(RS[:, :], st[:, 1, :], st[:, 4, :], ALU.subtract))
                chain.mark(V.tensor_tensor(NM[:, :], st[:, 2, :], st[:, 5, :], ALU.add))
                chain.settle()
                chain.mark(V.tensor_scalar(MV[:, :, 0], SD[:, :], 0.5, None, ALU.mult))
                chain.mark(V.scalar_tensor_tensor(out=RS[:, :], in0=RS[:, :], scalar=0.25, in1=RS[:, :], op0=ALU.mult, op1=ALU.mult))
                chain.settle()
                return V.scalar_tensor_tensor(out=MV[:, :, 1], in0=NM[:, :], scalar=1.0 / C, in1=RS[:, :], op0=ALU.mult, op1=ALU.add)

            UN = 5
            assert TILES % UN == 0

            def tile_statistics(t, done):
                V.bn_stats(ST[:, bass.ds(t * 6, 6)], X[:, tile(t)]).then_inc(done, 1)

            def statistics(tiles, done):
                with dve.Fori(0, tiles // UN) as n:
                    for m in range(UN):
                        tile_statistics(n * UN + m, done)

            dve.wait_ge(e_in, 48)
            chain.mark(V.tensor_scalar(EBI[:, :], EROW[:, :], 7, None, ALU.arith_shift_right))
            chain.mark(V.tensor_scalar(ELO[:, :], EROW[:, :], P - 1, None, ALU.bitwise_and))
            chain.mark(V.tensor_scalar(EPCI[:, :], ECOL[:, :], 7, None, ALU.arith_shift_left))
            chain.settle()
            chain.mark(V.tensor_copy(EBF[:, :], EBI[:, :]))
            chain.link(V.tensor_tensor(TMPI[:, :], EPCI[:, :], ELO[:, :], ALU.bitwise_or))
            chain.link(V.tensor_copy(EPC[:, :], TMPI[:, :]))

            dve.wait_ge(iota_ready, 1)
            with chain.loop(TILES // UN, UN) as n:
                for m in range(UN):
                    b = n * UN + m
                    chain.mark(V.tensor_scalar(OH[:, bass.ds(b, 1), :].rearrange("p a k -> p (a k)"), EBF[:, :],
                                               iota[:, bass.ds(b, 1)], None, ALU.is_equal))

            dve.wait_ge(x_in, 16)
            statistics(TILES, stats_done)
            dve.wait_ge(stats_done, TILES)
            mean_and_variance().then_inc(aggr_done, 1)

            chain.settle()
            dve.wait_ge(pool_const, 1)

            def running_counts(b):
                V.tensor_tensor_scan(SC[:, bass.ds(b, 1), :].rearrange("p a k -> p (a k)"), RESTART[:, :],
                                     OH[:, bass.ds(b, 1), :].rearrange("p a k -> p (a k)"), 0.0,
                                     ALU.mult, ALU.add).then_inc(counted, 1)

            for b in range(UN - 2):
                running_counts(b)
            dve.wait_ge(std_ready, 1)
            chain.link(V.reciprocal(RS[:, :], SD[:, :]))
            V.scalar_tensor_tensor(out=NM[:, :], in0=MV[:, :, 0], scalar=-1.0, in1=RS[:, :],
                                   op0=ALU.mult, op1=ALU.mult).then_inc(rstd_ready, 1)
            for b in range(UN - 2, UN):
                running_counts(b)
            with dve.Fori(1, TILES // UN) as n:
                for m in range(UN):
                    running_counts(n * UN + m)
            dve.wait_ge(totals_done, 1)
            HB = TILES // 2
            chain.mark(V.tensor_copy(CNT[:, 0:HB, :], bank[4][:, 0:HB * NG].rearrange("p (b g) -> p b g", g=NG)))
            chain.link(V.tensor_copy(CNT[:, HB:TILES, :], bank[5][:, 0:(TILES - HB) * NG].rearrange("p (b g) -> p b g", g=NG)))
            flat = lambda m: m[:, :, :].rearrange("p a b -> p (a b)")
            gb = lambda m: m[:, :, :].rearrange("p b g -> p g b")
            chain.link(V.tensor_tensor_scan(flat(Q1), flat(RSB), flat(CNT), 0.0, ALU.mult, ALU.add))
            chain.mark(V.tensor_tensor(flat(Q0), flat(Q1), flat(CNT), ALU.subtract))
            chain.mark(V.tensor_copy(flat(Q1I), flat(Q1)))
            chain.mark(V.tensor_scalar(NBF[:, :], Q1[:, :, NG - 1], float(P - 1), None, ALU.add))
            chain.settle()
            chain.mark(V.tensor_copy(flat(Q0I), flat(Q0)))
            chain.mark(V.tensor_copy(NBI[:, :], NBF[:, :]))
            chain.settle()
            chain.mark(V.tensor_scalar(flat(QLI), flat(Q0I), P - 1, None, ALU.bitwise_and))
            chain.mark(V.tensor_scalar(flat(Q0I), flat(Q0I), 7, None, ALU.arith_shift_right))
            chain.mark(V.tensor_scalar(flat(Q1I), flat(Q1I), 7, None, ALU.arith_shift_right))
            chain.mark(V.tensor_scalar(NBI[:, :], NBI[:, :], 7, None, ALU.arith_shift_right))
            chain.settle()
            chain.mark(V.tensor_copy(flat(F0), flat(Q0I)))
            chain.mark(V.tensor_copy(flat(F1), flat(Q1I)))
            chain.mark(V.tensor_copy(TAB0[:, :, :], gb(QLI)))
            chain.mark(V.tensor_copy(NBF[:, :], NBI[:, :]))
            chain.settle()
            chain.mark(V.tensor_tensor(flat(F1), flat(F1), flat(F0), ALU.subtract))
            chain.mark(V.tensor_tensor_scan(CBI[:, :], ones[:, 0:TILES], NBF[:, :], 0.0, ALU.mult, ALU.add))
            chain.settle()
            chain.mark(V.tensor_scalar(TCH[:, :, :], gb(F1), 1.0, None, ALU.add))
            chain.mark(V.tensor_tensor(CB[:, :], CBI[:, :], NBF[:, :], ALU.subtract))
            chain.settle()
            chain.mark(V.tensor_tensor(CBD[:, :], CB[:, :], ident[:, 0:TILES], ALU.mult))
            chain.link(V.tensor_tensor_scan(flat(LINC), flat(RSG), flat(TCH), 0.0, ALU.mult, ALU.add))
            chain.mark(V.tensor_reduce(CBP[:, :], CBD[:, :], AX.X, ALU.add))
            chain.mark(V.tensor_tensor(flat(LOFF), flat(LINC), flat(TCH), ALU.subtract))
            chain.mark(V.tensor_tensor(DC[:, :, :], gb(F0), CB[:, :].rearrange("p (o b) -> p o b", o=1).to_broadcast([P, NG, TILES]), ALU.add))
            chain.settle()
            V.tensor_scalar(flat(TAB1), flat(LOFF), float(P), None, ALU.mult).then_inc(tables_ready, 1)
            V.tensor_scalar(CMP[:, :], iota_c[:, :], CBP[:, 0:1], None, ALU.is_ge).then_inc(bid_cmp, 1)
            chain.link(V.tensor_tensor(flat(DC), flat(DC), flat(LOFF), ALU.subtract))
            chain.mark(V.tensor_copy(DD[:, :, 0:1], DC[:, :, 0:1]))
            chain.mark(V.tensor_tensor(DD[:, :, 1:TILES], DC[:, :, 1:TILES], DC[:, :, 0:TILES - 1], ALU.subtract))
            chain.mark(V.tensor_scalar(local_i[:, :], local_i[:, :], LC - 1, None, ALU.bitwise_and))
            chain.settle()
            chain.link(V.tensor_copy(local_p[:, :], local_i[:, :]))
            chain.link(V.scalar_tensor_tensor(out=flat(DC), in0=flat(LOFF), scalar=local_p[:, 0:1], in1=flat(DD),
                                              op0=ALU.is_le, op1=ALU.mult))
            chain.link(V.tensor_reduce(JMAP[:, :], DC[:, :, :], AX.X, ALU.add))
            chain.link(V.tensor_scalar(JMAP[:, :], JMAP[:, :], local_p[:, 0:1], None, ALU.add))
            for u in range(2):
                of_u = JMAP[u * LC:(u + 1) * LC, :].rearrange("p (g u) -> p g u", u=2)[:, :, u]
                chain.mark(V.tensor_copy(JPAIR[u * LC:(u + 1) * LC, :], of_u))
            dve.wait_ge(bid_sum, 1)
            whole = ROUNDS * RC
            chain.link(V.tensor_scalar(BID[0:1, 0:ROUNDS, 0:RC], bank[6][0:1, 0:whole].rearrange("p (r c) -> p r c", c=RC),
                                       -1.0, float(C), ALU.add, ALU.mult))
            V.tensor_scalar(BID[0:1, ROUNDS, 0:COLS - whole], bank[6][0:1, whole:COLS],
                            -1.0, float(C), ALU.add, ALU.mult).then_inc(bid_ready, 1)
            dve.wait_ge(bid_ready, 1)

            def slot_rank(g):
                at = lambda s: bass.ds((2 * g + s) * GC, GC)
                so_far = chain.n
                for s in range(2):
                    dve.wait_ge(rank_done[s], g + 1)
                    dve.wait_ge(dve_step, so_far - 1 + s)
                    V.tensor_tensor(PRD[:, s, :, :], bank[4 + s][:, 0:TILES * GC].rearrange("p (b k) -> p b k", k=GC),
                                    OH[:, :, at(s)], ALU.mult).then_inc(rank_read[s], 1)
                for s in range(2):
                    dve.wait_ge(rank_read[s], g + 1)
                    chain.mark(V.tensor_reduce(SLOT[:, at(s)], PRD[:, s, :, :].rearrange("p b k -> p k b"), AX.X, ALU.add))

            with chain.loop(NG // 2, 2) as g:
                slot_rank(g)
            chain.settle()
            chain.link(V.tensor_copy(SLOTI[:, :], SLOT[:, :]))
            chain.mark(V.tensor_scalar(TMPI[:, :], SLOTI[:, :], 7, None, ALU.arith_shift_right))
            chain.mark(V.tensor_scalar(SLOTI[:, :], SLOTI[:, :], P - 1, None, ALU.bitwise_and))
            chain.settle()
            chain.mark(V.tensor_copy(LCOL[:, :], TMPI[:, :]))
            V.tensor_copy(LANE[:, :], SLOTI[:, :]).then_inc(lanes_ready, 1)
            chain.settle()
            dve.wait_ge(lanes_ready, 1)

            def pair_operands(i, j):
                pair = (2 * j, 2 * j + 1)
                for s in pair:
                    if not first_of(i):
                        dve.wait_ge(ap_ready, 4 * i + (s - 3))
                    if not first_of(i):
                        dve.wait_ge(as_ready, 4 * i + (s - 3))
                    V.tensor_tensor(LH[:, s, :, :], per_row(LC), per_chunk(LCOL, i, s, LC), ALU.is_equal).then_inc(lh_ready, 1)
                for s in reversed(pair):
                    if not first_of(i):
                        dve.wait_ge(grp_done, 4 * i + (s - 3))
                    if s == pair[1]:
                        V.tensor_tensor(OI[:, s, :, :], per_row(P), per_chunk(LANE, i, s, P), ALU.is_equal).then_inc(oi_ready[s], 1)
                for s in pair:
                    dve.wait_ge(lh_ready, 4 * i + (s + 1))
                    V.tensor_tensor(AS[:, s, :, 0:LC], LH[:, s, :, :], per_chunk(EW, i, s, LC), ALU.mult).then_inc(as_ready, 1)
                dve.wait_ge(placed[j], i)
                V.tensor_scalar(OJ[:, j, :], iota_c[:, :], JPAIR[:, bass.ds(2 * i + j, 1)], None, ALU.is_equal).then_inc(oj_ready[j], 1)

            pair_operands(0, 0)
            pair_operands(0, 1)
            with dve.Fori(1, NG // 4) as i:
                pair_operands(i, 0)
                pair_operands(i, 1)

            dve.wait_ge(table_done, 1)
            chain.mark(V.tensor_copy(SW[:, :], bank[6][:, 0:COLS]))
            chain.link(V.tensor_copy(SPI[:, :], bank[7][:, 0:COLS]))
            chain.mark(V.tensor_scalar(SLI[:, :], SPI[:, :], P - 1, None, ALU.bitwise_and))
            V.tensor_scalar(SIX[:, :], SPI[:, :], 7, None, ALU.arith_shift_right).then_inc(slots_ready, 1)
            chain.settle()
            chain.link(V.tensor_copy(SLO[:, :], SLI[:, :]))

            def targets(r, cols=RC):
                _, base = nc.values_load_multi_w_load_instructions(
                    BID[0:1, bass.ds(r, 1), 0:cols].rearrange("p a c -> p (a c)"), engines=[mybir.EngineType.DVE],
                    min_val=0, max_val=(TILES - 1) * C,
                    skip_runtime_bounds_check_because="BID counts the buckets whose first column is at or before the "
                    "column, less one: the first bucket starts at column 0, so it lies in 0 .. TILES - 1, times C")
                return base

            def nth(r, h, k):
                return r * (RC // 2) + (h * (HAND // 2) + k // 2)

            def select(r, h, k):
                at = bass.ds(r * RC + (h * HAND + k), 1)
                V.tensor_scalar(SEL[:, k, :], iota[:, :], SLO[:, at], SW[:, at], ALU.is_equal, ALU.mult).then_inc(sel_ready[k % 2], 1)

            def add(base, r, h, k):
                s = k % 2
                dve.wait_ge(chunk_mm[s], nth(r, h, k) + 1)
                dve.wait_ge(x_added[1 - s], nth(r, h, k + s) )
                xt = X[:, bass.ds(base[h * HAND + k], C)]
                V.tensor_tensor(xt, bank[6 + s][:, 0:C], xt, ALU.add).then_inc(x_added[s], 1)

            def hand(base, r, h, ks=range(HAND), final=False):
                for k in ks:
                    add(base, r, h, k)
                    if not final:
                        select(r, h + 1, k)

            for k in range(HAND):
                select(0, 0, k)
            dve.wait_ge(x_biased, TILES)

            def a_feature(i, slots):
                for s in slots:
                    dve.wait_ge(ek_ready[s], i + 1)
                    dve.wait_ge(kvacc_done[s], i)
                    V.tensor_tensor(KS[:, s, :], KR[:, s, :], EXK[:, s, :], ALU.add).then_inc(ks_ready[s], 1)
                n = len(slots) * P
                dve.wait_ge(eq_ready, i + 1)
                V.tensor_tensor(QT[:, :, toks(2 * i, n)], QR[:, :, 0:n], EQ[:, :, 0:n], ALU.add).then_inc(qt_ready, 1)

            with dve.Fori(0, PAIRS) as i:
                base = targets(i)
                hand(base, i, 0)
                hand(base, i, 1)
                a_feature(i, (0, 1))
                hand(base, i, 2)
            base = targets(PAIRS)
            hand(base, PAIRS, 0)
            a_feature(PAIRS, (0,))

            dve.wait_ge(kv_summed, 1)
            for c in range(CC):
                ins = V.tensor_tensor(KVM[:, c, :], bank[4][:, c * VE:(c + 1) * VE], hmask[:, :], ALU.mult)
                ins.then_inc(kvm_ready, 1)

            def links(steps, carried=False):
                for step in steps:
                    for ins in step:
                        chain.mark(ins())
                    if carried and step is steps[-1]:
                        settle_for_aggr()
                    else:
                        chain.settle()

            def aggregate(m, slots, var):
                for s in slots:
                    ins = V.bn_aggr(MV2[:, m, s, :], ST2[:, m, s, :])
                ins.then_inc(var, 1)

            def b_attend(i, slots):
                per_s = lambda f: [lambda s=s: f(s) for s in slots]
                for s in slots:
                    dve.wait_ge(t_done[s], i + 1)
                    dve.wait_ge(x1_ready[s], i)
                ps = lambda s: bank[1 + s][:, 0:CC * VE].rearrange("p (c n) -> p c n", n=VE)
                links([
                    per_s(lambda s: V.tensor_scalar(DEN[:, s, :].rearrange("p (c h) -> p c h", c=CC), ps(s)[:, :, P:VE], EPS_ATTN, None, ALU.add)),
                    per_s(lambda s: V.reciprocal(RZ[:, s, :], DEN[:, s, :])),
                    [lambda s=s, c=c: V.tensor_tensor(
                        TX[:, s, c * P:(c + 1) * P].rearrange("p (h d) -> p h d", d=HD),
                        ps(s)[:, c, 0:P].rearrange("p (h d) -> p h d", d=HD),
                        RZ[:, s, c * HH:(c + 1) * HH].rearrange("p (h o) -> p h o", o=1).to_broadcast([P, HH, HD]), ALU.mult)
                        for s in slots for c in range(CC)],
                    per_s(lambda s: V.tensor_tensor(TX[:, s, :], TX[:, s, :], XN[:, tile(2 * i + s)], ALU.add)),
                    per_s(lambda s: V.bn_stats(ST2[:, 0, s, :], TX[:, s, :])),
                ], carried=True)
                aggregate(0, slots, var1)

            def b_x1(i, slots):
                n = len(slots)
                dve.wait_ge(sd1, i + 1)
                chain.link(V.reciprocal(RS2[:, 0, 0:n], SD2[:, 0, 0:n]))
                V.scalar_tensor_tensor(out=NM2[:, 0:n], in0=MV2[:, 0, 0:n, 0], scalar=-1.0, in1=RS2[:, 0, 0:n],
                                       op0=ALU.mult, op1=ALU.mult).then_inc(nm1, 1)

            def b_out(i, slots):
                for s in slots:
                    dve.wait_ge(y_done[s], i + 1)
                links([[lambda s=s: V.bn_stats(ST2[:, 1, s, :], bank[3 + s][:, 0:C]) for s in slots]], carried=True)
                aggregate(1, slots, var2)
                dve.wait_ge(var2, i + 1)
                for s in slots:
                    V.scalar_tensor_tensor(out=TN[:, s, :], in0=bank[3 + s][:, 0:C], scalar=MV2[:, 1, s, 0:1],
                                           in1=L2G, op0=ALU.subtract, op1=ALU.mult).then_inc(y_used[s], 1)

            def b_update(i, slots, r, h, k):
                n = len(slots)
                dve.wait_ge(sd2, i + 1)
                chain.link(V.reciprocal(RS2[:, 1, 0:n], SD2[:, 1, 0:n]))
                for s in range(2):
                    dve.wait_ge(x_added[s], nth(r, h, k + 1 - s))
                for s in slots:
                    dve.wait_ge(y_used[s], i + 1)
                    xt = X[:, tile(2 * i + s)]
                    chain.mark(V.scalar_tensor_tensor(out=xt, in0=TN[:, s, :], scalar=RS2[:, 1, s:s + 1], in1=xt,
                                                      op0=ALU.mult, op1=ALU.add))
                chain.settle()

            b_attend_n, b_x1_n, b_out_n, b_update_n = 12, 1, 2, 3
            hand(base, PAIRS, 1)
            b_attend(0, (0, 1))
            hand(base, PAIRS, 2, range(0, 3))
            b_x1(0, (0, 1))
            hand(base, PAIRS, 2, range(3, 6))

            def b_step(i, before=None):
                r = i + PAIRS
                base = targets(r)
                hand(base, r, 0)
                b_attend(i, (0, 1))
                hand(base, r, 1, range(0, 3))
                b_x1(i, (0, 1))
                if before is not None:
                    b_update(before, (0, 1), r, 1, 3)
                hand(base, r, 1, range(3, 6))
                hand(base, r, 2)
                b_out(i - 1, (0, 1))

            b_step(1)
            with chain.loop(PAIRS - 2, b_attend_n + b_x1_n + b_out_n + b_update_n, first=2) as i:
                b_step(i, before=i - 2)
            base = targets(ROUNDS, TAIL * HAND)
            hand(base, ROUNDS, 0)
            b_update(PAIRS - 2, (0, 1), ROUNDS, 0, HAND)
            b_attend(PAIRS, (0,))
            b_out(PAIRS - 1, (0, 1))
            b_x1(PAIRS, (0,))
            hand(base, ROUNDS, 1, final=True)
            b_update(PAIRS - 1, (0, 1), ROUNDS, 1, HAND)
            statistics(TILES - UN, f_stats)
            b_out(PAIRS, (0,))
            for t in range(TILES - UN, TILES - 1):
                tile_statistics(t, f_stats)
            b_update(PAIRS, (0,), ROUNDS, 1, HAND)

            tile_statistics(TILES - 1, f_stats)
            dve.wait_ge(f_stats, TILES)
            mean_and_variance().then_inc(f_aggr, 1)
            dve.wait_ge(f_sd, 1)
            chain.link(V.reciprocal(RS[:, :], SD[:, :]))
            V.scalar_tensor_tensor(out=NM[:, :], in0=MV[:, :, 0], scalar=-1.0, in1=RS[:, :],
                                   op0=ALU.mult, op1=ALU.mult).then_inc(f_rstd, 1)
            with dve.Fori(0, TILES // UN) as n:
                for m in range(UN):
                    t = n * UN + m
                    V.tensor_scalar(XN[:, tile(t)], X[:, tile(t)], MV[:, bass.ds(t, 1), 0], RS[:, bass.ds(t, 1)],
                                    ALU.subtract, ALU.mult).then_inc(f_xn, 1)

            dve.wait_ge(mean_done, 1)
            V.tensor_scalar(MEANR[:, :], bank[3][0:1, 0:C], 1.0 / N, None, ALU.mult).then_inc(mean_ready, 1)
            dve.wait_ge(mean_turned, 1)
            V.tensor_copy(MEAN[:, :], bank[4][:, 0:CC]).then_inc(mean_col, 1)
            dve.wait_ge(logits_done, 1)
            chain.link(V.tensor_tensor(R[0:1, 0, :], bank[5][0:1, 0:NE], RB[:, :], ALU.add))

            def softmax(src, dst, width, n):
                chain.link(V.tensor_reduce(R[0:1, 1, 0:1], src, AX.X, ALU.max))
                V.tensor_scalar(R[0:1, 10, 0:width], src, R[0:1, 1, 0:1], None, ALU.subtract).then_inc(r_shift, 1)
                dve.wait_ge(r_exp, n)
                chain.link(V.tensor_reduce(R[0:1, 1, 1:2], R[0:1, 11, 0:width], AX.X, ALU.add))
                chain.link(V.reciprocal(R[0:1, 1, 2:3], R[0:1, 1, 1:2]))
                return V.tensor_scalar(dst, R[0:1, 11, 0:width], R[0:1, 1, 2:3], None, ALU.mult)

            chain.link(softmax(R[0:1, 0, :], R[0:1, 2, :], NE, 1))
            chain.link(V.tensor_scalar(R[0:1, 3, :], R[0:1, 2, :], float(N), 1.0, ALU.mult, ALU.max))
            chain.link(V.reciprocal(R[0:1, 4, :], R[0:1, 3, :]))
            chain.link(V.tensor_scalar(R[0:1, 5, :], R[0:1, 4, :], CAPACITY, 1.0, ALU.mult, ALU.min))
            chain.link(V.tensor_tensor(R[0:1, 6, :], R[0:1, 2, :], R[0:1, 5, :], ALU.mult))
            chain.link(softmax(R[0:1, 6, :], R[0:1, 7, :], NE, 2))
            chain.link(V.max(R[0:1, 8, :], R[0:1, 7, :]))
            V.max_index(RI[0:1, :], R[0:1, 8, :], R[0:1, 7, :]).then_inc(topi_ready, 1)
            softmax(R[0:1, 8, 0:TOPK], R[0:1, 9, 0:TOPK], TOPK, 3).then_inc(topw_ready, 1)

            dve.wait_ge(up_in, 16 * 2 * TOPK)
            chain.link(V.tensor_copy(W1H[:, :, :, :], FW1[:, :, :, :]))
            V.tensor_tensor(W1L[:, :, :, :], FW1[:, :, :, :], W1H[:, :, :, :].bitcast(f32), ALU.subtract).then_inc(w1_split, 1)
            dve.wait_ge(wb_done, 1)
            chain.link(V.tensor_copy(WB[:, :], bank[6][:, 0:TOPK]))
            dve.wait_ge(down_in, 16 * 2 * TOPK)
            chain.link(V.tensor_scalar(B2C[:, :], FB2[:, 0, :], WB[:, 0:1], None, ALU.mult))
            V.scalar_tensor_tensor(out=B2C[:, :], in0=FB2[:, 1, :], scalar=WB[:, 1:2], in1=B2C[:, :],
                                   op0=ALU.mult, op1=ALU.add).then_inc(b2_ready, 1)
            for e in range(TOPK):
                chain.mark(V.tensor_scalar(FW2[:, e * FJ:(e + 1) * FJ, :], FW2[:, e * FJ:(e + 1) * FJ, :], WB[:, e:e + 1], None, ALU.mult))
            chain.settle()
            chain.link(V.tensor_copy(W2H[:, :, :], FW2[:, :, :]))
            V.tensor_tensor(W2L[:, :, :], FW2[:, :, :], W2H[:, :, :].bitcast(f32), ALU.subtract).then_inc(w2_scaled, 1)

            def split_hidden(b, par, ns, width=BLK):
                for n in ns:
                    s = n % UPS
                    dve.wait_ge(gelu_done, b * NH + (n + 1))
                    V.tensor_tensor(HFL[:, par, n, 0:width], HF[:, s, 0:width], HFH[:, par, n, 0:width].bitcast(f32),
                                    ALU.subtract).then_inc(hl_ready, 1)

            def out_statistics(b, s):
                dve.wait_ge(down_done[s], b + 1)
                dve.wait_ge(res_ready, 4 * b + 2 * (s + 1))
                V.tensor_tensor(Y[:, s, :], bank[4 + s][:, 0:C], XN[:, tile(2 * b + s)], ALU.add).then_inc(y_read[s], 1)
                dve.wait_ge(y_read[s], b + 1)
                chain.mark(V.bn_stats(ST3[:, s, :], Y[:, s, :]))
                settle_for_aggr()
                chain.link(V.bn_aggr(MV3[:, s, :], ST3[:, s, :]))
                V.tensor_scalar(VE3[:, s:s + 1], MV3[:, s, 1:2], EPS_LN, None, ALU.add).then_inc(v3_ready, 1)

            def out_norm(b, s):
                chain.mark(V.scalar_tensor_tensor(out=YN[:, s, :], in0=Y[:, s, :], scalar=MV3[:, s, 0:1], in1=FG,
                                                  op0=ALU.subtract, op1=ALU.mult))
                dve.wait_ge(rs3_ready, 2 * b + (s + 1))
                dve.wait_ge(out_done[s], b * 16)
                chain.settle()
                V.scalar_tensor_tensor(out=YO[:, s, :], in0=YN[:, s, :], scalar=RS3[:, s:s + 1], in1=X[:, tile(2 * b + s)],
                                       op0=ALU.mult, op1=ALU.add).then_inc(yo_ready[s], 1)

            def out_step(b, par, before=True, width=BLK):
                split_hidden(b + 1, par, range(0, 4), width)
                if before:
                    out_norm(b - 1, 1)
                out_statistics(b, 0)
                split_hidden(b + 1, par, range(4, 8), width)
                out_norm(b, 0)
                out_statistics(b, 1)

            split_hidden(0, 0, range(NH))
            out_step(0, 1, before=False)
            with chain.loop(NBLK // 2 - 1, 12) as j:
                out_step(2 * j + 1, 0)
                out_step(2 * j + 2, 1)
            out_step(NBLK - 1, 0, width=P)
            out_norm(NBLK - 1, 1)
            out_statistics(NBLK, 0)
            out_norm(NBLK, 0)

        @block.tensor
        def _(pe):
            T = nc.tensor
            pe.wait_ge(gw_in, 16)
            pe.wait_ge(pool_const, 1)

            def transpose_tile(into, src):
                for c in range(CC):
                    ins = T.transpose(into[:, c * P:(c + 1) * P], src[:, c * P:(c + 1) * P], ident[:, :])
                return ins

            def transpose_xn(i, s):
                pe.wait_ge(xs_ready[s], i + 1)
                pe.wait_ge(xt_ready[s], i)
                transpose_tile(bank[3 * s], XS[:, s, :]).then_inc(tp_done[s], 1)

            def xg_tiles(i, slots, following):
                for s in slots:
                    pe.wait_ge(xt_ready[s], i + 1)
                    pe.wait_ge(xg_evac[s], i)
                    for c in range(CC):
                        ins = T.matmul(bank[1 + s][:, 0:C], XT[:, c, s, :], GW[:, c, :], start=(c == 0), stop=(c == CC - 1))
                    ins.then_inc(g_done[s], 1)
                    if s in following:
                        transpose_xn(i + 1, s)

            BEFORE = PAIRS // 3
            transpose_xn(0, 0)
            transpose_xn(0, 1)
            with pe.Fori(0, BEFORE) as i:
                xg_tiles(i, (0, 1), (0, 1))

            HB = TILES // 2
            pe.wait_ge(counted, TILES)
            last_k = SC[:, :, :].rearrange("p b (g k) -> p b g k", k=GC)[:, :, :, GC - 1]
            T.matmul(bank[4][:, 0:HB * NG], onesb[:, :], last_k[:, 0:HB, :], start=True, stop=True)
            T.matmul(bank[5][:, 0:(TILES - HB) * NG], onesb[:, :], last_k[:, HB:TILES, :], start=True, stop=True).then_inc(totals_done, 1)

            with pe.Fori(BEFORE, PAIRS - 1) as i:
                xg_tiles(i, (0, 1), (0, 1))
            xg_tiles(PAIRS - 1, (0, 1), (0,))
            xg_tiles(PAIRS, (0,), ())

            pe.wait_ge(bid_cmp, 1)
            T.matmul(bank[6][0:1, 0:COLS], ones[0:TILES, 0:1], CMP[0:TILES, :], start=True, stop=True).then_inc(bid_sum, 1)

            pe.wait_ge(tables_ready, 1)

            def rank(g, s):
                G = 2 * g + s
                pe.wait_ge(rank_read[s], g)
                at = bass.ds(G * GC, GC)
                ps = bank[4 + s][:, 0:TILES * GC]
                tab = lambda m: m[:, bass.ds(G, 1), :].rearrange("p g (b o) -> p (g b) o", o=1).to_broadcast([P, TILES, GC])
                T.matmul(ps, onesb[:, :], SC[:, :, at], start=True, stop=False)
                T.matmul(ps, from_here[:, :], OH[:, :, at], start=False, stop=False)
                T.matmul(ps, row0[:, :], tab(TAB0), start=False, stop=False)
                T.matmul(ps, row0[:, :], tab(TAB1), start=False, stop=True).then_inc(rank_done[s], 1)

            with pe.Fori(0, NG // 2) as g:
                rank(g, 0)
                rank(g, 1)

            pe.wait_ge(bid_ready, 1)
            T.matmul(bank[6][:, 0:COLS], zeros[:, :], iota_c[:, :], start=True, stop=False)
            T.matmul(bank[7][:, 0:COLS], zeros[:, :], iota_c[:, :], start=True, stop=False)

            def group(i, s):
                pe.wait_ge(as_ready, 4 * i + (s + 1))
                pe.wait_ge(ap_ready, 4 * i + (s + 1))
                pe.wait_ge(oi_ready[s], i + 1)
                pe.wait_ge(gs_ready[s // 2], i)
                for k in range(GC):
                    ins = T.matmul(bank[s][:, 0:P], AS[:, s, k, :], OI[:, s, k, :], start=(k == 0), stop=(k == GC - 1))
                ins.then_inc(grp_done, 1)

            def place(i, j):
                pe.wait_ge(gs_ready[j], i + 1)
                pe.wait_ge(oj_ready[j], i + 1)
                T.matmul(bank[6][:, 0:COLS], GSW[:, j, :], OJ[:, j, :], start=False, stop=False, skip_group_check=True)
                T.matmul(bank[7][:, 0:COLS], GSP[:, j, :], OJ[:, j, :], start=False, stop=False, skip_group_check=True).then_inc(placed[j], 1)

            def sort_step(i, before=True):
                group(i, 0)
                group(i, 1)
                if before:
                    place(i - 1, 1)
                group(i, 2)
                group(i, 3)
                place(i, 0)

            sort_step(0, before=False)
            with pe.Fori(1, NG // 4) as i:
                sort_step(i)
            place(NG // 4 - 1, 1)
            T.matmul(bank[6][:, 0:COLS], zeros[:, :], iota_c[:, :], start=False, stop=True)
            T.matmul(bank[7][:, 0:COLS], zeros[:, :], iota_c[:, :], start=False, stop=True).then_inc(table_done, 1)

            def hand(r, h, ks=range(HAND)):
                for k in ks:
                    s = k % 2
                    n = r * (RC // 2) + (h * (HAND // 2) + k // 2)
                    pe.wait_ge(sel_ready[s], n + 1)
                    pe.wait_ge(x_added[s], n)
                    if k == ks[0]:
                        pe.wait_ge(gathered[h], r * (16 * HAND) + 16 * HAND)
                    T.matmul(bank[6 + s][:, 0:C], SEL[:, k, :], RING[:, h * HAND + k, :], start=True, stop=True).then_inc(chunk_mm[s], 1)

            pe.wait_ge(w_in, WEIGHTS_IN)
            pe.wait_ge(slots_ready, 1)
            T.matmul(bank[4][:, 0:CC * VE], zeros[:, :], iota_c[:, 0:CC * VE], start=True, stop=False)

            def a_transpose(i, slots):
                for s in slots:
                    pe.wait_ge(a_xs[s], i + 1)
                    pe.wait_ge(a_xt[s], i)
                    transpose_tile(bank[s], XS[:, s, :]).then_inc(a_tp[s], 1)

            def a_project(i, slots):
                for s in slots:
                    pe.wait_ge(a_xt[s], i + 1)
                    pe.wait_ge(vx_ready[s], i)
                    for c in range(CC):
                        ins = T.matmul(bank[2 + s][:, :], XT[:, c, s, :], QKVW[:, c, C:3 * C], start=(c == 0), stop=(c == CC - 1))
                    ins.then_inc(kv_done[s], 1)
                pe.wait_ge(eq_ready, i)
                n = len(slots) * P
                for h in range(CC):
                    for c in range(CC):
                        ins = T.matmul(bank[5][:, h * 2 * P:h * 2 * P + n], QKVW[:, c, h * P:(h + 1) * P],
                                       XT[:, c, 0:len(slots), :], start=(c == 0), stop=(c == CC - 1))
                ins.then_inc(q_done, 1)

            def a_outer(i, slots, rows=P):
                for s in slots:
                    pe.wait_ge(ks_ready[s], i + 1)
                    pe.wait_ge(vx_ready[s], i + 1)
                    for c in range(CC):
                        ins = T.matmul(bank[4][:, c * VE:(c + 1) * VE], KS[0:rows, s, c * P:(c + 1) * P], VX[0:rows, s, c, :],
                                       start=False, stop=False, skip_group_check=True)
                    ins.then_inc(kvacc_done[s], 1)

            with pe.Fori(0, PAIRS) as i:
                a_transpose(i, (0, 1))
                hand(i, 0)
                a_project(i, (0, 1))
                hand(i, 1)
                hand(i, 2)
                a_outer(i, (0, 1))
            a_transpose(PAIRS, (0,))
            hand(PAIRS, 0)
            a_project(PAIRS, (0,))
            hand(PAIRS, 1, range(0, 2))
            a_outer(PAIRS, (0,), LAST)
            T.matmul(bank[4][:, 0:CC * VE], zeros[:, :], iota_c[:, 0:CC * VE], start=False, stop=True).then_inc(kv_summed, 1)

            hand(PAIRS, 1, range(2, 6))

            pe.wait_ge(kvm_ready, CC)

            def b_attend(i, slots):
                for s in slots:
                    pe.wait_ge(qs_ready[s], i + 1)
                    pe.wait_ge(var1, i)
                    for c in range(CC):
                        ins = T.matmul(bank[1 + s][:, c * VE:(c + 1) * VE], QS[:, s, c, :], KVM[:, c, :], start=True, stop=True)
                    ins.then_inc(t_done[s], 1)

            def b_transpose(i, slots):
                pe.wait_ge(x1t, i * CC)
                for s in slots:
                    pe.wait_ge(x1_ready[s], i + 1)
                    ins = transpose_tile(bank[0][:, s * C:(s + 1) * C], XS[:, s, :])
                ins.then_inc(x1tp, 1)

            def b_hidden(i, slots):
                n = len(slots) * P
                pe.wait_ge(x1t, i * CC + CC)
                pe.wait_ge(hs_ready, i * CC)
                for h in range(CC):
                    for c in range(CC):
                        ins = T.matmul(bank[5][:, h * 2 * P:h * 2 * P + n], W1[:, c, h * P:(h + 1) * P],
                                       XT[:, c, 0:len(slots), :], start=(c == 0), stop=(c == CC - 1))
                ins.then_inc(h_done, 1)

            def b_project(i, slots):
                pe.wait_ge(hs_ready, i * CC + CC)
                for s in slots:
                    pe.wait_ge(y_used[s], i)
                    for h in range(CC):
                        T.matmul(bank[3 + s][:, 0:C], HS[:, h, s, :], W2[:, h, :], start=(h == 0), stop=False)
                    for c in range(CC):
                        T.matmul(bank[3 + s][:, c * P:(c + 1) * P], XT[:, c, s, :], ident[:, :], start=False, stop=False, skip_group_check=True)
                    T.matmul(bank[3 + s][:, 0:C], ones[0:1, :], B2R[0:1, :], start=False, stop=True).then_inc(y_done[s], 1)

            b_attend(0, (0, 1))
            hand(PAIRS, 2)
            b_attend(1, (0, 1))
            b_transpose(0, (0, 1))
            b_hidden(0, (0, 1))

            def b_step(i, following):
                r = i + PAIRS
                hand(r, 0)
                b_project(i - 1, (0, 1))
                hand(r, 1, range(0, 5))
                b_attend(i + 1, following)
                hand(r, 1, range(5, 6))
                b_transpose(i, (0, 1))
                hand(r, 2)
                b_hidden(i, (0, 1))

            with pe.Fori(1, PAIRS - 1) as i:
                b_step(i, (0, 1))
            b_step(PAIRS - 1, (0,))
            hand(ROUNDS, 0)
            b_project(PAIRS - 1, (0, 1))
            hand(ROUNDS, 1, range(0, 2))
            b_transpose(PAIRS, (0,))
            hand(ROUNDS, 1, range(2, 6))
            b_hidden(PAIRS, (0,))
            b_project(PAIRS, (0,))

            pe.wait_ge(f_rstd, 1)
            T.matmul(bank[3][0:1, 0:C], zeros[:, 0:1], iota_c[:, 0:C], start=True, stop=False)

            def ffn_transpose(i, slots):
                for s in slots:
                    pe.wait_ge(f_xs[s], i + 1)
                    pe.wait_ge(f_xt[s], i)
                    transpose_tile(bank[s], XS[:, s, :]).then_inc(f_tp[s], 1)

            def ffn_sum(i, slots, rows=P):
                for s in slots:
                    pe.wait_ge(f_xn, 2 * i + (s + 1))
                    T.matmul(bank[3][0:1, 0:C], ones[0:rows, 0:1], XN[0:rows, tile(2 * i + s)],
                             start=False, stop=False, skip_group_check=True)

            with pe.Fori(0, EARLY) as i:
                ffn_transpose(i, (0, 1))
                ffn_sum(2 * i, (0, 1))
                ffn_sum(2 * i + 1, (0, 1))
            ffn_sum(PAIRS, (0,), LAST)
            T.matmul(bank[3][0:1, 0:C], zeros[:, 0:1], iota_c[:, 0:C], start=False, stop=True).then_inc(mean_done, 1)
            pe.wait_ge(mean_ready, 1)
            for c in range(CC):
                ins = T.matmul(bank[4][:, c:c + 1], MEANR[0:1, c * P:(c + 1) * P], ones[0:1, 0:1], start=True, stop=True)
            ins.then_inc(mean_turned, 1)
            pe.wait_ge(mean_col, 1)
            for c in range(CC):
                ins = T.matmul(bank[5][0:1, 0:NE], MEAN[:, c:c + 1], RW[:, c, :], start=(c == 0), stop=(c == CC - 1))
            ins.then_inc(logits_done, 1)
            with pe.Fori(EARLY, PAIRS) as i:
                ffn_transpose(i, (0, 1))
            ffn_transpose(PAIRS, (0,))
            pe.wait_ge(topw_ready, 1)
            T.matmul(bank[6][:, 0:TOPK], ones[0:1, :], R[0:1, 9, 0:TOPK], start=True, stop=True).then_inc(wb_done, 1)
            pe.wait_ge(w1_split, 1)
            for s in range(2):
                pe.wait_ge(f_xt[s], PAIRS + (s == 0))

            def products(into, pairs):
                terms = [term for lh, ll, rh, rl in pairs for term in ((ll, rh), (lh, rl), (lh, rh))]
                for m, (left, right) in enumerate(terms):
                    ins = T.matmul(into, left, right, start=(m == 0), stop=(m == len(terms) - 1))
                return ins

            def up(b, n, width):
                s = n % UPS
                e, j = divmod(n, FJ)
                f, at = slice(j * P, (j + 1) * P), bass.ds(b * BLK, width)
                if n == 0:
                    pe.wait_ge(q_split, b + 1)
                if not first_of(b) or n >= UPS:
                    pe.wait_ge(gelu_done, b * NH + (n + 1 - UPS))
                products(bank[s][:, 0:width], [(W1H[:, e, c, f], W1L[:, e, c, f], QH[:, c, at], QL[:, c, at])
                                                   for c in range(CC)]).then_inc(up_done, 1)

            def down(b, par, u):
                if u == 0:
                    pe.wait_ge(hl_ready, b * NH + NH)
                pe.wait_ge(y_read[u], b)
                rows = slice(u * P, (u + 1) * P)
                products(bank[4 + u][:, 0:C], [(HFH[:, par, n, rows], HFL[:, par, n, rows], W2H[:, n, :], W2L[:, n, :])
                                               for n in range(NH)]).then_inc(down_done[u], 1)

            def block_step(b, par, width=BLK):
                for u in range(2):
                    for n in range(u * NH // 2, (u + 1) * NH // 2):
                        up(b + 1, n, width)
                    down(b, par, u)

            for n in range(NH):
                up(0, n, BLK)
            pe.wait_ge(w2_scaled, 1)
            with pe.Fori(0, NBLK // 2 - 1) as j:
                block_step(2 * j, 0)
                block_step(2 * j + 1, 1)
            block_step(NBLK - 2, 0)
            block_step(NBLK - 1, 1, P)
            down(NBLK, 0, 0)


def kernel(**inputs):
    import numpy as _np
    import concourse.bacc as _bacc
    from concourse import mybir as _mybir
    from concourse.bass_utils import run_bass_kernel_spmd as _run

    get = lambda n: _np.asarray(inputs[n])
    x = get("x")
    n, c = x.shape
    tiles = -(-n // 128)
    n_edges = get("src").shape[0]
    chunks = -(-n_edges // (128 * 13)) * 13

    def edges(a):
        flat = _np.zeros(128 * chunks, a.dtype)
        flat[:n_edges] = a
        return flat.reshape(128, chunks)

    xp = _np.zeros((tiles * 128, c), x.dtype)
    xp[:n] = x
    b1 = get("L0_ffn_b1")
    ne, ff = b1.shape
    rowv = lambda name: get(name).reshape(1, -1)
    colv = lambda name: get(name).reshape(-1, 128).T
    laid = {
        "x": xp, "row": edges(get("src")), "col": edges(get("dst")), "weight": edges(get("edge_weight")),
        "gnn_wT": get("L0_gnn_W").T, "gnn_b": rowv("L0_gnn_b"), "qkv_wT": get("L0_mix_Wqkv").T,
        "ln1_g": colv("L0_mix_ln1_g"), "ln1_b": colv("L0_mix_ln1_b"), "mix_w1T": get("L0_mix_W1").T,
        "mix_b1": colv("L0_mix_b1"), "mix_w2T": get("L0_mix_W2").T, "mix_b2": rowv("L0_mix_b2"),
        "ln2_g": rowv("L0_mix_ln2_g"), "ln2_b": rowv("L0_mix_ln2_b"),
        "router_w": get("L0_ffn_Wr"), "router_b": rowv("L0_ffn_br"), "exp_w1": get("L0_ffn_W1"),
        "exp_b1": b1.reshape(ne, ff // 128, 128).transpose(0, 2, 1), "exp_w2": get("L0_ffn_W2"), "exp_b2": get("L0_ffn_b2"),
        "ffn_g": rowv("L0_ffn_gamma"), "ffn_b": rowv("L0_ffn_beta"),
    }
    nc = _bacc.Bacc("TRN2", target_bir_lowering=False, num_devices=1)
    arrays, args = {}, []
    for name, a in laid.items():
        a = _np.ascontiguousarray(a)
        arrays[f"in_{name}"] = a
        args.append(nc.dram_tensor(f"in_{name}", a.shape, _mybir.dt.from_np(a.dtype), kind="ExternalInput").ap())
    f32 = _mybir.dt.float32
    args.append(nc.dram_tensor("out_0", (n, c), f32, kind="ExternalOutput").ap())
    args.append(nc.dram_tensor("xg_rows", (tiles * 128, c), f32, kind="Internal").ap())
    gps_layer_program(nc, *args)
    r = _run(nc, [arrays], core_ids=[0])
    return r.results[0]["out_0"]
```
